# Optimizing a Trainium2 kernel written in Bass

```python
import numpy as np
import jax
import jax.numpy as jnp

def _softmax(x, axis=-1):
    return jax.nn.softmax(x, axis=axis)

def _gelu(x):
    return jax.nn.gelu(x, approximate=True)

def _silu(x):
    return jax.nn.silu(x)

def _sigmoid(x):
    return jax.nn.sigmoid(x)

def _layernorm(x, axis=-1, eps=1e-05):
    m = jnp.mean(x, axis=axis, keepdims=True)
    v = jnp.var(x, axis=axis, keepdims=True)
    return (x - m) / jnp.sqrt(v + eps)

def _scatter_add(tgt, idx, src, axis=0):
    return tgt.at[idx].add(src)

def _segment_sum(src, seg, n):
    return jax.ops.segment_sum(src, seg, n)
kernel_name = 'mk_perceiver_d2_seqx_r2_709398'

def setup_inputs(seed: int=0):
    np.random.seed(seed)
    _w = jnp.asarray

    def _rec_inputs():
        import jax
        import jax.numpy as jnp
        _rk = jax.random.key(seed)
        x = -0.0003929 + 0.9999 * jax.random.normal(jax.random.fold_in(_rk, 1), (32, 32, 512), jnp.float32)
        _lenS = 32 - jax.random.randint(jax.random.fold_in(_rk, 7), (32,), 0, max(1, 32 // 4) + 1, jnp.int32)
        _lenS2 = 257 - jax.random.randint(jax.random.fold_in(_rk, 8), (32,), 0, max(1, 257 // 4) + 1, jnp.int32)
        _ctx_1024P = jax.random.normal(jax.random.fold_in(_rk, 11), (32, 16, 512), jnp.float32)
        _ctx_1024c = jax.random.dirichlet(jax.random.fold_in(_rk, 511), 0.3 * jnp.ones((16,), jnp.float32), (32, 257))
        _ctx_1024t = jnp.einsum('bsk,bkd->bsd', _ctx_1024c, _ctx_1024P)
        _ctx_1024t = _ctx_1024t * jax.lax.rsqrt(jnp.mean(jnp.square(_ctx_1024t)) + 1e-12) * 0.953939
        ctx_1024 = 2.81802e-05 + 1.00001 * (_ctx_1024t + 0.3 * jax.random.normal(jax.random.fold_in(_rk, 611), (32, 257, 512), jnp.float32))
        _validS = jnp.arange(32)[None, :] < _lenS[:, None]
        _validS2 = jnp.arange(257)[None, :] < _lenS2[:, None]
        _causal = jnp.tril(jnp.ones((32, 32), dtype=bool))
        mask_1x1xSxS2_bk0 = jnp.logical_not(jnp.broadcast_to(_validS2[0:1, None, None, :], (1, 1, 32, 257)))
        return (x, ctx_1024, mask_1x1xSxS2_bk0)
    x, ctx_1024, mask_1x1xSxS2_bk0 = _rec_inputs()

    def _L0_xattn_setup():
        import jax, jax.numpy as jnp
        import numpy as np
        import math
        DIM_IN, DIM_Q, DIM_V = (512, 512, 512)
        N, K = (8, 1024)

        def _uniform_linear(key, d_out, d_in):
            c = math.sqrt(6.0 / (d_in + d_out))
            return jax.random.uniform(key, (d_out, d_in), jnp.float32, -c, c)
        key = jax.random.key(seed)
        ks = jax.random.split(key, 9)
        return {'query': jax.random.normal(ks[0], (N, K, DIM_IN), jnp.float32), 'key': jax.random.normal(ks[1], (N, K, DIM_IN), jnp.float32), 'value': jax.random.normal(ks[2], (N, K, DIM_IN), jnp.float32), 'Wq': _uniform_linear(ks[3], DIM_Q, DIM_IN), 'bq': jnp.zeros((DIM_Q,), jnp.float32), 'Wk': _uniform_linear(ks[4], DIM_Q, DIM_IN), 'bk': jnp.zeros((DIM_Q,), jnp.float32), 'Wv': _uniform_linear(ks[5], DIM_V, DIM_IN), 'bv': jnp.zeros((DIM_V,), jnp.float32)}
    _L0_xattn_all = _L0_xattn_setup()
    _L0_xattn_in = {k: v for k, v in _L0_xattn_all.items() if k in ('Wq', 'bq', 'Wk', 'bk', 'Wv', 'bv')}
    del _L0_xattn_all

    def _L0_attn_setup():
        import jax, jax.numpy as jnp
        import numpy as np
        GAMMA_MIN, GAMMA_MAX = (0.15, 1.0)
        ALPHA_CAP = 1.0
        EPS_L2 = 1e-08
        EPS_RMS = 1e-06

        def _rmsnorm(x, w):
            return x * jax.lax.rsqrt(jnp.mean(x * x, axis=-1, keepdims=True) + EPS_RMS) * w

        def _l2norm(x):
            n = jnp.linalg.norm(x, axis=-1, keepdims=True)
            return x / jnp.maximum(n, EPS_L2)

        def _causal_conv(h, kernel):
            K = kernel.shape[0]
            S = h.shape[1]
            hp = jnp.pad(h, ((0, 0), (K - 1, 0), (0, 0)))
            out = jnp.zeros_like(h)
            for j in range(K):
                out = out + kernel[j] * hp[:, K - 1 - j:K - 1 - j + S, :]
            return out
        B, S, D, R, K = (8, 512, 512, 16, 4)
        key = jax.random.key(seed)
        ks = jax.random.split(key, 8)
        return {'h': jax.random.normal(ks[0], (B, S, D), dtype=jnp.float32), 'u': jax.random.normal(ks[1], (D, R), dtype=jnp.float32) * 0.05, 'v': jax.random.normal(ks[2], (D, R), dtype=jnp.float32) * 0.05, 'decay_logit': jnp.zeros((R,), jnp.float32), 'alpha_logit': jnp.zeros((R,), jnp.float32), 'k_base_gate_logit': jnp.float32(0.0), 'k_base_kernel': jax.random.normal(ks[3], (K,), dtype=jnp.float32) * 0.05, 'proj_w': jax.random.normal(ks[4], (D, D), dtype=jnp.float32) * 0.02, 'proj_b': jnp.zeros((D,), jnp.float32), 'norm1_w': jnp.ones((D,), jnp.float32), 'norm2_w': jnp.ones((D,), jnp.float32), 'mlp_w1': jax.random.normal(ks[5], (D, 4 * D), dtype=jnp.float32) * 0.02, 'mlp_b1': jnp.zeros((4 * D,), jnp.float32), 'mlp_w2': jax.random.normal(ks[6], (4 * D, D), dtype=jnp.float32) * 0.02, 'mlp_b2': jnp.zeros((D,), jnp.float32)}
    _L0_attn_all = _L0_attn_setup()
    _L0_attn_in = {k: v for k, v in _L0_attn_all.items() if k in ('u', 'v', 'decay_logit', 'alpha_logit', 'k_base_gate_logit', 'k_base_kernel', 'proj_w', 'proj_b', 'norm1_w', 'norm2_w', 'mlp_w1', 'mlp_b1', 'mlp_w2', 'mlp_b2')}
    del _L0_attn_all

    def _L0_ffn_setup():
        import jax, jax.numpy as jnp
        import numpy as np
        D_MODEL = 512
        N_HEADS = 16
        N_EXPERTS = 8
        TOP_K = 2
        EXPERT_HIDDEN = D_MODEL * 4 // N_EXPERTS

        def layer_norm(x, g, b, eps=1e-05):
            mu = jnp.mean(x, axis=-1, keepdims=True)
            var = jnp.var(x, axis=-1, keepdims=True)
            return (x - mu) * jax.lax.rsqrt(var + eps) * g + b
        key = jax.random.key(seed)
        ks = jax.random.split(key, 12)
        s = 1.0 / np.sqrt(D_MODEL)
        return {'x': jax.random.normal(ks[0], (2, 1024, D_MODEL), dtype=jnp.float32), 'Wq': jax.random.normal(ks[1], (D_MODEL, D_MODEL), dtype=jnp.float32) * s, 'Wk': jax.random.normal(ks[2], (D_MODEL, D_MODEL), dtype=jnp.float32) * s, 'Wv': jax.random.normal(ks[3], (D_MODEL, D_MODEL), dtype=jnp.float32) * s, 'Wo': jax.random.normal(ks[4], (D_MODEL, D_MODEL), dtype=jnp.float32) * s, 'g1': jnp.ones((D_MODEL,), jnp.float32), 'b1': jnp.zeros((D_MODEL,), jnp.float32), 'g2': jnp.ones((D_MODEL,), jnp.float32), 'b2': jnp.zeros((D_MODEL,), jnp.float32), 'Wg': jax.random.normal(ks[5], (D_MODEL, N_EXPERTS), dtype=jnp.float32) * s, 'W1': jax.random.normal(ks[6], (N_EXPERTS, D_MODEL, EXPERT_HIDDEN), dtype=jnp.float32) * s, 'W2': jax.random.normal(ks[7], (N_EXPERTS, EXPERT_HIDDEN, D_MODEL), dtype=jnp.float32) * (1.0 / np.sqrt(EXPERT_HIDDEN))}
    _L0_ffn_all = _L0_ffn_setup()
    _L0_ffn_in = {k: v for k, v in _L0_ffn_all.items() if k in ('Wq', 'Wk', 'Wv', 'Wo', 'g1', 'b1', 'g2', 'b2', 'Wg', 'W1', 'W2')}
    del _L0_ffn_all

    def _L1_xattn_setup():
        import jax, jax.numpy as jnp
        import numpy as np
        DIM = 512
        HEADS = 16
        DIM_K = DIM // HEADS
        B, S = (2, 1024)
        key = jax.random.key(seed)
        ks = jax.random.split(key, 8)
        scale = 1.0 / np.sqrt(DIM)
        Q = jax.random.normal(ks[0], (B, S, DIM), dtype=jnp.float32)
        K = jax.random.normal(ks[1], (B, S, DIM), dtype=jnp.float32)
        V = jax.random.normal(ks[2], (B, S, DIM), dtype=jnp.float32)
        mask = jnp.tril(jnp.ones((S, S), dtype=bool))[None, None, :, :]
        wq = jax.random.normal(ks[3], (DIM, DIM), dtype=jnp.float32) * scale
        wk = jax.random.normal(ks[4], (DIM, DIM), dtype=jnp.float32) * scale
        wv = jax.random.normal(ks[5], (DIM, DIM), dtype=jnp.float32) * scale
        wo_w = jax.random.normal(ks[6], (DIM, DIM), dtype=jnp.float32) * scale
        wo_b = jnp.zeros((DIM,), dtype=jnp.float32)
        return {'Q': Q, 'K': K, 'V': V, 'mask': mask, 'wq': wq, 'wk': wk, 'wv': wv, 'wo_w': wo_w, 'wo_b': wo_b}
    _L1_xattn_all = _L1_xattn_setup()
    _L1_xattn_in = {k: v for k, v in _L1_xattn_all.items() if k in ('wq', 'wk', 'wv', 'wo_w', 'wo_b')}
    del _L1_xattn_all

    def _L1_attn_setup():
        import jax, jax.numpy as jnp
        import numpy as np
        EMBED_DIM = 512
        NUM_HEADS = 16
        HEAD_DIM = EMBED_DIM // NUM_HEADS
        LAMBDA_ENTANGLE = 0.35
        key = jax.random.key(seed)
        ks = jax.random.split(key, 10)
        B, S, D = (2, 1024, EMBED_DIM)
        init = 1.0 / np.sqrt(D)
        x = jax.random.normal(ks[0], (B, S, D), dtype=jnp.float32)
        Wq = jax.random.uniform(ks[1], (D, D), jnp.float32, -init, init)
        bq = jax.random.uniform(ks[2], (D,), jnp.float32, -init, init)
        Wk = jax.random.uniform(ks[3], (D, D), jnp.float32, -init, init)
        bk = jax.random.uniform(ks[4], (D,), jnp.float32, -init, init)
        Wv = jax.random.uniform(ks[5], (D, D), jnp.float32, -init, init)
        bv = jax.random.uniform(ks[6], (D,), jnp.float32, -init, init)
        Wo = jax.random.uniform(ks[7], (D, D), jnp.float32, -init, init)
        bo = jax.random.uniform(ks[8], (D,), jnp.float32, -init, init)
        J_attn = jax.random.normal(ks[9], (NUM_HEADS, HEAD_DIM, HEAD_DIM), dtype=jnp.float32) * 0.02
        lambda_attn = jnp.asarray(LAMBDA_ENTANGLE, dtype=jnp.float32)
        return {'x': x, 'Wq': Wq, 'bq': bq, 'Wk': Wk, 'bk': bk, 'Wv': Wv, 'bv': bv, 'Wo': Wo, 'bo': bo, 'J_attn': J_attn, 'lambda_attn': lambda_attn}
    _L1_attn_all = _L1_attn_setup()
    _L1_attn_in = {k: v for k, v in _L1_attn_all.items() if k in ('Wq', 'bq', 'Wk', 'bk', 'Wv', 'bv', 'Wo', 'bo', 'J_attn', 'lambda_attn')}
    del _L1_attn_all

    def _L1_ffn_setup():
        import jax, jax.numpy as jnp
        import numpy as np
        D = 512
        F = 512
        E = 8
        K = 2
        B, T = (2, 1024)

        def _moe_forward(x, router_w, w1, w2, shared_gate_up, shared_down, shared_gate_w):
            b, t, d = x.shape
            xf = x.reshape(-1, d)
            n = xf.shape[0]
            logits = xf @ router_w
            probs = jax.nn.softmax(logits, axis=-1)
            topw, topi = jax.lax.top_k(probs, K)
            combine = jnp.zeros((n, E), dtype=probs.dtype).at[jnp.arange(n)[:, None], topi].add(topw)
            h = jax.nn.silu(jnp.einsum('nd,edf->nef', xf, w1))
            ye = jnp.einsum('nef,efd->ned', h, w2)
            routed = jnp.einsum('ne,ned->nd', combine, ye)
            gu = xf @ shared_gate_up
            gate, up = (gu[:, :F], gu[:, F:])
            shared = jax.nn.silu(gate) * up @ shared_down
            shared = jax.nn.sigmoid(xf @ shared_gate_w) * shared
            return (routed + shared).reshape(b, t, d)
        key = jax.random.key(seed)
        ks = jax.random.split(key, 7)
        std = 0.02
        x = jax.random.normal(ks[0], (B, T, D), dtype=jnp.float32)
        router_w = jax.random.normal(ks[1], (D, E), dtype=jnp.float32) * std
        w1 = jax.random.normal(ks[2], (E, D, F), dtype=jnp.float32) * std
        w2 = jax.random.normal(ks[3], (E, F, D), dtype=jnp.float32) * std
        shared_gate_up = jax.random.normal(ks[4], (D, 2 * F), dtype=jnp.float32) * std
        shared_down = jax.random.normal(ks[5], (F, D), dtype=jnp.float32) * std
        shared_gate_w = jax.random.normal(ks[6], (D, 1), dtype=jnp.float32) * std
        return {'x': x, 'router_w': router_w, 'w1': w1, 'w2': w2, 'shared_gate_up': shared_gate_up, 'shared_down': shared_down, 'shared_gate_w': shared_gate_w}
    _L1_ffn_all = _L1_ffn_setup()
    _L1_ffn_in = {k: v for k, v in _L1_ffn_all.items() if k in ('router_w', 'w1', 'w2', 'shared_gate_up', 'shared_down', 'shared_gate_w')}
    del _L1_ffn_all
    return {'x': x, 'ctx_1024': ctx_1024, 'mask_1x1xSxS2_bk0': mask_1x1xSxS2_bk0, 'L0_xattn_Wq': _L0_xattn_in['Wq'], 'L0_xattn_bq': _L0_xattn_in['bq'], 'L0_xattn_Wk': _L0_xattn_in['Wk'], 'L0_xattn_bk': _L0_xattn_in['bk'], 'L0_xattn_Wv': _L0_xattn_in['Wv'], 'L0_xattn_bv': _L0_xattn_in['bv'], 'L0_attn_u': _L0_attn_in['u'], 'L0_attn_v': _L0_attn_in['v'], 'L0_attn_decay_logit': _L0_attn_in['decay_logit'], 'L0_attn_alpha_logit': _L0_attn_in['alpha_logit'], 'L0_attn_k_base_gate_logit': _L0_attn_in['k_base_gate_logit'], 'L0_attn_k_base_kernel': _L0_attn_in['k_base_kernel'], 'L0_attn_proj_w': _L0_attn_in['proj_w'], 'L0_attn_proj_b': _L0_attn_in['proj_b'], 'L0_attn_norm1_w': _L0_attn_in['norm1_w'], 'L0_attn_norm2_w': _L0_attn_in['norm2_w'], 'L0_attn_mlp_w1': _L0_attn_in['mlp_w1'], 'L0_attn_mlp_b1': _L0_attn_in['mlp_b1'], 'L0_attn_mlp_w2': _L0_attn_in['mlp_w2'], 'L0_attn_mlp_b2': _L0_attn_in['mlp_b2'], 'L0_ffn_Wq': _L0_ffn_in['Wq'], 'L0_ffn_Wk': _L0_ffn_in['Wk'], 'L0_ffn_Wv': _L0_ffn_in['Wv'], 'L0_ffn_Wo': _L0_ffn_in['Wo'], 'L0_ffn_g1': _L0_ffn_in['g1'], 'L0_ffn_b1': _L0_ffn_in['b1'], 'L0_ffn_g2': _L0_ffn_in['g2'], 'L0_ffn_b2': _L0_ffn_in['b2'], 'L0_ffn_Wg': _L0_ffn_in['Wg'], 'L0_ffn_W1': _L0_ffn_in['W1'], 'L0_ffn_W2': _L0_ffn_in['W2'], 'L1_xattn_wq': _L1_xattn_in['wq'], 'L1_xattn_wk': _L1_xattn_in['wk'], 'L1_xattn_wv': _L1_xattn_in['wv'], 'L1_xattn_wo_w': _L1_xattn_in['wo_w'], 'L1_xattn_wo_b': _L1_xattn_in['wo_b'], 'L1_attn_Wq': _L1_attn_in['Wq'], 'L1_attn_bq': _L1_attn_in['bq'], 'L1_attn_Wk': _L1_attn_in['Wk'], 'L1_attn_bk': _L1_attn_in['bk'], 'L1_attn_Wv': _L1_attn_in['Wv'], 'L1_attn_bv': _L1_attn_in['bv'], 'L1_attn_Wo': _L1_attn_in['Wo'], 'L1_attn_bo': _L1_attn_in['bo'], 'L1_attn_J_attn': _L1_attn_in['J_attn'], 'L1_attn_lambda_attn': _L1_attn_in['lambda_attn'], 'L1_ffn_router_w': _L1_ffn_in['router_w'], 'L1_ffn_w1': _L1_ffn_in['w1'], 'L1_ffn_w2': _L1_ffn_in['w2'], 'L1_ffn_shared_gate_up': _L1_ffn_in['shared_gate_up'], 'L1_ffn_shared_down': _L1_ffn_in['shared_down'], 'L1_ffn_shared_gate_w': _L1_ffn_in['shared_gate_w']}

def reference(x, ctx_1024, mask_1x1xSxS2_bk0, L0_xattn_Wq, L0_xattn_bq, L0_xattn_Wk, L0_xattn_bk, L0_xattn_Wv, L0_xattn_bv, L0_attn_u, L0_attn_v, L0_attn_decay_logit, L0_attn_alpha_logit, L0_attn_k_base_gate_logit, L0_attn_k_base_kernel, L0_attn_proj_w, L0_attn_proj_b, L0_attn_norm1_w, L0_attn_norm2_w, L0_attn_mlp_w1, L0_attn_mlp_b1, L0_attn_mlp_w2, L0_attn_mlp_b2, L0_ffn_Wq, L0_ffn_Wk, L0_ffn_Wv, L0_ffn_Wo, L0_ffn_g1, L0_ffn_b1, L0_ffn_g2, L0_ffn_b2, L0_ffn_Wg, L0_ffn_W1, L0_ffn_W2, L1_xattn_wq, L1_xattn_wk, L1_xattn_wv, L1_xattn_wo_w, L1_xattn_wo_b, L1_attn_Wq, L1_attn_bq, L1_attn_Wk, L1_attn_bk, L1_attn_Wv, L1_attn_bv, L1_attn_Wo, L1_attn_bo, L1_attn_J_attn, L1_attn_lambda_attn, L1_ffn_router_w, L1_ffn_w1, L1_ffn_w2, L1_ffn_shared_gate_up, L1_ffn_shared_down, L1_ffn_shared_gate_w):
    import jax
    import jax.numpy as jnp

    def _L0_xattn_ref(query, key, value, Wq, bq, Wk, bk, Wv, bv):
        import jax, jax.numpy as jnp
        import numpy as np
        import math
        DIM_IN, DIM_Q, DIM_V = (512, 512, 512)
        N, K = (8, 1024)

        def _uniform_linear(key, d_out, d_in):
            c = math.sqrt(6.0 / (d_in + d_out))
            return jax.random.uniform(key, (d_out, d_in), jnp.float32, -c, c)
        q = jnp.einsum('nkm,qm->nkq', query, Wq) + bq
        k = jnp.einsum('nkm,qm->nkq', key, Wk) + bk
        v = jnp.einsum('nkm,vm->nkv', value, Wv) + bv
        M = q.shape[-1]
        scores = jnp.einsum('nqd,nkd->nqk', q, k) / jnp.sqrt(jnp.float32(M))
        w = jax.nn.softmax(scores, axis=-1)
        y = jnp.einsum('nqk,nkv->nqv', w, v)
        return y

    def _L0_attn_ref(h, u, v, decay_logit, alpha_logit, k_base_gate_logit, k_base_kernel, proj_w, proj_b, norm1_w, norm2_w, mlp_w1, mlp_b1, mlp_w2, mlp_b2):
        import jax, jax.numpy as jnp
        import numpy as np
        GAMMA_MIN, GAMMA_MAX = (0.15, 1.0)
        ALPHA_CAP = 1.0
        EPS_L2 = 1e-08
        EPS_RMS = 1e-06

        def _rmsnorm(x, w):
            return x * jax.lax.rsqrt(jnp.mean(x * x, axis=-1, keepdims=True) + EPS_RMS) * w

        def _l2norm(x):
            n = jnp.linalg.norm(x, axis=-1, keepdims=True)
            return x / jnp.maximum(n, EPS_L2)

        def _causal_conv(h, kernel):
            K = kernel.shape[0]
            S = h.shape[1]
            hp = jnp.pad(h, ((0, 0), (K - 1, 0), (0, 0)))
            out = jnp.zeros_like(h)
            for j in range(K):
                out = out + kernel[j] * hp[:, K - 1 - j:K - 1 - j + S, :]
            return out
        B, S, D = h.shape
        R = u.shape[1]
        residual = h
        h_norm = _rmsnorm(h, norm1_w)
        gate = jax.nn.sigmoid(k_base_gate_logit)
        out = gate * _causal_conv(h_norm, k_base_kernel)
        alpha = ALPHA_CAP * jax.nn.sigmoid(alpha_logit)
        qk = h_norm @ jnp.concatenate((u, v), axis=1)
        q_raw, k_raw = (qk[..., :R], qk[..., R:])
        q = _l2norm(q_raw)
        k = _l2norm(k_raw)
        gamma = jnp.clip(jax.nn.sigmoid(decay_logit), GAMMA_MIN, GAMMA_MAX)
        pos = jnp.arange(S, dtype=h.dtype)
        diff = jnp.maximum(pos[:, None] - pos[None, :], 0.0)
        mask = jnp.tril(jnp.ones((S, S), dtype=h.dtype))
        w = gamma[:, None, None] ** diff * mask
        q_alpha = q * alpha
        A = jnp.einsum('bir,bjr,rij->bij', q_alpha, k, w)
        decay_out = jnp.einsum('bij,bjd->bid', A, h_norm)
        out = out + decay_out
        out = out @ proj_w.T + proj_b
        h2 = residual + out
        hn2 = _rmsnorm(h2, norm2_w)
        mlp_out = jax.nn.gelu(hn2 @ mlp_w1 + mlp_b1) @ mlp_w2 + mlp_b2
        return h2 + mlp_out

    def _L0_ffn_ref(x, Wq, Wk, Wv, Wo, g1, b1, g2, b2, Wg, W1, W2):
        import jax, jax.numpy as jnp
        import numpy as np
        D_MODEL = 512
        N_HEADS = 16
        N_EXPERTS = 8
        TOP_K = 2
        EXPERT_HIDDEN = D_MODEL * 4 // N_EXPERTS

        def layer_norm(x, g, b, eps=1e-05):
            mu = jnp.mean(x, axis=-1, keepdims=True)
            var = jnp.var(x, axis=-1, keepdims=True)
            return (x - mu) * jax.lax.rsqrt(var + eps) * g + b
        B, S, D = x.shape
        H, dk = (N_HEADS, D // N_HEADS)
        xn = layer_norm(x, g1, b1)
        q = (xn @ Wq).reshape(B, S, H, dk).transpose(0, 2, 1, 3)
        k = (xn @ Wk).reshape(B, S, H, dk).transpose(0, 2, 1, 3)
        v = (xn @ Wv).reshape(B, S, H, dk).transpose(0, 2, 1, 3)
        scores = jnp.einsum('bhqd,bhkd->bhqk', q, k) / np.sqrt(dk)
        attn = jax.nn.softmax(scores, axis=-1)
        o = jnp.einsum('bhqk,bhkd->bhqd', attn, v)
        o = o.transpose(0, 2, 1, 3).reshape(B, S, D) @ Wo
        x = x + o
        xn2 = layer_norm(x, g2, b2)
        xf = xn2.reshape(B * S, D)
        gate = xf @ Wg
        topv, topi = jax.lax.top_k(gate, TOP_K)
        probs = jax.nn.softmax(topv, axis=-1)
        cw = jnp.sum(jax.nn.one_hot(topi, N_EXPERTS, dtype=xf.dtype) * probs[..., None], axis=1)
        h = jax.nn.relu(jnp.einsum('td,edh->teh', xf, W1))
        y = jnp.einsum('teh,ehd->ted', h, W2)
        moe = jnp.einsum('ted,te->td', y, cw).reshape(B, S, D)
        return x + moe

    def _L1_xattn_ref(Q, K, V, mask, wq, wk, wv, wo_w, wo_b):
        import jax, jax.numpy as jnp
        import numpy as np
        DIM = 512
        HEADS = 16
        DIM_K = DIM // HEADS
        B, S = (2, 1024)
        b, s, d = Q.shape
        n_k = K.shape[1]
        q = (Q @ wq.T).reshape(b, s, HEADS, DIM_K).transpose(0, 2, 1, 3)
        k = (K @ wk.T).reshape(b, n_k, HEADS, DIM_K).transpose(0, 2, 1, 3)
        v = (V @ wv.T).reshape(b, n_k, HEADS, DIM_K).transpose(0, 2, 1, 3)
        inv_sqrt_dk = 1.0 / np.sqrt(DIM_K).astype(np.float32)
        scores = jnp.einsum('bhsd,bhtd->bhst', q, k) * inv_sqrt_dk
        scores = jnp.where(mask, scores, jnp.float32(-1000000000.0))
        weights = jax.nn.softmax(scores, axis=-1)
        out = jnp.einsum('bhst,bhtd->bhsd', weights, v)
        out = out.transpose(0, 2, 1, 3).reshape(b, s, d)
        return out @ wo_w.T + wo_b

    def _L1_attn_ref(x, Wq, bq, Wk, bk, Wv, bv, Wo, bo, J_attn, lambda_attn):
        import jax, jax.numpy as jnp
        import numpy as np
        EMBED_DIM = 512
        NUM_HEADS = 16
        HEAD_DIM = EMBED_DIM // NUM_HEADS
        LAMBDA_ENTANGLE = 0.35
        B, S, D = x.shape
        H, Hd = (NUM_HEADS, HEAD_DIM)
        scale = jnp.sqrt(jnp.asarray(Hd, dtype=x.dtype))

        def heads(W, b):
            y = jnp.einsum('bsd,ed->bse', x, W) + b
            return y.reshape(B, S, H, Hd).transpose(0, 2, 1, 3)
        Q = heads(Wq, bq)
        K = heads(Wk, bk)
        V = heads(Wv, bv)
        scores = jnp.einsum('bhid,bhjd->bhij', Q, K) / scale
        QJ = jnp.einsum('bhid,hde->bhie', jnp.tanh(Q), J_attn)
        delta = jnp.einsum('bhie,bhje->bhij', QJ, jnp.tanh(K))
        scores = scores + lambda_attn * delta
        causal = jnp.triu(jnp.ones((S, S), dtype=bool), k=1)
        scores = jnp.where(causal, -jnp.inf, scores)
        probs = jax.nn.softmax(scores, axis=-1)
        out = jnp.einsum('bhij,bhjd->bhid', probs, V)
        out = out.transpose(0, 2, 1, 3).reshape(B, S, D)
        return jnp.einsum('bsd,ed->bse', out, Wo) + bo

    def _L1_ffn_ref(x, router_w, w1, w2, shared_gate_up, shared_down, shared_gate_w):
        import jax, jax.numpy as jnp
        import numpy as np
        D = 512
        F = 512
        E = 8
        K = 2
        B, T = (2, 1024)

        def _moe_forward(x, router_w, w1, w2, shared_gate_up, shared_down, shared_gate_w):
            b, t, d = x.shape
            xf = x.reshape(-1, d)
            n = xf.shape[0]
            logits = xf @ router_w
            probs = jax.nn.softmax(logits, axis=-1)
            topw, topi = jax.lax.top_k(probs, K)
            combine = jnp.zeros((n, E), dtype=probs.dtype).at[jnp.arange(n)[:, None], topi].add(topw)
            h = jax.nn.silu(jnp.einsum('nd,edf->nef', xf, w1))
            ye = jnp.einsum('nef,efd->ned', h, w2)
            routed = jnp.einsum('ne,ned->nd', combine, ye)
            gu = xf @ shared_gate_up
            gate, up = (gu[:, :F], gu[:, F:])
            shared = jax.nn.silu(gate) * up @ shared_down
            shared = jax.nn.sigmoid(xf @ shared_gate_w) * shared
            return (routed + shared).reshape(b, t, d)
        return _moe_forward(x, router_w, w1, w2, shared_gate_up, shared_down, shared_gate_w)
    x = x + _L0_xattn_ref(_layernorm(x, axis=-1), ctx_1024, ctx_1024, L0_xattn_Wq, L0_xattn_bq, L0_xattn_Wk, L0_xattn_bk, L0_xattn_Wv, L0_xattn_bv)
    x = x + _L0_attn_ref(_layernorm(x, axis=-1), L0_attn_u, L0_attn_v, L0_attn_decay_logit, L0_attn_alpha_logit, L0_attn_k_base_gate_logit, L0_attn_k_base_kernel, L0_attn_proj_w, L0_attn_proj_b, L0_attn_norm1_w, L0_attn_norm2_w, L0_attn_mlp_w1, L0_attn_mlp_b1, L0_attn_mlp_w2, L0_attn_mlp_b2)
    x = x + _L0_ffn_ref(_layernorm(x, axis=-1), L0_ffn_Wq, L0_ffn_Wk, L0_ffn_Wv, L0_ffn_Wo, L0_ffn_g1, L0_ffn_b1, L0_ffn_g2, L0_ffn_b2, L0_ffn_Wg, L0_ffn_W1, L0_ffn_W2)
    x = x + _L1_xattn_ref(_layernorm(x, axis=-1), ctx_1024, ctx_1024, mask_1x1xSxS2_bk0, L1_xattn_wq, L1_xattn_wk, L1_xattn_wv, L1_xattn_wo_w, L1_xattn_wo_b)
    x = x + _L1_attn_ref(_layernorm(x, axis=-1), L1_attn_Wq, L1_attn_bq, L1_attn_Wk, L1_attn_bk, L1_attn_Wv, L1_attn_bv, L1_attn_Wo, L1_attn_bo, L1_attn_J_attn, L1_attn_lambda_attn)
    x = x + _L1_ffn_ref(_layernorm(x, axis=-1), L1_ffn_router_w, L1_ffn_w1, L1_ffn_w2, L1_ffn_shared_gate_up, L1_ffn_shared_down, L1_ffn_shared_gate_w)
    return x

_drawn_inputs = setup_inputs


def setup_inputs(seed=0):
    import zlib

    import numpy as np

    out = dict(_drawn_inputs(seed))
    spreads = {'L0_xattn_bq': (0.0, 0.306),
     'L0_xattn_bk': (0.0, 2.0),
     'L0_xattn_bv': (0.0, 0.1),
     'L0_attn_decay_logit': (0.0, 0.8),
     'L0_attn_alpha_logit': (0.0, 0.8),
     'L0_attn_proj_b': (0.0, 0.1),
     'L0_attn_norm1_w': (1.0, 0.6),
     'L0_attn_norm2_w': (1.0, 0.2),
     'L0_attn_mlp_b1': (0.0, 0.1),
     'L0_attn_mlp_b2': (0.0, 0.1),
     'L0_ffn_g1': (1.0, 0.2),
     'L0_ffn_b1': (0.0, 0.1),
     'L0_ffn_g2': (1.0, 0.2),
     'L0_ffn_b2': (0.0, 0.1),
     'L1_xattn_wo_b': (0.0, 0.1)}
    factors = {'L0_attn_k_base_kernel': 3.071,
     'L1_attn_Wq': 7.445,
     'L1_attn_bq': 24.75,
     'L1_attn_Wk': 6.971,
     'L1_attn_bk': 64.0,
     'L1_attn_bv': 8.0,
     'L1_attn_bo': 7.461,
     'L1_attn_J_attn': 8.0,
     'L1_ffn_router_w': 6.918,
     'L1_ffn_w1': 6.147,
     'L1_ffn_w2': 6.009,
     'L1_ffn_shared_gate_up': 7.388,
     'L1_ffn_shared_down': 7.348,
     'L1_ffn_shared_gate_w': 8.0}
    for name, (base, spread) in spreads.items():
        noise = np.random.default_rng([zlib.crc32(name.encode()), seed]).standard_normal(out[name].shape)
        drawn = base * np.exp(spread * noise) if base else spread * noise
        out[name] = jnp.asarray(drawn.astype(out[name].dtype))
    for name, factor in factors.items():
        out[name] = (out[name] * factor).astype(out[name].dtype)
    return out
```

```python
from contextlib import ExitStack

import numpy as np

import concourse.bass as bass
from concourse import mybir

ALU = mybir.AluOpType
ACT = mybir.ActivationFunctionType
AX_X = mybir.AxisListType.X
F32 = mybir.dt.float32
U8 = mybir.dt.uint8

P = 128
D = 512
C = D // P
BATCH, SEQ = 32, 32
TOK = BATCH * SEQ
T = TOK // P
PB = P // SEQ
G = TOK // 512
TG = T // G
KEYS = 257
KT = 2
HEADS, DK = 16, 32
HG = 4
R = 16
E = 8
NW = 5
NC1 = 8
NC4 = 4
NVR = 4

VEC = ["bq0", "norm1", "norm2", "mb10", "mb11", "mb12", "mb13", "g1", "b1", "g2", "b2", "bq5", "bk5", "bk0"]
ROW = ["bv0", "proj_b", "mb2", "wo_b", "bv5", "bo5"]
SCL = {"decay": (0, R), "alpha": (R, R), "gate": (2 * R, 1), "kern": (2 * R + 1, 4), "lam": (2 * R + 5, 1)}
NSCL = 2 * R + 6
SML = {"uv": (0, 2 * R), "wg": (2 * R, E), "router": (2 * R + E, E + 1)}
NSML = 2 * R + E + E + 1
CON = {"ident": (0, P), "lower": (P, P), "shift": (2 * P, 4 * P), "causal": (6 * P, SEQ), "before": (6 * P + SEQ, E * E),
       "pos": (6 * P + SEQ + E * E, 1)}
NCON = 6 * P + SEQ + E * E + 1


def constants():
    con = np.zeros((P, NCON), np.float32)
    j, i = np.meshgrid(np.arange(P), np.arange(P), indexing="ij")
    same = (j // SEQ) == (i // SEQ)
    con[:, 0:P] = np.eye(P)
    con[:, P:2 * P] = same & (i >= j)
    for m in range(4):
        con[:, (2 + m) * P:(3 + m) * P] = same & (i - j == m)
    q, k = np.meshgrid(np.arange(P) % SEQ, np.arange(SEQ), indexing="ij")
    con[:, 6 * P:6 * P + SEQ] = np.where(k > q, -1e30, 0.0)
    e, f = np.meshgrid(np.arange(E), np.arange(E), indexing="ij")
    con[:, 6 * P + SEQ:6 * P + SEQ + E * E] = (f < e).astype(np.float32).reshape(1, -1)
    con[:, -1] = np.arange(P) % SEQ
    return con


UNITS = (["0.wq", "0.wk", "0.wv", "1.proj"] + [f"1.w{i}.{b}" for b in range(4) for i in (1, 2)]
         + ["2.q", "2.k", "2.v", "2.o"] + [f"2.w{i}.{b}" for b in range(4) for i in (1, 2)]
         + ["3.q", "3.k", "3.v", "3.o", "4.q", "4.k", "4.v", "4.o"]
         + [f"5.w{i}.{b}" for b in range(E) for i in (1, 2)] + ["5.gate", "5.up", "5.down"])
UNIT = {name: i for i, name in enumerate(UNITS)}


class Jobs:

    def __init__(self):
        self.ready, self.bank, self.drain, self.frees, self.last = {}, {}, {}, {}, {}
        self.at, self.count, self.owner = 0, {"act": 0, "dve": 0}, [None] * 8

    def add(self, key, drain, banks=1, unit=None):
        self.at += -self.at % banks
        b = self.at % 8
        before = [self.owner[x] for x in range(b, b + banks) if self.owner[x] is not None]
        need = {}
        for k in before:
            eng, n = self.drain[k]
            need[eng] = max(need.get(eng, 0), n)
        self.frees[key] = need
        for x in range(b, b + banks):
            self.owner[x] = key
        self.at = (b + banks) % 8
        self.bank[key] = b
        self.ready[key] = len(self.ready) + 1
        self.count[drain] += 1
        self.drain[key] = (drain, self.count[drain])
        if unit is not None:
            self.last[unit] = self.ready[key]


def plan(stop):
    J = Jobs()
    for g in range(G):
        for t in range(g * TG, g * TG + TG):
            J.add(("t1", t), "act")
        for m in range(C):
            J.add(("q", g, m), "act", unit="0.wq")
    J.add(("c",), "dve")
    for g in range(G):
        for m in range(C):
            J.add(("qk", g, m), "act", unit="0.wk")
    for t in range(T + 1):
        if t < T:
            J.add(("s", t), "act")
        if t >= 1:
            J.add(("pt", t - 1), "act")
            J.add(("u", t - 1), "dve")
    for t in range(T):
        J.add(("y", t), "dve", unit="0.wv")
    if stop == 1:
        return J
    for name, eng in (("t2", "dve"), ("uv", "dve"), ("kq", "act"), ("A", "dve"), ("d", "dve"), ("pr", "dve"), ("t3", "dve")):
        for t in range(T):
            J.add((name, t), eng, unit="1.proj" if name == "pr" else None)
    for b in range(4):
        for g in range(G):
            for m in range(C):
                J.add(("h1", b, g, m), "act", unit=f"1.w1.{b}")
        for t in range(T):
            J.add(("o1", b, t), "dve", unit=f"1.w2.{b}")
    if stop == 2:
        return J
    for t in range(T):
        J.add(("t4", t), "dve")
    for g in range(G):
        for m in range(C):
            J.add(("q3", g, m), "act", unit="2.q")
    for g in range(G):
        for m in range(C):
            J.add(("k3", g, m), "act", unit="2.k")
    for t in range(T):
        J.add(("v3", t), "act", unit="2.v")
    for t in range(T + 1):
        if t < T:
            J.add(("s3", t), "act", banks=4)
        if t >= 1:
            J.add(("o3", t - 1), "dve", banks=4)
    for t in range(T):
        J.add(("x3", t), "dve", unit="2.o")
    for t in range(T):
        J.add(("t6", t), "dve")
    J.add(("g3",), "dve")
    for b in range(4):
        for g in range(G):
            for m in range(C):
                J.add(("h2", b, g, m), "act", unit=f"2.w1.{b}")
        for t in range(T):
            for e in range(2):
                J.add(("o2", b, t, e), "dve", unit=f"2.w2.{b}")
    if stop == 3:
        return J
    for t in range(T):
        J.add(("t5", t), "act")
    for g in range(G):
        for m in range(C):
            J.add(("q4", g, m), "act", unit="3.q")
    J.add(("vl",), "act")
    for b in range(BATCH + 1):
        if b < BATCH:
            J.add(("k4", b), "act", banks=4, unit="3.k")
            J.add(("v4", b), "dve", banks=2, unit="3.v")
            J.add(("s4", b), "dve", banks=4)
        if b >= 1:
            J.add(("p4", b - 1), "act", banks=2)
            J.add(("l4", b - 1), "act")
            J.add(("o4", b - 1), "dve")
    for t in range(T):
        J.add(("x4", t), "dve", unit="3.o")
    if stop == 4:
        return J
    for t in range(T):
        J.add(("t7", t), "act")
    for g in range(G):
        for m in range(C):
            J.add(("q5", g, m), "act", unit="4.q")
    for g in range(G):
        for m in range(C):
            J.add(("k5", g, m), "act", unit="4.k")
    for t in range(T):
        J.add(("v5", t), "dve", unit="4.v")
    for g in range(G):
        for m in range(C):
            J.add(("qj", g, m), "act")
    for t in range(T + 1):
        if t < T:
            J.add(("s5", t), "dve", banks=4)
        if t >= 1:
            J.add(("o5", t - 1), "act", banks=4)
    for t in range(T):
        J.add(("x5", t), "dve", unit="4.o")
    if stop == 5:
        return J
    for t in range(T):
        J.add(("t8", t), "act")
    J.add(("r6",), "dve")
    for b in range(E):
        for g in range(G):
            for m in range(C):
                J.add(("h3", b, g, m), "act", unit=f"5.w1.{b}")
        for t in range(T):
            J.add(("o6", b, t), "dve", unit=f"5.w2.{b}")
    for g in range(G):
        for m in range(C):
            J.add(("sg", g, m), "act", unit="5.gate")
            J.add(("su", g, m), "dve", unit="5.up")
    for t in range(T):
        J.add(("os", t), "dve", unit="5.down")
    return J


def build(nc, x, ctx, ctx_t, ctx_last, mask, units, vecs, rows, scalars, small, jbd, con, out, stop=6):
    J = plan(stop)
    n_units = {1: 3, 2: 12, 3: 24, 4: 28, 5: 32, 6: 51}[stop]

    with ExitStack() as stack:
        def sb(name, shape, dt=F32):
            return stack.enter_context(nc.sbuf_tensor(name, shape, dt))

        def sem(name):
            return stack.enter_context(nc.semaphore(name))

        X = sb("X", [P, T, D])
        H = sb("H", [P, T, D])
        T1 = sb("T1", [P, C, TOK])
        B1 = sb("B1", [P, C, TOK])
        pool_area = sb("pool_area", [P, 4 * 4096])
        W = sb("W", [P, NW, C, D])
        XN = sb("XN", [P, 2, D])
        vec = sb("vec", [P, len(VEC), C])
        row = sb("row", [P, len(ROW), D])
        scl = sb("scl", [P, NSCL])
        sml = sb("sml", [P, C, NSML])
        cst = sb("cst", [P, NCON])
        jb = sb("jb", [P, C, P])
        mk8 = sb("mk8", [P, KEYS], U8)
        mk = sb("mk", [P, KEYS])
        nm = sb("nm", [P, KEYS])
        half = sb("half", [P, R])
        bns = sb("bns", [P, 6])
        mv = sb("mv", [P, T, 2])
        ve = sb("ve", [P, 4, T])
        rs = sb("rs", [P, 4, T])
        tiny = sb("tiny", [P, 16, 64])
        rank_in = sb("rank_in", [P, 2, T, E * E])
        cw = sb("cw", [P, T, E + 1])
        dec = sb("dec", [P, 8, R])
        convm = sb("convm", [P, P])
        PS = stack.enter_context(nc.psum_tensor("PS", [P, 8, 512], F32))

        def area(first, *shape):
            n = int(np.prod(shape))
            v = pool_area[:, first:first + n]
            names = " ".join("abcd"[:len(shape)])
            return v if len(shape) == 1 else v.rearrange(f"p ({names}) -> p {names}", **{k: s for k, s in zip("abcd", shape)})

        B2, B3, B4, B5 = (area(4096 * i, C, TOK) for i in range(4))
        B3t = area(4096, T, D)
        B5t = area(3 * 4096, T, D)
        ident = cst[:, 0:P]

        def con_(name):
            a, n = CON[name]
            return cst[:, a:a + n]

        def v_(name):
            return vec[:, VEC.index(name), :]

        def r_(name):
            return row[:, ROW.index(name), :]

        def s_(name):
            a, n = SCL[name]
            return scl[:, a:a + n]

        def bc(ap, *shape):
            return ap.to_broadcast(shape)

        ready = sem("ready")
        act_drained = sem("act_drained")
        dve_drained = sem("dve_drained")
        drained = {"act": act_drained, "dve": dve_drained}
        w_full = [sem(f"w_full{i}") for i in range(NW)]
        const_in = sem("const_in")
        x_in = sem("x_in")
        ctx_t_in = [sem(f"ctx_t_in{i}") for i in range(NC1)]
        ctx_in = [sem(f"ctx_in{i}") for i in range(NC1)]
        ctx4_in = [sem(f"ctx4_in{i}") for i in range(NC4)]
        last_in = sem("last_in")
        vrow_in = [sem(f"vrow_in{i}") for i in range(NVR)]
        stored = sem("stored")
        dve_step = sem("dve_step")
        act_step = sem("act_step")
        pool_step = sem("pool_step")
        base_ready = sem("base_ready")
        power_ready = sem("power_ready")
        xn_ready = sem("xn_ready")
        bias_ready = sem("bias_ready")
        exp_ready = sem("exp_ready")
        prob_ready = sem("prob_ready")
        qk_scaled = sem("qk_scaled")
        qbd_ready = sem("qbd_ready")
        zero_ready = sem("zero_ready")
        setup_ready = sem("setup_ready")
        gated = sem("gated")

        norms = ["n1", "n2", "n3", "n4", "n6", "n5", "n7", "n8"]
        XNB = {}
        seq = {1: ["t1"], 2: ["t1", "t3"], 3: ["t1", "t3", "t4", "t6"], 4: ["t1", "t3", "t4", "t6", "t5"],
               5: ["t1", "t3", "t4", "t6", "t5", "t7"], 6: ["t1", "t3", "t4", "t6", "t5", "t7", "t8"]}[stop]
        for i, name in enumerate(seq):
            XNB[name] = i * T
        powers = {}
        for name in ["dec", "n1", "n2", "n2r", "uv", "n3", "n4", "n4r", "n6", "n5", "n7", "n8"]:
            powers[name] = len(powers) + 1
        soft = {}
        for t in range(T):
            soft["s", t] = len(soft) + 1
        for t in range(T):
            soft["s3", t] = len(soft) + 1
        soft["g3"] = len(soft) + 1
        for b in range(BATCH):
            soft["s4", b] = len(soft) + 1
        for t in range(T):
            soft["s5", t] = len(soft) + 1
        soft["r6"] = len(soft) + 1
        prob = {}
        for key in soft:
            if key not in ("g3", "r6"):
                prob[key] = len(prob) + 1

        def banks(key, n=1):
            b = J.bank[key]
            return PS[:, b, :] if n == 1 else PS[:, b:b + n, :]

        kslot = 3 * D
        assert 4096 + 4 * C * KEYS + 5 * kslot <= 4 * 4096
        CT = [area(4096 + i * C * KEYS, C, KEYS) for i in range(NC1 // 2)]
        CT += [H[:, :, :].rearrange("p a b -> p (a b)")[:, i * C * KEYS:(i + 1) * C * KEYS].rearrange("p (c k) -> p c k", c=C)
               for i in range(3)]
        CK = [area(4096 + 4 * C * KEYS + i * kslot, 3, D) for i in range(5)]
        NCT, NCK = len(CT), len(CK)
        P1 = sb("P1", [P, 2, KEYS])
        PT1 = sb("PT1", [P, 2, 3 * P])
        cs = tiny[:, 0, 0:T]

        o = 0
        KTb = []
        for i in range(2):
            KTb.append(area(o, C, KEYS)); o += C * KEYS
        Vb = []
        for i in range(2):
            Vb.append(area(o, KT, D)); o += KT * D
        CT4 = []
        for i in range(NC4):
            CT4.append(area(o, C, KEYS)); o += C * KEYS
        S4 = []
        for i in range(2):
            S4.append(area(o, C, KEYS)); o += C * KEYS
        PT4 = []
        for i in range(2):
            PT4.append(area(o, KT, D)); o += KT * D
        Qbd = []
        for i in range(2):
            Qbd.append(area(o, C, P)); o += C * P
        assert o <= 4 * 4096, o
        o = 0
        Hf = H[:, :, :].rearrange("p a b -> p (a b)")
        ctxl = Hf[:, 0:C * BATCH].rearrange("p (c b) -> p c b", c=C)
        VL = Hf[:, 512:1024]
        vrow = Hf[:, 1024:1024 + NVR * D].rearrange("p (n d) -> p n d", n=NVR)
        pl4 = Hf[:, 3072:3072 + 2 * D].rearrange("p (n d) -> p n d", n=2)

        qk2 = area(4096, T, 2 * R)
        sq = area(4096 + 512, T, 2 * R)
        ksq = area(4096 + 1024, T, 2 * P)
        AT = area(2 * 4096, T, P)
        HH = B5t

        def tok(t):
            return slice(t * P, (t + 1) * P)

        def grp(g):
            return slice(g * 512, (g + 1) * 512)

        block = stack.enter_context(nc.Block())

        @block.sync
        def _(sp):
            def load_unit(u):
                if u >= NW:
                    sp.wait_ge(ready, J.last[UNITS[u - NW]])
                sp.dma_start(W[:, u % NW, :, :], units[u]).then_inc(w_full[u % NW], 16)

            sp.dma_start(cst[:, :], con).then_inc(const_in, 16)
            for t in range(T):
                sp.dma_start(X[:, t, :], x[t]).then_inc(x_in, 16)
            sp.dma_start(vec[:, :, :], vecs).then_inc(const_in, 16)
            load_unit(0)
            load_unit(1)
            sp.dma_start(row[:, :, :], rows.rearrange("(o r) d -> o r d", o=1).to_broadcast([P, len(ROW), D])).then_inc(const_in, 16)
            sp.dma_start(scl[:, :], scalars.rearrange("(o r) -> o r", o=1).to_broadcast([P, NSCL])).then_inc(const_in, 16)
            sp.dma_start(sml[:, :, :], small).then_inc(const_in, 16)
            sp.dma_start(jb[:, :, :], jbd).then_inc(const_in, 16)
            for j in range(PB):
                sp.dma_start(mk8[j * SEQ:(j + 1) * SEQ, :], mask).then_inc(const_in, 16)
            for u in range(2, min(NW, n_units)):
                load_unit(u)
            for i in range(BATCH + PB):
                if i < BATCH:
                    if i >= NCT:
                        sp.wait_ge(ready, J.ready["s", (i - NCT) // PB])
                    sp.dma_start(CT[i % NCT], ctx_t[i]).then_inc(ctx_t_in[i % NCT], 16)
                b = i - PB
                if b >= 0:
                    if b >= NCK:
                        sp.wait_ge(ready, J.ready["u", (b - NCK) // PB])
                    sp.dma_start(CK[b % NCK][:, 0:KT, :], ctx[b, 0:KT * P, :].rearrange("(k p) d -> p k d", p=P)).then_inc(ctx_in[b % NCK], 16)
                    sp.dma_start(CK[b % NCK][0:1, KT, :], ctx[b, KT * P:KEYS, :]).then_inc(ctx_in[b % NCK], 16)
            for u in range(NW, min(28, n_units)):
                load_unit(u)
            if stop >= 4:
                sp.wait_ge(ready, J.ready["o2", 3, T - 1, 1])
                sp.dma_start(ctxl, ctx_last).then_inc(last_in, 16)
                for b in range(BATCH):
                    if b >= NC4:
                        sp.wait_ge(ready, J.ready["v4", b - NC4])
                    sp.dma_start(CT4[b % NC4], ctx_t[b]).then_inc(ctx4_in[b % NC4], 16)
                    if b == 1:
                        sp.wait_ge(act_drained, J.drain["vl",][1])
                    if b >= 1:
                        v = b - 1
                        if v >= NVR:
                            sp.wait_ge(ready, J.ready["o4", v - NVR])
                        sp.dma_start(vrow[0:1, v % NVR, :], VL[v:v + 1, :]).then_inc(vrow_in[v % NVR], 16)
                v = BATCH - 1
                sp.wait_ge(ready, J.ready["o4", v - NVR])
                sp.dma_start(vrow[0:1, v % NVR, :], VL[v:v + 1, :]).then_inc(vrow_in[v % NVR], 16)
                for u in range(28, n_units):
                    load_unit(u)
            last = {1: ("y",), 2: ("o1", 3), 3: ("o2", 3), 4: ("x4",), 5: ("x5",), 6: ("os",)}[stop]
            for t in range(T):
                key = last + (t,) + ((1,) if stop == 3 else ())
                sp.wait_ge(dve_drained, J.drain[key][1])
                sp.dma_start(out[t], X[:, t, :]).then_inc(stored, 16)
            sp.wait_ge(stored, 16 * T)

        @block.tensor
        def _(pe):
            def wait_banks(key):
                for eng, n in J.frees[key].items():
                    pe.wait_ge(drained[eng], n)

            def wait_unit(name):
                u = UNIT[name]
                pe.wait_ge(w_full[u % NW], 16 * (u // NW + 1))
                return W[:, u % NW, :, :]

            def transposes(name, src, ready_at):
                for t in range(T):
                    transpose_tile(name, t, src, ready_at)

            def transpose_tile(name, t, src, ready_at):
                pe.wait_ge(xn_ready, ready_at + t + 1)
                wait_banks((name, t))
                o_ = banks((name, t))
                for c in range(C):
                    mm = nc.tensor.transpose(o_[:, c * P:(c + 1) * P], src(t)[:, c * P:(c + 1) * P], ident)
                mm.then_inc(ready, 1)

            def feature_major(name, w, src, g, waits=()):
                for s, n in waits:
                    pe.wait_ge(s, n)
                for m in range(C):
                    wait_banks(name + (g, m))
                    for c in range(C):
                        mm = nc.tensor.matmul(banks(name + (g, m)), w[:, c, m * P:(m + 1) * P], src[:, c, grp(g)],
                                              start=(c == 0), stop=(c == C - 1))
                    mm.then_inc(ready, 1)

            def token_major(key, w, src, t, chunks=range(C)):
                wait_banks(key)
                for c in chunks:
                    mm = nc.tensor.matmul(banks(key), src[:, c, tok(t)], w[:, c, :],
                                          start=(c == chunks[0]), stop=(c == chunks[-1]))
                mm.then_inc(ready, 1)

            def after(key):
                eng, n = J.drain[key]
                return drained[eng], n

            def wait(key):
                pe.wait_ge(*after(key))

            xn = lambda t: XN[:, t % 2, :]
            pe.wait_ge(const_in, 16 * 10)
            w = None
            for g in range(G):
                for t in range(g * TG, g * TG + TG):
                    transpose_tile("t1", t, xn, XNB["t1"])
                w = wait_unit("0.wq")
                wait(("t1", g * TG + TG - 1))
                feature_major(("q",), w, T1, g)
            wait(("q", G - 1, C - 1))
            wait_banks(("c",))
            for t in range(T):
                for c in range(C):
                    mm = nc.tensor.matmul(banks(("c",))[:, t:t + 1], B1[:, c, tok(t)], v_("bk0")[:, c:c + 1],
                                          start=(c == 0), stop=(c == C - 1))
            mm.then_inc(ready, 1)
            w = wait_unit("0.wk")
            for g in range(G):
                feature_major(("qk",), w, B1, g)
            for t in range(T + 1):
                if t < T:
                    wait(("qk", t // TG, C - 1))
                    wait_banks(("s", t))
                    for j in range(PB):
                        b = t * PB + j
                        pe.wait_ge(ctx_t_in[b % NCT], 16 * (b // NCT + 1))
                        for c in range(C):
                            mm = nc.tensor.matmul(banks(("s", t))[j * SEQ:(j + 1) * SEQ, 0:KEYS],
                                                  B2[:, c, b * SEQ:(b + 1) * SEQ], CT[b % NCT][:, c, :],
                                                  start=(c == 0), stop=(c == C - 1))
                    mm.then_inc(ready, 1)
                if t >= 1:
                    v = t - 1
                    pe.wait_ge(prob_ready, prob["s", v])
                    wait_banks(("pt", v))
                    bk = banks(("pt", v))
                    for k in range(KT):
                        nc.tensor.transpose(bk[:, k * P:(k + 1) * P], P1[:, v % 2, k * P:(k + 1) * P], ident)
                    nc.tensor.transpose(bk[0:1, KT * P:(KT + 1) * P], P1[:, v % 2, KT * P:KEYS], ident).then_inc(ready, 1)
                    wait(("pt", v))
                    wait_banks(("u", v))
                    bk = banks(("u", v))
                    for j in range(PB):
                        b = v * PB + j
                        pe.wait_ge(ctx_in[b % NCK], 32 * (b // NCK + 1))
                        for c in range(C):
                            col = slice(c * P + j * SEQ, c * P + (j + 1) * SEQ)
                            for k in range(KT + 1):
                                n = P if k < KT else 1
                                mm = nc.tensor.matmul(bk[:, col], CK[b % NCK][0:n, k, c * P:(c + 1) * P],
                                                      PT1[0:n, v % 2, k * P + j * SEQ:k * P + (j + 1) * SEQ],
                                                      start=(k == 0), stop=(k == KT))
                    mm.then_inc(ready, 1)
            w = wait_unit("0.wv")
            for t in range(T):
                wait(("u", t))
                token_major(("y", t), w, T1, t)
            if stop == 1:
                return

            def small_(name):
                a, n = SML[name]
                return sml[:, :, a:a + n]

            for t in range(T):
                pe.wait_ge(qk_scaled, t + 1)
                wait_banks(("t2", t))
                for c in range(C):
                    mm = nc.tensor.transpose(banks(("t2", t))[:, c * P:(c + 1) * P], HH[:, t, c * P:(c + 1) * P], ident)
                mm.then_inc(ready, 1)
            for t in range(T):
                wait(("t2", t))
                wait_banks(("uv", t))
                for c in range(C):
                    mm = nc.tensor.matmul(banks(("uv", t))[:, 0:2 * R], T1[:, c, tok(t)], small_("uv")[:, c, :],
                                          start=(c == 0), stop=(c == C - 1))
                mm.then_inc(ready, 1)
            for t in range(T):
                pe.wait_ge(qk_scaled, T + 1)
                wait_banks(("kq", t))
                for i in range(2):
                    mm = nc.tensor.transpose(banks(("kq", t))[0:R, i * P:(i + 1) * P], qk2[:, t, i * R:(i + 1) * R], ident)
                mm.then_inc(ready, 1)
            for t in range(T):
                wait(("kq", t))
                wait_banks(("A", t))
                nc.tensor.matmul(banks(("A", t))[:, 0:P], ksq[0:R, t, P:2 * P], ksq[0:R, t, 0:P],
                                 start=True, stop=True).then_inc(ready, 1)
            for t in range(T):
                wait(("A", t))
                wait_banks(("d", t))
                for c in range(C):
                    mm = nc.tensor.matmul(banks(("d", t))[:, c * P:(c + 1) * P], HH[:, t, c * P:(c + 1) * P], AT[:, t, :],
                                          start=True, stop=True)
                mm.then_inc(ready, 1)
            w = wait_unit("1.proj")
            for t in range(T):
                wait(("d", t))
                token_major(("pr", t), w, B1, t)
            transposes("t3", xn, XNB["t3"])
            wait(("t3", T - 1))
            for b in range(4):
                w = wait_unit(f"1.w1.{b}")
                for g in range(G):
                    feature_major(("h1", b), w, T1, g)
                w = wait_unit(f"1.w2.{b}")
                for t in range(T):
                    wait(("h1", b, t // TG, C - 1))
                    token_major(("o1", b, t), w, B1, t)
            if stop == 2:
                return

            def self_scores(name, t, pairs):
                wait_banks((name, t))
                bk = banks((name, t), 4)
                for hb in range(C):
                    for hl in range(HG):
                        for i, (a, k) in enumerate(pairs):
                            mm = nc.tensor.matmul(bk[:, hl, hb * P:(hb + 1) * P], a[hl * DK:(hl + 1) * DK, hb, tok(t)],
                                                  k[hl * DK:(hl + 1) * DK, hb, tok(t)], start=(i == 0), stop=(i == len(pairs) - 1))
                mm.then_inc(ready, 1)

            def self_values(name, t, V, PTs):
                wait_banks((name, t))
                bk = banks((name, t), 4)
                for hb in range(C):
                    for j in range(PB):
                        mm = nc.tensor.matmul(bk[:, j, hb * P:(hb + 1) * P], V[j * SEQ:(j + 1) * SEQ, t, hb * P:(hb + 1) * P],
                                              PTs[j * SEQ:(j + 1) * SEQ, hb * P:(hb + 1) * P], start=True, stop=True)
                mm.then_inc(ready, 1)

            transposes("t4", xn, XNB["t4"])
            wait(("t4", T - 1))
            for n in ("q", "k"):
                w = wait_unit(f"2.{n}")
                for g in range(G):
                    feature_major((f"{n}3",), w, T1, g)
            w = wait_unit("2.v")
            for t in range(T):
                token_major(("v3", t), w, T1, t)
            wait(("v3", T - 1))
            for t in range(T + 1):
                if t < T:
                    self_scores("s3", t, [(B1, B2)])
                if t >= 1:
                    pe.wait_ge(prob_ready, prob["s3", t - 1])
                    self_values("o3", t - 1, B3t, B4[:, 2 + (t - 1) % 2, 0:D])
            w = wait_unit("2.o")
            for t in range(T):
                wait(("o3", t))
                token_major(("x3", t), w, T1, t)
            transposes("t6", xn, XNB["t6"])
            wait(("t6", T - 1))
            wait_banks(("g3",))
            for t in range(T):
                for c in range(C):
                    mm = nc.tensor.matmul(banks(("g3",))[:, t * E:(t + 1) * E], T1[:, c, tok(t)], small_("wg")[:, c, :],
                                          start=(c == 0), stop=(c == C - 1))
            mm.then_inc(ready, 1)
            for b in range(4):
                w = wait_unit(f"2.w1.{b}")
                for g in range(G):
                    feature_major(("h2", b), w, T1, g)
                w = wait_unit(f"2.w2.{b}")
                for t in range(T):
                    wait(("h2", b, t // TG, C - 1))
                    for e in range(2):
                        token_major(("o2", b, t, e), w, B1, t, chunks=[2 * e, 2 * e + 1])
            if stop == 3:
                return

            transposes("t5", xn, XNB["t5"])
            wait(("t5", T - 1))
            w = wait_unit("3.q")
            for g in range(G):
                feature_major(("q4",), w, T1, g)
            wv = wait_unit("3.v")
            pe.wait_ge(last_in, 16)
            wait_banks(("vl",))
            for c in range(C):
                mm = nc.tensor.matmul(banks(("vl",))[0:BATCH, :], ctxl[:, c, :], wv[:, c, :], start=(c == 0), stop=(c == C - 1))
            mm.then_inc(ready, 1)
            wk = wait_unit("3.k")
            for b in range(BATCH + 1):
                if b < BATCH:
                    pe.wait_ge(ctx4_in[b % NC4], 16 * (b // NC4 + 1))
                    ct = CT4[b % NC4]
                    wait_banks(("k4", b))
                    bk = banks(("k4", b), 4)
                    for m in range(C):
                        for c in range(C):
                            mm = nc.tensor.matmul(bk[:, m, 0:KEYS], wk[:, c, m * P:(m + 1) * P], ct[:, c, :],
                                                  start=(c == 0), stop=(c == C - 1))
                    mm.then_inc(ready, 1)
                    wait_banks(("v4", b))
                    bk = banks(("v4", b), 2)
                    for k in range(KT):
                        for c in range(C):
                            mm = nc.tensor.matmul(bk[:, k, :], ct[:, c, k * P:(k + 1) * P], wv[:, c, :],
                                                  start=(c == 0), stop=(c == C - 1))
                    mm.then_inc(ready, 1)
                    wait(("k4", b))
                    pe.wait_ge(qbd_ready, b + 1)
                    wait_banks(("s4", b))
                    bk = banks(("s4", b), 4)
                    for hb in range(C):
                        mm = nc.tensor.matmul(bk[:, hb, 0:KEYS], Qbd[b % 2][:, hb, :], KTb[b % 2][:, hb, :], start=True, stop=True)
                    mm.then_inc(ready, 1)
                if b >= 1:
                    v = b - 1
                    pe.wait_ge(prob_ready, prob["s4", v])
                    wait_banks(("p4", v))
                    bk = banks(("p4", v), 2)
                    for k in range(KT):
                        for hb in range(C):
                            mm = nc.tensor.transpose(bk[:, k, hb * P:(hb + 1) * P], S4[v % 2][:, hb, k * P:(k + 1) * P], ident)
                    mm.then_inc(ready, 1)
                    wait_banks(("l4", v))
                    bk = banks(("l4", v))
                    for hb in range(C):
                        mm = nc.tensor.transpose(bk[0:1, hb * P:(hb + 1) * P], S4[v % 2][:, hb, KT * P:KEYS], ident)
                    mm.then_inc(ready, 1)
                    wait(("l4", v))
                    wait(("v4", v))
                    pe.wait_ge(vrow_in[v % NVR], 16 * (v // NVR + 1))
                    wait_banks(("o4", v))
                    bk = banks(("o4", v))
                    for hb in range(C):
                        hs = slice(hb * P, (hb + 1) * P)
                        for k in range(KT):
                            nc.tensor.matmul(bk[:, hs], Vb[v % 2][:, k, hs], PT4[v % 2][:, k, hs], start=(k == 0), stop=False)
                        mm = nc.tensor.matmul(bk[:, hs], vrow[0:1, v % NVR, hs], pl4[0:1, v % 2, hs], start=False, stop=True)
                    mm.then_inc(ready, 1)
            w = wait_unit("3.o")
            wait(("o4", BATCH - 1))
            for t in range(T):
                token_major(("x4", t), w, T1, t)
            if stop == 4:
                return

            transposes("t7", xn, XNB["t7"])
            wait(("t7", T - 1))
            for n in ("q", "k"):
                w = wait_unit(f"4.{n}")
                for g in range(G):
                    feature_major((f"{n}5",), w, T1, g)
            w = wait_unit("4.v")
            for t in range(T):
                token_major(("v5", t), w, T1, t)
            wait(("k5", G - 1, C - 1))
            for g in range(G):
                for m in range(C):
                    wait_banks(("qj", g, m))
                    nc.tensor.matmul(banks(("qj", g, m)), jb[:, m, :], B3[:, m, grp(g)], start=True, stop=True).then_inc(ready, 1)
            wait(("v5", T - 1))
            wait(("qj", G - 1, C - 1))
            QJ = Hf.rearrange("p (c t) -> p c t", c=C)
            for t in range(T + 1):
                if t < T:
                    self_scores("s5", t, [(B1, B2), (QJ, B4)])
                if t >= 1:
                    pe.wait_ge(prob_ready, prob["s5", t - 1])
                    self_values("o5", t - 1, B5t, B3[:, 2 + (t - 1) % 2, 0:D])
            w = wait_unit("4.o")
            for t in range(T):
                wait(("o5", t))
                token_major(("x5", t), w, T1, t)
            if stop == 5:
                return

            transposes("t8", xn, XNB["t8"])
            wait(("t8", T - 1))
            wait_banks(("r6",))
            for t in range(T):
                for c in range(C):
                    mm = nc.tensor.matmul(banks(("r6",))[:, t * (E + 1):(t + 1) * (E + 1)], T1[:, c, tok(t)], small_("router")[:, c, :],
                                          start=(c == 0), stop=(c == C - 1))
            mm.then_inc(ready, 1)
            for b in range(E):
                w = wait_unit(f"5.w1.{b}")
                for g in range(G):
                    feature_major(("h3", b), w, T1, g)
                w = wait_unit(f"5.w2.{b}")
                for t in range(T):
                    wait(("h3", b, t // TG, C - 1))
                    token_major(("o6", b, t), w, B1, t)
            wg = wait_unit("5.gate")
            wu = wait_unit("5.up")
            for g in range(G):
                for m in range(C):
                    for n, w in (("sg", wg), ("su", wu)):
                        wait_banks((n, g, m))
                        for c in range(C):
                            mm = nc.tensor.matmul(banks((n, g, m)), w[:, c, m * P:(m + 1) * P], T1[:, c, grp(g)],
                                                  start=(c == 0), stop=(c == C - 1))
                        mm.then_inc(ready, 1)
            w = wait_unit("5.down")
            for t in range(T):
                wait(("su", t // TG, C - 1))
                token_major(("os", t), w, B1, t)

        @block.scalar
        def _(act):
            def drain_features(name, dst, func=ACT.Identity, bias=None, scale=1.0):
                for g in range(G):
                    for m in range(C):
                        act.wait_ge(ready, J.ready[name + (g, m)])
                        b = 0.0 if bias is None else bias[:, m:m + 1]
                        nc.scalar.activation(dst[:, m, grp(g)], banks(name + (g, m)), func, bias=b,
                                             scale=scale).then_inc(act_drained, 1)

            def drain_transposes(name, t):
                act.wait_ge(ready, J.ready[name, t])
                nc.scalar.copy(T1[:, :, tok(t)], banks((name, t)).rearrange("p (c n) -> p c n", c=C)).then_inc(act_drained, 1)

            act.wait_ge(const_in, 16 * 10)
            nc.scalar.activation(scl[:, 0:2 * R + 1], scl[:, 0:2 * R + 1], ACT.Exp, scale=-1.0).then_inc(exp_ready, 1)
            for g in range(G):
                for t in range(g * TG, g * TG + TG):
                    drain_transposes("t1", t)
                for m in range(C):
                    act.wait_ge(ready, J.ready["q", g, m])
                    nc.scalar.activation(B1[:, m, grp(g)], banks(("q", g, m)), ACT.Identity,
                                         bias=v_("bq0")[:, m:m + 1]).then_inc(act_drained, 1)
            drain_features(("qk",), B2)
            for t in range(T + 1):
                if t < T:
                    act.wait_ge(bias_ready, soft["s", t])
                    nc.scalar.activation(P1[:, t % 2, :], banks(("s", t))[:, 0:KEYS], ACT.Exp, bias=tiny[:, 2 + t % 2, 0:1],
                                         scale=float(D) ** -0.5, accum_out=tiny[:, 4 + t % 2, 0:1]).then_inc(act_drained, 1)
                if t >= 1:
                    v = t - 1
                    act.wait_ge(ready, J.ready["pt", v])
                    nc.scalar.copy(PT1[:, v % 2, 0:KT * P], banks(("pt", v))[:, 0:KT * P]).then_inc(act_step, 1)
                    nc.scalar.copy(PT1[0:1, v % 2, KT * P:], banks(("pt", v))[0:1, KT * P:(KT + 1) * P]).then_inc(act_drained, 1)
            if stop == 1:
                return
            for t in range(T):
                act.wait_ge(ready, J.ready["kq", t])
                nc.scalar.copy(ksq[0:R, t, :], banks(("kq", t))[0:R, 0:2 * P]).then_inc(act_drained, 1)
            for b in range(4):
                drain_features(("h1", b), B1, ACT.Gelu_apprx_tanh, v_(f"mb1{b}"))
            if stop == 2:
                return
            drain_features(("q3",), B1)
            drain_features(("k3",), B2)
            for t in range(T):
                act.wait_ge(ready, J.ready["v3", t])
                nc.scalar.copy(B3t[:, t, :], banks(("v3", t))).then_inc(act_drained, 1)
            for t in range(T):
                if t >= 2:
                    act.wait_ge(prob_ready, prob["s3", t - 2])
                act.wait_ge(ready, J.ready["s3", t])
                bk = banks(("s3", t), 4)
                for j in range(PB):
                    js = slice(j * SEQ, (j + 1) * SEQ)
                    src = bk[js, :, :].rearrange("p l (h k) -> p l h k", h=C)[:, :, :, js]
                    dst = B4[js, t % 2, 0:D].rearrange("p (h l k) -> p l h k", l=HG, k=SEQ)
                    mm = nc.scalar.activation(dst, src, ACT.Copy, scale=float(DK) ** -0.5)
                    mm.then_inc(act_drained if j == PB - 1 else act_step, 1)
                act.wait_ge(bias_ready, soft["s3", t])
                nc.scalar.activation(B4[:, t % 2, 0:D], B4[:, t % 2, 0:D], ACT.Exp).then_inc(exp_ready, 1)
            act.wait_ge(bias_ready, soft["g3"])
            nc.scalar.activation(tiny[:, 6, :], tiny[:, 6, :], ACT.Exp).then_inc(exp_ready, 1)
            for b in range(4):
                drain_features(("h2", b), B1, ACT.Relu)
            if stop == 3:
                return
            for t in range(T):
                drain_transposes("t5", t)
            drain_features(("q4",), B1, scale=float(DK) ** -0.5)
            act.wait_ge(ready, J.ready["vl",])
            nc.scalar.copy(VL[0:BATCH, :], banks(("vl",))[0:BATCH, :]).then_inc(act_drained, 1)
            for b in range(BATCH + 1):
                if b < BATCH:
                    act.wait_ge(ready, J.ready["k4", b])
                    nc.scalar.copy(KTb[b % 2], banks(("k4", b), 4)[:, :, 0:KEYS]).then_inc(act_drained, 1)
                if b >= 1:
                    v = b - 1
                    act.wait_ge(ready, J.ready["p4", v])
                    nc.scalar.copy(PT4[v % 2], banks(("p4", v), 2)).then_inc(act_drained, 1)
                    act.wait_ge(ready, J.ready["l4", v])
                    nc.scalar.copy(pl4[0:1, v % 2, :], banks(("l4", v))[0:1, :]).then_inc(act_drained, 1)
                if b < BATCH:
                    act.wait_ge(bias_ready, soft["s4", b])
                    for hb in range(C):
                        nc.scalar.activation(S4[b % 2][:, hb, :], S4[b % 2][:, hb, :], ACT.Exp, bias=tiny[:, 7 + b % 2, hb:hb + 1],
                                             accum_out=tiny[:, 9 + b % 2, hb:hb + 1]).then_inc(exp_ready if hb == C - 1 else act_step, 1)
            if stop == 4:
                return
            for t in range(T):
                drain_transposes("t7", t)
            for n, b, dst, th in (("q5", "bq5", B1, B3), ("k5", "bk5", B2, B4)):
                for g in range(G):
                    for m in range(C):
                        act.wait_ge(ready, J.ready[n, g, m])
                        nc.scalar.activation(dst[:, m, grp(g)], banks((n, g, m)), ACT.Identity, bias=v_(b)[:, m:m + 1]).then_inc(act_step, 1)
                        nc.scalar.activation(th[:, m, grp(g)], banks((n, g, m)), ACT.Tanh, bias=v_(b)[:, m:m + 1]).then_inc(act_drained, 1)
            QJ = Hf.rearrange("p (c t) -> p c t", c=C)
            act.wait_ge(setup_ready, 1)
            for g in range(G):
                for m in range(C):
                    act.wait_ge(ready, J.ready["qj", g, m])
                    nc.scalar.activation(QJ[:, m, grp(g)], banks(("qj", g, m)), ACT.Copy, scale=tiny[:, 11, 0:1]).then_inc(act_drained, 1)
            for t in range(T + 1):
                if t < T:
                    act.wait_ge(bias_ready, soft["s5", t])
                    nc.scalar.activation(B3[:, t % 2, 0:D], B3[:, t % 2, 0:D], ACT.Exp).then_inc(exp_ready, 1)
                if t >= 1:
                    v = t - 1
                    act.wait_ge(ready, J.ready["o5", v])
                    bk = banks(("o5", v), 4)
                    for hl in range(HG):
                        hs = slice(hl * DK, (hl + 1) * DK)
                        src = bk[hs, :, :].rearrange("p j (h q) -> p j h q", h=C)[:, :, :, hs]
                        dst = T1[hs, :, tok(v)].rearrange("p h (j q) -> p j h q", j=PB)
                        nc.scalar.copy(dst, src).then_inc(act_drained if hl == HG - 1 else act_step, 1)
            if stop == 5:
                return
            for t in range(T):
                drain_transposes("t8", t)
            act.wait_ge(bias_ready, soft["r6"])
            nc.scalar.activation(tiny[:, 6, :], tiny[:, 6, :], ACT.Exp).then_inc(exp_ready, 1)
            nc.scalar.activation(tiny[:, 12, 0:T], tiny[:, 12, 0:T], ACT.Exp, scale=-1.0).then_inc(exp_ready, 1)
            for b in range(E):
                drain_features(("h3", b), B1, ACT.Silu)
            drain_features(("sg",), B2, ACT.Silu)

        @block.gpsimd
        def _(pool):
            def power(name, out_, base, n):
                pool.wait_ge(base_ready, powers[name])
                nc.gpsimd.tensor_tensor(out_, base, half[:, 0:n], ALU.pow).then_inc(power_ready, 1)

            pool.wait_ge(base_ready, powers["dec"])
            nc.gpsimd.tensor_tensor(dec[:, 4, :], dec[:, 0, :], dec[:, 2, :], ALU.pow).then_inc(pool_step, 1)
            nc.gpsimd.tensor_tensor(dec[:, 5, :], dec[:, 0, :], dec[:, 3, :], ALU.pow).then_inc(power_ready, 1)
            power("n1", rs[:, 0, :], ve[:, 0, :], T)
            if stop == 1:
                return
            power("n2", rs[:, 0, :], ve[:, 0, :], T)
            power("n2r", rs[:, 1, :], ve[:, 1, :], T)
            pool.wait_ge(base_ready, powers["uv"])
            nc.gpsimd.tensor_tensor(tiny[:, 13, 0:2 * T], tiny[:, 14, 0:2 * T], half[:, 0:2 * T], ALU.pow).then_inc(power_ready, 1)
            power("n3", rs[:, 0, :], ve[:, 0, :], T)
            if stop == 2:
                return
            power("n4", rs[:, 0, :], ve[:, 0, :], T)
            power("n4r", rs[:, 1, :], ve[:, 1, :], T)
            power("n6", rs[:, 0, :], ve[:, 0, :], T)
            if stop == 3:
                return
            pool.wait_ge(ready, J.ready["o2", 3, T - 1, 1])
            for i in range(2):
                nc.gpsimd.memset(Qbd[i], 0.0).then_inc(zero_ready, 1)
            power("n5", rs[:, 0, :], ve[:, 0, :], T)
            pool.wait_ge(zero_ready, 2)
            pool.wait_ge(act_drained, J.drain["q4", G - 1, C - 1][1])
            for b in range(BATCH):
                if b >= 2:
                    pool.wait_ge(ready, J.ready["s4", b - 2])
                for hl in range(HG):
                    hs = slice(hl * DK, (hl + 1) * DK)
                    nc.gpsimd.tensor_copy(Qbd[b % 2][hs, :, hs], B1[hs, :, b * SEQ:(b + 1) * SEQ]).then_inc(
                        qbd_ready if hl == HG - 1 else pool_step, 1)
            if stop == 4:
                return
            power("n7", rs[:, 0, :], ve[:, 0, :], T)
            if stop == 5:
                return
            power("n8", rs[:, 0, :], ve[:, 0, :], T)

        @block.vector
        def _(dve):
            steps = [0]

            def link(ins):
                steps[0] += 1
                ins.then_inc(dve_step, 1)
                dve.wait_ge(dve_step, steps[0])

            def step(ins):
                steps[0] += 1
                ins.then_inc(dve_step, 1)

            def stats(src, t):
                link(nc.vector.bn_stats(bns[:, :], src[:, t, :]))
                link(nc.vector.bn_aggr(mv[:, t, :], bns[:, :]))

            def normalise(name, job, src, eps):
                nc.vector.tensor_scalar(ve[:, 0, :], mv[:, :, 1], eps, None, ALU.add).then_inc(base_ready, 1)
                dve.wait_ge(power_ready, powers[name])
                for t in range(T):
                    if t >= 2:
                        dve.wait_ge(ready, J.ready[job, t - 2])
                    nc.vector.tensor_scalar(XN[:, t % 2, :], src[:, t, :], mv[:, t, 0:1], rs[:, 0, t:t + 1],
                                            ALU.subtract, ALU.mult).then_inc(xn_ready, 1)

            def wait(sem_, n):
                dve.wait_ge(sem_, n)

            def fence():
                dve.wait_ge(dve_step, steps[0])

            link(nc.vector.memset(half[:, :], -0.5))
            dve.wait_ge(const_in, 16 * 10)
            dve.wait_ge(exp_ready, 1)
            link(nc.vector.tensor_scalar(scl[:, 0:2 * R + 1], scl[:, 0:2 * R + 1], 1.0, None, ALU.add))
            link(nc.vector.reciprocal(scl[:, 0:2 * R + 1], scl[:, 0:2 * R + 1]))
            step(nc.vector.tensor_scalar(dec[:, 0, :], s_("decay"), 0.15, 1.0, ALU.max, ALU.min))
            link(nc.vector.memset(dec[:, 1, :], 1.0))
            link(nc.vector.tensor_scalar(dec[:, 2, :], dec[:, 1, :], con_("pos"), None, ALU.mult))
            nc.vector.tensor_scalar(dec[:, 3, :], dec[:, 2, :], -1.0, None, ALU.mult).then_inc(base_ready, 1)
            dve.wait_ge(power_ready, powers["dec"])
            link(nc.vector.tensor_tensor(dec[:, 4, :], dec[:, 4, :], s_("alpha"), ALU.mult))
            link(nc.vector.tensor_scalar(s_("kern"), s_("kern"), s_("gate"), None, ALU.mult))
            link(nc.vector.tensor_scalar(convm[:, :], con_("shift")[:, 0:P], s_("kern")[:, 0:1], None, ALU.mult))
            for m in range(1, 4):
                link(nc.vector.scalar_tensor_tensor(convm[:, :], con_("shift")[:, m * P:(m + 1) * P], s_("kern")[:, m:m + 1],
                                                    convm[:, :], ALU.mult, ALU.add))
            link(nc.vector.tensor_copy(mk[:, :], mk8[:, :]))
            step(nc.vector.tensor_scalar(nm[:, :], mk[:, :], 1.0, 1e9, ALU.subtract, ALU.mult))
            nc.vector.tensor_scalar(tiny[:, 11, 0:1], s_("lam"), float(DK) ** 0.5, None, ALU.mult).then_inc(setup_ready, 1)

            dve.wait_ge(x_in, 16 * T)
            for t in range(T):
                stats(X, t)
            normalise("n1", "t1", X, 1e-5)
            dve.wait_ge(ready, J.ready["c",])
            isd = float(D) ** -0.5
            nc.vector.tensor_scalar(cs, banks(("c",))[:, 0:T], isd, None, ALU.mult).then_inc(dve_drained, 1)
            dve.wait_ge(dve_drained, J.drain["c",][1])

            def u_drain(v):
                dve.wait_ge(ready, J.ready["u", v])
                nc.vector.tensor_copy(T1[:, :, tok(v)], banks(("u", v)).rearrange("p (c n) -> p c n", c=C)).then_inc(dve_drained, 1)

            for t in range(T):
                dve.wait_ge(ready, J.ready["s", t])
                link(nc.vector.reduce_max(tiny[:, 1, 0:1], banks(("s", t))[:, 0:KEYS], AX_X))
                link(nc.vector.scalar_tensor_tensor(tiny[:, 1, 1:2], tiny[:, 1, 0:1], isd, cs[:, t:t + 1], ALU.mult, ALU.add))
                nc.vector.scalar_tensor_tensor(tiny[:, 2 + t % 2, 0:1], tiny[:, 1, 1:2], -1.0, cs[:, t:t + 1],
                                               ALU.mult, ALU.add).then_inc(bias_ready, 1)
                dve.wait_ge(act_drained, J.drain["s", t][1])
                link(nc.vector.reciprocal(tiny[:, 1, 2:3], tiny[:, 4 + t % 2, 0:1]))
                nc.vector.tensor_scalar(P1[:, t % 2, :], P1[:, t % 2, :], tiny[:, 1, 2:3], None, ALU.mult).then_inc(prob_ready, 1)
                if t >= 1:
                    u_drain(t - 1)
            u_drain(T - 1)

            def residual(key, dst, bias, fin=None, then=None):
                t = key[1] if fin is None else fin
                dve.wait_ge(ready, J.ready[key])
                if bias is None:
                    nc.vector.tensor_tensor(dst[:, t, :], banks(key), dst[:, t, :], ALU.add).then_inc(dve_drained, 1)
                else:
                    link(nc.vector.tensor_tensor(dst[:, t, :], banks(key), dst[:, t, :], ALU.add))
                    nc.vector.tensor_tensor(dst[:, t, :], dst[:, t, :], bias, ALU.add).then_inc(dve_drained, 1)

            for t in range(T):
                residual(("y", t), X, r_("bv0"))
                if stop > 1:
                    dve.wait_ge(dve_drained, J.drain["y", t][1])
                    stats(X, t)
            if stop == 1:
                return

            def second_norm(n1, n2, eps2):
                nc.vector.tensor_scalar(ve[:, 0, :], mv[:, :, 1], 1e-5, None, ALU.add).then_inc(base_ready, 1)
                dve.wait_ge(power_ready, powers[n1])
                link(nc.vector.tensor_tensor(ve[:, 2, :], mv[:, :, 1], rs[:, 0, :], ALU.mult))
                link(nc.vector.tensor_tensor(ve[:, 2, :], ve[:, 2, :], rs[:, 0, :], ALU.mult))
                nc.vector.tensor_scalar(ve[:, 1, :], ve[:, 2, :], eps2, None, ALU.add).then_inc(base_ready, 1)
                dve.wait_ge(power_ready, powers[n2])

            second_norm("n2", "n2r", 1e-6)
            for t in range(T):
                link(nc.vector.tensor_scalar(H[:, t, :], X[:, t, :], mv[:, t, 0:1], rs[:, 0, t:t + 1], ALU.subtract, ALU.mult))
                nc.vector.tensor_scalar(HH[:, t, :], H[:, t, :], rs[:, 1, t:t + 1], None, ALU.mult).then_inc(qk_scaled, 1)

            def drain_scaled(key, dst, w, b=None):
                t = key[1]
                dve.wait_ge(ready, J.ready[key])
                src = banks(key).rearrange("p (c n) -> p c n", c=C)
                if b is None:
                    nc.vector.tensor_tensor(dst[:, :, tok(t)], src, bc(w.unsqueeze(2), P, C, P), ALU.mult).then_inc(dve_drained, 1)
                else:
                    link(nc.vector.tensor_tensor(dst[:, :, tok(t)], src, bc(w.unsqueeze(2), P, C, P), ALU.mult))
                    nc.vector.tensor_tensor(dst[:, :, tok(t)], dst[:, :, tok(t)], bc(b.unsqueeze(2), P, C, P), ALU.add).then_inc(dve_drained, 1)

            for t in range(T):
                drain_scaled(("t2", t), T1, v_("norm1"))
            for t in range(T):
                dve.wait_ge(ready, J.ready["uv", t])
                nc.vector.tensor_copy(qk2[:, t, :], banks(("uv", t))[:, 0:2 * R]).then_inc(dve_drained, 1)
            dve.wait_ge(dve_drained, J.drain["uv", T - 1][1])
            link(nc.vector.tensor_tensor(sq, qk2, qk2, ALU.mult))
            link(nc.vector.reduce_sum(tiny[:, 15, 0:2 * T].rearrange("p (t i) -> p t i", i=2), sq.rearrange("p t (i r) -> p t i r", i=2), AX_X))
            nc.vector.tensor_scalar(tiny[:, 14, 0:2 * T], tiny[:, 15, 0:2 * T], 1e-16, None, ALU.max).then_inc(base_ready, 1)
            dve.wait_ge(power_ready, powers["uv"])
            q4d = qk2.rearrange("p t (i r) -> p t i r", i=2)
            link(nc.vector.tensor_tensor(qk2.rearrange("p t (i r) -> p (t i) r", i=2), qk2.rearrange("p t (i r) -> p (t i) r", i=2),
                                         bc(tiny[:, 13, 0:2 * T].unsqueeze(2), P, 2 * T, R), ALU.mult))
            link(nc.vector.tensor_tensor(q4d[:, :, 0, :], q4d[:, :, 0, :], bc(dec[:, 4:5, :], P, T, R), ALU.mult))
            nc.vector.tensor_tensor(q4d[:, :, 1, :], q4d[:, :, 1, :], bc(dec[:, 5:6, :], P, T, R), ALU.mult).then_inc(qk_scaled, 1)
            for t in range(T):
                dve.wait_ge(ready, J.ready["A", t])
                link(nc.vector.tensor_tensor(AT[:, t, :], banks(("A", t))[:, 0:P], con_("lower"), ALU.mult))
                nc.vector.tensor_tensor(AT[:, t, :], AT[:, t, :], convm[:, :], ALU.add).then_inc(dve_drained, 1)
            for t in range(T):
                drain_scaled(("d", t), B1, v_("norm1"))
            for t in range(T):
                residual(("pr", t), H, r_("proj_b"))
                dve.wait_ge(dve_drained, J.drain["pr", t][1])
                stats(H, t)
                step(nc.vector.tensor_tensor(X[:, t, :], X[:, t, :], H[:, t, :], ALU.add))
            link(nc.vector.tensor_tensor(ve[:, 2, :], mv[:, :, 0], mv[:, :, 0], ALU.mult))
            link(nc.vector.tensor_tensor(ve[:, 2, :], ve[:, 2, :], mv[:, :, 1], ALU.add))
            nc.vector.tensor_scalar(ve[:, 0, :], ve[:, 2, :], 1e-6, None, ALU.add).then_inc(base_ready, 1)
            dve.wait_ge(power_ready, powers["n3"])
            for t in range(T):
                if t >= 2:
                    dve.wait_ge(ready, J.ready["t3", t - 2])
                nc.vector.tensor_scalar(XN[:, t % 2, :], H[:, t, :], rs[:, 0, t:t + 1], None, ALU.mult).then_inc(xn_ready, 1)
            for t in range(T):
                drain_scaled(("t3", t), T1, v_("norm2"))
            for b in range(4):
                for t in range(T):
                    if b:
                        dve.wait_ge(dve_drained, J.drain["o1", b - 1, t][1])
                    residual(("o1", b, t), X, r_("mb2") if b == 3 else None, fin=t)
                    if b == 3 and stop > 2:
                        dve.wait_ge(dve_drained, J.drain["o1", b, t][1])
                        stats(X, t)
            if stop == 2:
                return

            second_norm("n4", "n4r", 1e-5)
            for t in range(T):
                link(nc.vector.tensor_scalar(H[:, t, :], X[:, t, :], mv[:, t, 0:1], rs[:, 0, t:t + 1], ALU.subtract, ALU.mult))
                if t >= 2:
                    dve.wait_ge(ready, J.ready["t4", t - 2])
                nc.vector.tensor_scalar(XN[:, t % 2, :], H[:, t, :], rs[:, 1, t:t + 1], None, ALU.mult).then_inc(xn_ready, 1)
            for t in range(T):
                drain_scaled(("t4", t), T1, v_("g1"), v_("b1"))

            def softmax(name, t, SC, PTs):
                s3 = SC.rearrange("p (h k) -> p h k", k=SEQ)
                link(nc.vector.reduce_max(tiny[:, 1, 0:HEADS], s3, AX_X))
                nc.vector.tensor_tensor(s3, s3, bc(tiny[:, 1, 0:HEADS].unsqueeze(2), P, HEADS, SEQ), ALU.subtract).then_inc(bias_ready, 1)
                dve.wait_ge(exp_ready, exps[name, t])
                link(nc.vector.reduce_sum(tiny[:, 1, 16:32], s3, AX_X))
                link(nc.vector.reciprocal(tiny[:, 1, 32:48], tiny[:, 1, 16:32]))
                link(nc.vector.tensor_tensor(s3, s3, bc(tiny[:, 1, 32:48].unsqueeze(2), P, HEADS, SEQ), ALU.mult))
                if t >= 2:
                    dve.wait_ge(ready, J.ready[{"s3": "o3", "s5": "o5"}[name], t - 2])
                nc.vector.transpose(PTs, SC).then_inc(prob_ready, 1)

            exps = {}
            for t in range(T):
                exps["s3", t] = len(exps) + 2
            exps["g3"] = len(exps) + 2
            for b in range(BATCH):
                exps["s4", b] = len(exps) + 2
            for t in range(T):
                exps["s5", t] = len(exps) + 2
            exps["r6"] = len(exps) + 2
            exps["sig"] = len(exps) + 2

            def o_drain(v):
                dve.wait_ge(ready, J.ready["o3", v])
                bk = banks(("o3", v), 4)
                for hl in range(HG):
                    hs = slice(hl * DK, (hl + 1) * DK)
                    src = bk[hs, :, :].rearrange("p j (h q) -> p j h q", h=C)[:, :, :, hs]
                    dst = T1[hs, :, tok(v)].rearrange("p h (j q) -> p j h q", j=PB)
                    ins = nc.vector.tensor_copy(dst, src)
                    if hl == HG - 1:
                        ins.then_inc(dve_drained, 1)
                    else:
                        step(ins)

            for t in range(T):
                dve.wait_ge(act_drained, J.drain["s3", t][1])
                softmax("s3", t, B4[:, t % 2, 0:D], B4[:, 2 + t % 2, 0:D])
                if t >= 1:
                    o_drain(t - 1)
            o_drain(T - 1)
            for t in range(T):
                residual(("x3", t), H, None)
                dve.wait_ge(dve_drained, J.drain["x3", t][1])
                stats(H, t)
                step(nc.vector.tensor_tensor(X[:, t, :], X[:, t, :], H[:, t, :], ALU.add))
            normalise("n6", "t6", H, 1e-5)
            for t in range(T):
                drain_scaled(("t6", t), T1, v_("g2"), v_("b2"))

            def route(name, cols, renorm):
                L = tiny[:, 0, :].rearrange("p (t e) -> p t e", e=E)
                X6 = tiny[:, 6, :].rearrange("p (t e) -> p t e", e=E)
                sel = tiny[:, 5, :].rearrange("p (t e) -> p t e", e=E)
                dve.wait_ge(ready, J.ready[name,])
                src = banks((name,))[:, 0:T * cols].rearrange("p (t e) -> p t e", e=cols)
                if cols > E:
                    step(nc.vector.tensor_copy(tiny[:, 12, 0:T], src[:, :, E]))
                nc.vector.tensor_copy(L, src[:, :, 0:E]).then_inc(dve_drained, 1)
                dve.wait_ge(dve_drained, J.drain[name,][1])
                fence()
                link(nc.vector.reduce_max(tiny[:, 1, 0:T], L, AX_X))
                nc.vector.tensor_tensor(X6, L, bc(tiny[:, 1, 0:T].unsqueeze(2), P, T, E), ALU.subtract).then_inc(bias_ready, 1)
                other = bc(L.unsqueeze(2), P, T, E, E)
                own = bc(L.unsqueeze(3), P, T, E, E)
                gt = rank_in[:, 0, :, :].rearrange("p t (e f) -> p t e f", f=E)
                eq = rank_in[:, 1, :, :].rearrange("p t (e f) -> p t e f", f=E)
                step(nc.vector.tensor_tensor(gt, other, own, ALU.is_gt))
                link(nc.vector.tensor_tensor(eq, other, own, ALU.is_equal))
                link(nc.vector.tensor_tensor(rank_in[:, 1, :, :], rank_in[:, 1, :, :], bc(con_("before").unsqueeze(1), P, T, E * E), ALU.mult))
                link(nc.vector.tensor_tensor(rank_in[:, 0, :, :], rank_in[:, 0, :, :], rank_in[:, 1, :, :], ALU.add))
                link(nc.vector.reduce_sum(sel, gt, AX_X))
                link(nc.vector.tensor_scalar(sel, sel, 1.5, None, ALU.is_lt))
                dve.wait_ge(exp_ready, exps[name])
                if not renorm:
                    link(nc.vector.reduce_sum(tiny[:, 1, 8:16], X6, AX_X))
                link(nc.vector.tensor_tensor(X6, X6, sel, ALU.mult))
                if renorm:
                    link(nc.vector.reduce_sum(tiny[:, 1, 8:16], X6, AX_X))
                link(nc.vector.reciprocal(tiny[:, 1, 16:24], tiny[:, 1, 8:16]))
                link(nc.vector.tensor_tensor(cw[:, :, 0:E], X6, bc(tiny[:, 1, 16:24].unsqueeze(2), P, T, E), ALU.mult))

            route("g3", E, True)

            def weighted(key, t, e):
                dve.wait_ge(ready, J.ready[key])
                nc.vector.scalar_tensor_tensor(X[:, t, :], banks(key), cw[:, t, e:e + 1], X[:, t, :],
                                               ALU.mult, ALU.add).then_inc(dve_drained, 1)

            for b in range(4):
                for t in range(T):
                    for e in range(2):
                        if e == 1:
                            dve.wait_ge(dve_drained, J.drain["o2", b, t, 0][1])
                        weighted(("o2", b, t, e), t, 2 * b + e)
                    if b == 3 and stop > 3:
                        dve.wait_ge(dve_drained, J.drain["o2", b, t, 1][1])
                        stats(X, t)
            if stop == 3:
                return

            normalise("n5", "t5", X, 1e-5)

            def o4_drain(v):
                dve.wait_ge(ready, J.ready["o4", v])
                bk = banks(("o4", v)).rearrange("p (h q) -> p h q", h=C)
                for hl in range(HG):
                    hs = slice(hl * DK, (hl + 1) * DK)
                    ins = nc.vector.tensor_copy(T1[hs, :, v * SEQ:(v + 1) * SEQ], bk[hs, :, hs])
                    if hl == HG - 1:
                        ins.then_inc(dve_drained, 1)
                    else:
                        step(ins)

            for b in range(BATCH):
                S = S4[b % 2]
                dve.wait_ge(ready, J.ready["v4", b])
                nc.vector.tensor_copy(Vb[b % 2], banks(("v4", b), 2)).then_inc(dve_drained, 1)
                dve.wait_ge(ready, J.ready["s4", b])
                nc.vector.tensor_tensor(S, banks(("s4", b), 4)[:, :, 0:KEYS], bc(mk[:, :].unsqueeze(1), P, C, KEYS), ALU.mult).then_inc(dve_drained, 1)
                dve.wait_ge(dve_drained, J.drain["s4", b][1])
                link(nc.vector.tensor_tensor(S, S, bc(nm[:, :].unsqueeze(1), P, C, KEYS), ALU.add))
                link(nc.vector.reduce_max(tiny[:, 1, 0:C], S, AX_X))
                nc.vector.tensor_scalar(tiny[:, 7 + b % 2, 0:C], tiny[:, 1, 0:C], -1.0, None, ALU.mult).then_inc(bias_ready, 1)
                if b >= 1:
                    o4_drain(b - 1)
                dve.wait_ge(exp_ready, exps["s4", b])
                link(nc.vector.reciprocal(tiny[:, 1, 8:8 + C], tiny[:, 9 + b % 2, 0:C]))
                nc.vector.tensor_tensor(S, S, bc(tiny[:, 1, 8:8 + C].unsqueeze(2), P, C, KEYS), ALU.mult).then_inc(prob_ready, 1)
            o4_drain(BATCH - 1)
            for t in range(T):
                residual(("x4", t), X, r_("wo_b"))
                if stop > 4:
                    dve.wait_ge(dve_drained, J.drain["x4", t][1])
                    stats(X, t)
            if stop == 4:
                return

            normalise("n7", "t7", X, 1e-5)
            for t in range(T):
                dve.wait_ge(ready, J.ready["v5", t])
                nc.vector.tensor_tensor(B5t[:, t, :], banks(("v5", t)), r_("bv5"), ALU.add).then_inc(dve_drained, 1)
            for t in range(T):
                dve.wait_ge(ready, J.ready["s5", t])
                bk = banks(("s5", t), 4)
                for j in range(PB):
                    js = slice(j * SEQ, (j + 1) * SEQ)
                    for hl in range(HG):
                        src = bk[js, hl, :].rearrange("p (h k) -> p h k", h=C)[:, :, js]
                        dst = B3[js, t % 2, 0:D].rearrange("p (h l k) -> p l h k", l=HG, k=SEQ)[:, hl]
                        ins = nc.vector.scalar_tensor_tensor(dst, src, float(DK) ** -0.5, bc(con_("causal")[js].unsqueeze(1), SEQ, C, SEQ),
                                                             ALU.mult, ALU.add)
                        if j == PB - 1 and hl == HG - 1:
                            ins.then_inc(dve_drained, 1)
                        else:
                            step(ins)
                dve.wait_ge(dve_drained, J.drain["s5", t][1])
                fence()
                softmax("s5", t, B3[:, t % 2, 0:D], B3[:, 2 + t % 2, 0:D])
            for t in range(T):
                residual(("x5", t), X, r_("bo5"))
                if stop > 5:
                    dve.wait_ge(dve_drained, J.drain["x5", t][1])
                    stats(X, t)
            if stop == 5:
                return

            normalise("n8", "t8", X, 1e-5)
            route("r6", E + 1, False)
            dve.wait_ge(exp_ready, exps["sig"])
            link(nc.vector.tensor_scalar(tiny[:, 12, 0:T], tiny[:, 12, 0:T], 1.0, None, ALU.add))
            link(nc.vector.reciprocal(cw[:, :, E], tiny[:, 12, 0:T]))
            for b in range(E):
                for t in range(T):
                    if b:
                        dve.wait_ge(dve_drained, J.drain["o6", b - 1, t][1])
                    weighted(("o6", b, t), t, b)
            for g in range(G):
                for m in range(C):
                    dve.wait_ge(act_drained, J.drain["sg", g, m][1])
                    dve.wait_ge(ready, J.ready["su", g, m])
                    nc.vector.tensor_tensor(B1[:, m, grp(g)], banks(("su", g, m)), B2[:, m, grp(g)], ALU.mult).then_inc(dve_drained, 1)
            for t in range(T):
                weighted(("os", t), t, E)


def kernel(**inp):
    import concourse.bacc as _bacc
    from concourse.bass_utils import run_bass_kernel_spmd as _run

    A = {k: np.asarray(v) for k, v in inp.items()}

    def unit(w):
        return w.reshape(C, P, D).transpose(1, 0, 2)

    mats = [A["L0_xattn_Wq"].T, A["L0_xattn_Wk"], A["L0_xattn_Wv"].T, A["L0_attn_proj_w"].T]
    for b in range(4):
        mats += [A["L0_attn_mlp_w1"][:, b * D:(b + 1) * D], A["L0_attn_mlp_w2"][b * D:(b + 1) * D]]
    mats += [A["L0_ffn_Wq"], A["L0_ffn_Wk"], A["L0_ffn_Wv"], A["L0_ffn_Wo"]]
    for b in range(4):
        mats += [np.concatenate([A["L0_ffn_W1"][2 * b], A["L0_ffn_W1"][2 * b + 1]], 1),
                 np.concatenate([A["L0_ffn_W2"][2 * b], A["L0_ffn_W2"][2 * b + 1]], 0)]
    mats += [A["L1_xattn_wq"].T, A["L1_xattn_wk"].T, A["L1_xattn_wv"].T, A["L1_xattn_wo_w"].T]
    mats += [A["L1_attn_Wq"].T, A["L1_attn_Wk"].T, A["L1_attn_Wv"].T, A["L1_attn_Wo"].T]
    for e in range(E):
        mats += [A["L1_ffn_w1"][e], A["L1_ffn_w2"][e]]
    mats += [A["L1_ffn_shared_gate_up"][:, :D], A["L1_ffn_shared_gate_up"][:, D:], A["L1_ffn_shared_down"]]
    units = np.ascontiguousarray(np.stack([unit(m) for m in mats]))

    mb1 = A["L0_attn_mlp_b1"].reshape(4, D)
    vs = [A["L0_xattn_bq"], A["L0_attn_norm1_w"], A["L0_attn_norm2_w"], *mb1, A["L0_ffn_g1"], A["L0_ffn_b1"], A["L0_ffn_g2"],
          A["L0_ffn_b2"], A["L1_attn_bq"], A["L1_attn_bk"], A["L0_xattn_bk"]]
    vecs = np.ascontiguousarray(np.stack(vs).reshape(len(VEC), C, P).transpose(2, 0, 1))
    rows = np.stack([A["L0_xattn_bv"], A["L0_attn_proj_b"], A["L0_attn_mlp_b2"], A["L1_xattn_wo_b"], A["L1_attn_bv"], A["L1_attn_bo"]])
    scalars = np.concatenate([A["L0_attn_decay_logit"], A["L0_attn_alpha_logit"], A["L0_attn_k_base_gate_logit"].reshape(1),
                              A["L0_attn_k_base_kernel"], A["L1_attn_lambda_attn"].reshape(1)])
    sm = np.concatenate([A["L0_attn_u"], A["L0_attn_v"], A["L0_ffn_Wg"], A["L1_ffn_router_w"], A["L1_ffn_shared_gate_w"]], 1)
    small = np.ascontiguousarray(sm.reshape(C, P, NSML).transpose(1, 0, 2))
    jbd = np.zeros((P, C, P), np.float32)
    for h in range(HEADS):
        a = (h % HG) * DK
        jbd[a:a + DK, h // HG, a:a + DK] = A["L1_attn_J_attn"][h]
    ctx = A["ctx_1024"]
    arrays = {
        "x_dram": np.ascontiguousarray(A["x"].reshape(T, P, D)),
        "ctx_dram": np.ascontiguousarray(ctx),
        "ctx_t_dram": np.ascontiguousarray(ctx.transpose(0, 2, 1).reshape(BATCH, C, P, KEYS).transpose(0, 2, 1, 3)),
        "ctx_last_dram": np.ascontiguousarray(ctx[:, KEYS - 1, :].reshape(BATCH, C, P).transpose(2, 1, 0)),
        "mask_dram": np.ascontiguousarray(A["mask_1x1xSxS2_bk0"].reshape(SEQ, KEYS)),
        "units_dram": units, "vecs_dram": vecs, "rows_dram": rows, "scalars_dram": scalars, "small_dram": small,
        "jbd_dram": jbd, "con_dram": constants(),
    }
    nc = _bacc.Bacc("TRN2", target_bir_lowering=False, num_devices=1)
    args = [nc.dram_tensor(k, v.shape, mybir.dt.from_np(v.dtype), kind="ExternalInput").ap() for k, v in arrays.items()]
    args.append(nc.dram_tensor("out_dram", (T, P, D), F32, kind="ExternalOutput").ap())
    build(nc, *args)
    r = _run(nc, [arrays], core_ids=[0])
    return r.results[0]["out_dram"].reshape(BATCH, SEQ, D)
```

```python
from contextlib import ExitStack

import numpy as np

import concourse.bass as bass
from concourse import mybir

ALU = mybir.AluOpType
ACT = mybir.ActivationFunctionType
AX_X = mybir.AxisListType.X
F32 = mybir.dt.float32
F32R = mybir.dt.float32r
U8 = mybir.dt.uint8

P = 128
D = 512
C = D // P
BATCH, SEQ = 32, 32
TOK = BATCH * SEQ
T = TOK // P
PB = P // SEQ
G = TOK // 512
TG = T // G
KEYS = 257
KT = 2
HEADS, DK = 16, 32
HG = 4
R = 16
E = 8
NW = 2
NC4 = 2
NVR = 2
NR = 2
NTMP = 4

VEC = ["bq0", "norm1", "norm2", "mb10", "mb11", "mb12", "mb13", "g1", "b1", "g2", "b2", "bq5", "bk5", "bk0"]
ROW = ["bv0", "proj_b", "mb2", "wo_b", "bv5", "bo5"]
SCL = {"decay": (0, R), "alpha": (R, R), "gate": (2 * R, 1), "kern": (2 * R + 1, 4), "lam": (2 * R + 5, 1)}
NSCL = 2 * R + 6
SML = {"uv": (0, 2 * R), "wg": (2 * R, E), "router": (2 * R + E, E + 1)}
NSML = 2 * R + E + E + 1
CON = {"ident": (0, P), "lower": (P, P), "shift": (2 * P, 4 * P), "causal": (6 * P, P), "before": (7 * P, E * E),
       "row_of": (7 * P + E * E, PB), "pos": (7 * P + E * E + PB, 1)}
NCON = 7 * P + E * E + PB + 1


def constants():
    con = np.zeros((P, NCON), np.float32)
    j, i = np.meshgrid(np.arange(P), np.arange(P), indexing="ij")
    same = (j // SEQ) == (i // SEQ)
    con[:, 0:P] = np.eye(P)
    con[:, P:2 * P] = same & (i >= j)
    for m in range(4):
        con[:, (2 + m) * P:(3 + m) * P] = same & (i - j == m)
    q, k = np.meshgrid(np.arange(P) % SEQ, np.arange(P) % SEQ, indexing="ij")
    con[:, 6 * P:7 * P] = np.where(k > q, -1e30, 0.0)
    e, f = np.meshgrid(np.arange(E), np.arange(E), indexing="ij")
    con[:, 7 * P:7 * P + E * E] = (f < e).astype(np.float32).reshape(1, -1)
    con[:, -1 - PB:-1] = (np.arange(P)[:, None] // SEQ) == np.arange(PB)
    con[:, -1] = np.arange(P) % SEQ
    return con


UNITS = (["0.wq", "0.wk", "0.wv", "1.proj"] + [f"1.w{i}.{b}" for b in range(4) for i in (1, 2)]
         + ["2.q", "2.k", "2.v", "2.o"] + [f"2.w{i}.{b}" for b in range(4) for i in (1, 2)]
         + ["3.q", "3.k", "3.v", "3.o", "4.q", "4.k", "4.v", "4.o"]
         + [f"5.w{i}.{b}" for b in range(E) for i in (1, 2)] + ["5.gate", "5.up", "5.down"])
UNIT = {name: i for i, name in enumerate(UNITS)}


class Jobs:

    def __init__(self):
        self.ready, self.bank, self.drain, self.frees, self.last, self.hi = {}, {}, {}, {}, {}, {}
        self.at, self.count, self.owner = 0, {"act": 0, "dve": 0}, [None] * 8

    def add(self, key, drain, banks=1, unit=None, split=False):
        self.at += -self.at % banks
        b = self.at % 8
        before = [self.owner[x] for x in range(b, b + banks) if self.owner[x] is not None]
        need = {}
        for k in before:
            eng, n = self.drain[k]
            need[eng] = max(need.get(eng, 0), n)
        self.frees[key] = need
        for x in range(b, b + banks):
            self.owner[x] = key
        self.at = (b + banks) % 8
        self.bank[key] = b
        self.ready[key] = len(self.ready) + 1
        self.count[drain] += 1
        self.drain[key] = (drain, self.count[drain])
        if split:
            assert drain == "dve"
            self.hi[key] = len(self.hi) + 1
        if unit is not None:
            self.last[unit] = self.ready[key]


def plan(stop):
    J = Jobs()
    for g in range(G):
        for t in range(g * TG, g * TG + TG):
            J.add(("t1", t), "dve", split=True)
        for m in range(C):
            J.add(("q", g, m), "dve", unit="0.wq", split=True)
    J.add(("c",), "dve")
    for g in range(G):
        for m in range(C):
            J.add(("qk", g, m), "act", unit="0.wk")
    for t in range(T + 1):
        if t < T:
            J.add(("s", t), "act")
        if t >= 1:
            J.add(("pt", t - 1), "act")
            J.add(("u", t - 1), "act")
        if t >= 2:
            J.add(("ut", t - 2), "dve", split=True)
    J.add(("ut", T - 1), "dve", split=True)
    for t in range(T):
        J.add(("y", t), "dve", unit="0.wv")
    if stop == 1:
        return J
    for name, eng in (("t2", "dve"), ("uv", "dve"), ("kq", "act"), ("A", "dve"), ("d", "dve"), ("pr", "dve"), ("t3", "dve")):
        for t in range(T):
            J.add((name, t), eng, unit="1.proj" if name == "pr" else None, split=name in ("d", "t3"))
    for b in range(4):
        for g in range(G):
            for m in range(C):
                J.add(("h1", b, g, m), "dve", unit=f"1.w1.{b}", split=True)
        for t in range(T):
            J.add(("o1", b, t), "dve", unit=f"1.w2.{b}")
    if stop == 2:
        return J
    for t in range(T):
        J.add(("t4", t), "dve", split=True)
    for g in range(G):
        for m in range(C):
            J.add(("q3", g, m), "act", unit="2.q")
    for g in range(G):
        for m in range(C):
            J.add(("k3", g, m), "act", unit="2.k")
    for t in range(T):
        J.add(("v3", t), "act", unit="2.v")
    for t in range(T + 1):
        if t < T:
            J.add(("s3", t), "act", banks=4)
        if t >= 1:
            J.add(("o3", t - 1), "dve", banks=4, split=True)
    for t in range(T):
        J.add(("x3", t), "dve", unit="2.o")
    for t in range(T):
        J.add(("t6", t), "dve", split=True)
    J.add(("g3",), "dve")
    for b in range(4):
        for g in range(G):
            for m in range(C):
                J.add(("h2", b, g, m), "dve", unit=f"2.w1.{b}", split=True)
        for t in range(T):
            for e in range(2):
                J.add(("o2", b, t, e), "dve", unit=f"2.w2.{b}")
    if stop == 3:
        return J
    for t in range(T):
        J.add(("t5", t), "dve", split=True)
    for g in range(G):
        for m in range(C):
            J.add(("q4", g, m), "act", unit="3.q")
    J.add(("kl",), "act", unit="3.k")
    J.add(("vlt",), "act")
    J.add(("vl",), "act")
    for b in range(BATCH + 1):
        if b < BATCH:
            J.add(("k4", b), "act", banks=4, unit="3.k")
            J.add(("v4", b), "dve", banks=2, unit="3.v")
            J.add(("s4", b), "dve", banks=4)
        if b >= 1:
            J.add(("p4", b - 1), "act", banks=2)
            J.add(("l4", b - 1), "act")
            J.add(("o4", b - 1), "dve", split=True)
    for t in range(T):
        J.add(("x4", t), "dve", unit="3.o")
    if stop == 4:
        return J
    for t in range(T):
        J.add(("t7", t), "dve", split=True)
    for g in range(G):
        for m in range(C):
            J.add(("q5", g, m), "act", unit="4.q")
    for g in range(G):
        for m in range(C):
            J.add(("k5", g, m), "act", unit="4.k")
    for g in range(G):
        for m in range(C):
            J.add(("qj", g, m), "act")
    for t in range(T):
        J.add(("v5", t), "dve", unit="4.v")
    for t in range(T + 1):
        if t < T:
            J.add(("s5", t), "dve", banks=4)
        if t >= 1:
            J.add(("o5", t - 1), "dve", banks=4, split=True)
    for t in range(T):
        J.add(("x5", t), "dve", unit="4.o")
    if stop == 5:
        return J
    for t in range(T):
        J.add(("t8", t), "dve", split=True)
    J.add(("r6",), "dve")
    for b in range(E):
        for g in range(G):
            for m in range(C):
                J.add(("h3", b, g, m), "dve", unit=f"5.w1.{b}", split=True)
        for t in range(T):
            J.add(("o6", b, t), "dve", unit=f"5.w2.{b}")
    for g in range(G):
        for m in range(C):
            J.add(("sg", g, m), "act", unit="5.gate")
            J.add(("su", g, m), "dve", unit="5.up", split=True)
    for t in range(T):
        J.add(("os", t), "dve", unit="5.down")
    return J


def build(nc, x, ctx, ctx_t, ctx_last, mask, units, vecs, rows, scalars, small, jbd, con, out, stop=6):
    J = plan(stop)
    n_units = {1: 3, 2: 12, 3: 24, 4: 28, 5: 32, 6: 51}[stop]

    with ExitStack() as stack:
        def sb(name, shape, dt=F32):
            return stack.enter_context(nc.sbuf_tensor(name, shape, dt))

        def sem(name):
            return stack.enter_context(nc.semaphore(name))

        X = sb("X", [P, T, D])
        H = sb("H", [P, T, D])
        h_at = nc.sbuf_base - 4 * T * D
        pool_area = sb("pool_area", [P, 4 * 4096])
        area_at = nc.sbuf_base - 4 * 4 * 4096
        T1h = sb("T1h", [P, C, TOK], F32R)
        T1l = sb("T1l", [P, C, TOK], F32R)
        Wh = sb("Wh", [P, NW, C, D], F32R)
        Wl = sb("Wl", [P, NW, C, D], F32R)
        B1h = nc.alloc_sbuf_tensor_at("B1h", [P, C, TOK], F32R, offset=area_at)
        B1l = nc.alloc_sbuf_tensor_at("B1l", [P, C, TOK], F32R, offset=area_at + 4 * C * TOK)
        CTh = nc.alloc_sbuf_tensor_at("CTh", [P, NC4, C, KT * P], F32R, offset=h_at)
        CTl = nc.alloc_sbuf_tensor_at("CTl", [P, NC4, C, KT * P], F32R, offset=h_at + 4 * NC4 * C * KT * P)
        T1, B1 = (T1h, T1l), (B1h, B1l)
        W = sb("W", [P, NW, C, D])
        SCP = sb("SCP", [P, NTMP, D])
        XN = sb("XN", [P, 2, D])
        vec = sb("vec", [P, len(VEC), C])
        row = sb("row", [P, NR, D])
        scl = sb("scl", [P, NSCL])
        sml = sb("sml", [P, C, NSML])
        cst = sb("cst", [P, NCON])
        jb = sb("jb", [P, C, P])
        mk8 = sb("mk8", [P, KEYS], U8)
        mk = sb("mk", [P, KEYS])
        nm = sb("nm", [P, KEYS])
        half = sb("half", [P, R])
        bns = sb("bns", [P, 6])
        mv = sb("mv", [P, T, 2])
        ve = sb("ve", [P, 4, T])
        rs = sb("rs", [P, 4, T])
        tiny = sb("tiny", [P, 16, 64])
        cw = sb("cw", [P, T, E + 1])
        dec = sb("dec", [P, 8, R])
        clh = sb("clh", [P, C, BATCH], F32R)
        cll = sb("cll", [P, C, BATCH], F32R)
        PL = sb("PL", [P, 2, PB])
        PS = stack.enter_context(nc.psum_tensor("PS", [P, 8, 512], F32))

        def area(first, *shape):
            n = int(np.prod(shape))
            v = pool_area[:, first:first + n]
            names = " ".join("abcd"[:len(shape)])
            return v if len(shape) == 1 else v.rearrange(f"p ({names}) -> p {names}", **{k: s for k, s in zip("abcd", shape)})

        A0, A1, A2, A3 = (area(4096 * i, C, TOK) for i in range(4))
        A2t, A3t = (area(4096 * i, T, D) for i in (2, 3))
        Hf = H[:, :, :].rearrange("p a b -> p (a b)")
        QJ = Hf.rearrange("p (c t) -> p c t", c=C)
        rank_in = area(3 * 4096, 2, T, E * E)
        ident = cst[:, 0:P]
        convm = cst[:, CON["shift"][0]:CON["shift"][0] + P]

        def con_(name):
            a, n = CON[name]
            return cst[:, a:a + n]

        def v_(name):
            return vec[:, VEC.index(name), :]

        def r_(name):
            return row[:, ROW.index(name) % NR, :]

        def s_(name):
            a, n = SCL[name]
            return scl[:, a:a + n]

        def bc(ap, *shape):
            return ap.to_broadcast(shape)

        ready = sem("ready")
        act_drained = sem("act_drained")
        dve_drained = sem("dve_drained")
        drained = {"act": act_drained, "dve": dve_drained}
        w_full = [sem(f"w_full{i}") for i in range(NW)]
        w_high = sem("w_high")
        w_split = sem("w_split")
        tmp_ready = sem("tmp_ready")
        high = sem("high")
        row_in = [sem(f"row_in{i}") for i in range(NR)]
        s_batch = sem("s_batch")
        u_batch = sem("u_batch")
        ct_high = sem("ct_high")
        ct_split = sem("ct_split")
        const_in = sem("const_in")
        x_in = sem("x_in")
        ctx_t_in = [sem(f"ctx_t_in{i}") for i in range(8)]
        ctx_in = [sem(f"ctx_in{i}") for i in range(8)]
        ctx4_in = [sem(f"ctx4_in{i}") for i in range(NC4)]
        last_in = sem("last_in")
        cl_in = [sem(f"cl_in{i}") for i in range(2)]
        ownlast = sem("ownlast")
        vrow_in = [sem(f"vrow_in{i}") for i in range(NVR)]
        stored = sem("stored")
        dve_step = sem("dve_step")
        act_step = sem("act_step")
        pool_step = sem("pool_step")
        base_ready = sem("base_ready")
        power_ready = sem("power_ready")
        xn_ready = sem("xn_ready")
        bias_ready = sem("bias_ready")
        exp_ready = sem("exp_ready")
        prob_ready = sem("prob_ready")
        qk_scaled = sem("qk_scaled")
        qbd_ready = sem("qbd_ready")
        zero_ready = sem("zero_ready")
        setup_ready = sem("setup_ready")
        gated = sem("gated")

        norms = ["n1", "n2", "n3", "n4", "n6", "n5", "n7", "n8"]
        XNB = {}
        seq = {1: ["t1"], 2: ["t1", "t3"], 3: ["t1", "t3", "t4", "t6"], 4: ["t1", "t3", "t4", "t6", "t5"],
               5: ["t1", "t3", "t4", "t6", "t5", "t7"], 6: ["t1", "t3", "t4", "t6", "t5", "t7", "t8"]}[stop]
        for i, name in enumerate(seq):
            XNB[name] = i * T
        powers = {}
        for name in ["dec", "n1", "n2", "n2r", "uv", "n3", "n4", "n4r", "n6", "n5", "n7", "n8"]:
            powers[name] = len(powers) + 1
        soft = {}
        for t in range(T):
            soft["s", t] = len(soft) + 1
        for t in range(T):
            soft["s3", t] = len(soft) + 1
        soft["g3"] = len(soft) + 1
        for b in range(BATCH):
            soft["s4", b] = len(soft) + 1
        for t in range(T):
            soft["s5", t] = len(soft) + 1
        soft["r6"] = len(soft) + 1
        prob = {}
        for key in soft:
            if key not in ("g3", "r6"):
                prob[key] = len(prob) + 1

        tmps = {}
        for key in J.hi:
            if key[0] in ("d", "t3", "t4", "t6", "su"):
                tmps[key] = len(tmps) + 1
        ring = [key for key in J.hi if key[0] in ("h1", "h3")]

        def banks(key, n=1):
            b = J.bank[key]
            return PS[:, b, :] if n == 1 else PS[:, b:b + n, :]

        QK = A2
        KP = KEYS + 1
        ct_at = lambda base, at: base[:, at:at + C * KP].rearrange("p (c k) -> p c k", c=C)
        ck_at = lambda base, at: base[:, at:at + KT * D].rearrange("p (k d) -> p k d", k=KT)
        hi_area = 3 * 4096
        P1 = area(hi_area, 2, KEYS)
        PT1 = area(hi_area + 2 * KEYS, 2, 3 * P)
        free = hi_area + 2 * KEYS + 6 * P
        CT = [ct_at(Hf, i * C * KP) for i in range(3)] + [ct_at(pool_area, free)]
        CK = [ck_at(pool_area, free + C * KP)]
        CL = [Hf[0:PB, 3 * C * KP:3 * C * KP + D], pool_area[0:PB, free + C * KP + KT * D:free + C * KP + KT * D + D]]
        assert free + C * KP + (KT + 1) * D <= 4 * 4096
        CT += [ct_at(pool_area, i * C * KP) for i in range(3)]
        CK += [ck_at(pool_area, 3 * C * KP + i * KT * D) for i in range(4)]
        assert 3 * C * KP + 4 * KT * D <= 2 * 4096
        NCT, NCK = len(CT), len(CK)
        CT_EARLY, CK_EARLY = 4, 1
        cs = tiny[:, 0, 0:T]

        o = 4096
        take = []
        for shape in ([(C, KEYS)] * 2 + [(KT, D)] * 2 + [(C, KT * P)] * NC4 + [(C, KEYS)] * 2 + [(KT, D)] * 2 + [(C, P)] * 2):
            take.append(area(o, *shape))
            o += int(np.prod(shape))
        assert o <= 4 * 4096, o
        KTb, Vb, CT4, S4, PT4, Qbd = take[0:2], take[2:4], take[4:6], take[6:8], take[8:10], take[10:12]
        sc = SCP[:, :, :].rearrange("p a b -> p (a b)")
        ctxl = sc[:, 0:C * BATCH].rearrange("p (c b) -> p c b", c=C)
        KL = sc[:, P:P + C * BATCH].rearrange("p (c b) -> p c b", c=C)
        VLT = sc[:, 2 * P:2 * P + C * BATCH].rearrange("p (c b) -> p c b", c=C)
        VL = sc[:, 512:1024]
        pl4 = sc[:, 1024:2048].rearrange("p (n d) -> p n d", n=2)
        vrow = XN

        qk2 = area(4096, T, 2 * R)
        sq = area(4096 + 512, T, 2 * R)
        ksq = area(4096 + 1024, T, 2 * P)
        AT = area(2 * 4096, T, P)
        HH = A3t

        def tok(t):
            return slice(t * P, (t + 1) * P)

        def grp(g):
            return slice(g * 512, (g + 1) * 512)

        block = stack.enter_context(nc.Block())

        @block.sync
        def _(sp):
            def load_unit(u):
                if u >= NW:
                    sp.wait_ge(w_split, u - NW + 1)
                sp.dma_start(W[:, u % NW, :, :], units[u]).then_inc(w_full[u % NW], 16)

            def load_row(i, key=None):
                if key is not None:
                    sp.wait_ge(dve_drained, J.drain[key][1])
                sp.dma_start(row[:, i % NR, :], rows[i:i + 1, :].to_broadcast([P, D])).then_inc(row_in[i % NR], 16)

            sp.dma_start(cst[:, :], con).then_inc(const_in, 16)
            for t in range(T):
                sp.dma_start(X[:, t, :], x[t]).then_inc(x_in, 16)
            sp.dma_start(vec[:, :, :], vecs).then_inc(const_in, 16)
            load_unit(0)
            load_unit(1)
            sp.dma_start(scl[:, :], scalars.rearrange("(o r) -> o r", o=1).to_broadcast([P, NSCL])).then_inc(const_in, 16)
            sp.dma_start(sml[:, :, :], small).then_inc(const_in, 16)
            sp.dma_start(jb[:, :, :], jbd).then_inc(const_in, 16)
            for j in range(PB):
                sp.dma_start(mk8[j * SEQ:(j + 1) * SEQ, :], mask).then_inc(const_in, 16)
            load_row(0)
            load_row(1)

            def load_ct(i):
                if i == CT_EARLY:
                    sp.wait_ge(ready, J.ready["qk", G - 1, C - 1])
                if i >= NCT:
                    b = i - NCT
                    if b % PB == PB - 1:
                        sp.wait_ge(ready, J.ready["s", b // PB])
                    else:
                        sp.wait_ge(s_batch, (PB - 1) * (b // PB) + b % PB + 1)
                sp.dma_start(CT[i % NCT], ctx_t[i]).then_inc(ctx_t_in[i % NCT], 16)

            def load_ck(i):
                if i >= NCK:
                    b = i - NCK
                    if b % PB == PB - 1:
                        sp.wait_ge(ready, J.ready["u", b // PB])
                    else:
                        sp.wait_ge(u_batch, (PB - 1) * (b // PB) + b % PB + 1)
                sp.dma_start(CK[i % NCK][:, 0:KT, :], ctx[i, 0:KT * P, :].rearrange("(k p) d -> p k d", p=P)).then_inc(ctx_in[i % NCK], 16)

            def load_cl(t):
                if t >= 2:
                    sp.wait_ge(ready, J.ready["u", t - 2])
                sp.dma_start(CL[t % 2], ctx[t * PB:(t + 1) * PB, KT * P, :]).then_inc(cl_in[t % 2], 16)

            for i in range(CT_EARLY):
                load_ct(i)
            load_unit(2)
            load_ck(0)
            for i in range(CT_EARLY, BATCH + CT_EARLY + 3):
                if i < BATCH:
                    load_ct(i)
                if i == CT_EARLY + 1 and n_units > 3:
                    load_unit(3)
                b = i - CT_EARLY - 2
                if 0 <= b < BATCH and b % PB == 0:
                    load_cl(b // PB)
                if 1 <= b < BATCH:
                    load_ck(b)
            if stop >= 2:
                load_row(2, ("y", T - 1))
            for u in range(4, min(28, n_units)):
                load_unit(u)
                if u == 8:
                    load_row(3, ("pr", T - 1))
                if stop >= 4 and u == 14:
                    load_row(4, ("o1", 3, T - 1))
            if stop >= 4:
                sp.wait_ge(dve_drained, J.drain["t6", T - 1][1])
                sp.wait_ge(ready, J.ready["h2", 3, G - 1, C - 1])
                sp.dma_start(ctxl, ctx_last).then_inc(last_in, 16)
                sp.wait_ge(ready, J.ready["o2", 3, T - 1, 1])
                for b in range(BATCH):
                    if b >= NC4:
                        sp.wait_ge(ct_split, b - NC4 + 2)
                    sp.dma_start(CT4[b % NC4], ctx_t[b, :, :, 0:KT * P]).then_inc(ctx4_in[b % NC4], 16)
                    if b == 1:
                        sp.wait_ge(act_drained, J.drain["vl",][1])
                        sp.wait_ge(ready, J.ready["t5", T - 1])
                    if b >= 1:
                        v = b - 1
                        if v >= NVR:
                            sp.wait_ge(ready, J.ready["o4", v - NVR])
                        sp.dma_start(vrow[0:1, v % NVR, :], VL[v:v + 1, :]).then_inc(vrow_in[v % NVR], 16)
                v = BATCH - 1
                sp.wait_ge(ready, J.ready["o4", v - NVR])
                sp.dma_start(vrow[0:1, v % NVR, :], VL[v:v + 1, :]).then_inc(vrow_in[v % NVR], 16)
                if stop > 4:
                    for u in range(28, n_units):
                        load_unit(u)
                        if u == 29:
                            load_row(5, ("x4", T - 1))
            last = {1: ("y",), 2: ("o1", 3), 3: ("o2", 3), 4: ("x4",), 5: ("x5",), 6: ("os",)}[stop]
            for t in range(T):
                key = last + (t,) + ((1,) if stop == 3 else ())
                sp.wait_ge(dve_drained, J.drain[key][1])
                sp.dma_start(out[t], X[:, t, :]).then_inc(stored, 16)
            sp.wait_ge(stored, 16 * T)

        @block.tensor
        def _(pe):
            def wait_banks(key):
                for eng, n in J.frees[key].items():
                    pe.wait_ge(drained[eng], n)

            def wait_unit(name):
                u = UNIT[name]
                pe.wait_ge(w_split, u + 1)
                return Wh[:, u % NW, :, :], Wl[:, u % NW, :, :]

            def split_product(out_, a, b, first, last):
                nc.tensor.matmul(out_, a[0], b[0], start=first, stop=False)
                nc.tensor.matmul(out_, a[0], b[1], start=False, stop=False)
                return nc.tensor.matmul(out_, a[1], b[0], start=False, stop=last)

            def cut(pair, *at):
                return pair[0][at], pair[1][at]

            def transposes(name, src, ready_at):
                for t in range(T):
                    transpose_tile(name, t, src, ready_at)

            def transpose_tile(name, t, src, ready_at):
                pe.wait_ge(xn_ready, ready_at + t + 1)
                wait_banks((name, t))
                o_ = banks((name, t))
                for c in range(C):
                    mm = nc.tensor.transpose(o_[:, c * P:(c + 1) * P], src(t)[:, c * P:(c + 1) * P], ident)
                mm.then_inc(ready, 1)

            def feature_major(name, w, src, g, waits=()):
                for s, n in waits:
                    pe.wait_ge(s, n)
                for m in range(C):
                    wait_banks(name + (g, m))
                    for c in range(C):
                        mm = split_product(banks(name + (g, m)), cut(w, slice(None), c, slice(m * P, (m + 1) * P)),
                                           cut(src, slice(None), c, grp(g)), c == 0, c == C - 1)
                    mm.then_inc(ready, 1)

            def token_major(key, w, src, t, chunks=range(C)):
                wait_banks(key)
                for c in chunks:
                    mm = split_product(banks(key), cut(src, slice(None), c, tok(t)), cut(w, slice(None), c, slice(None)),
                                       c == chunks[0], c == chunks[-1])
                mm.then_inc(ready, 1)

            def after(key):
                eng, n = J.drain[key]
                return drained[eng], n

            def wait(key):
                pe.wait_ge(*after(key))

            xn = lambda t: XN[:, t % 2, :]
            pe.wait_ge(const_in, 16 * 9)
            w = None
            for g in range(G):
                for t in range(g * TG, g * TG + TG):
                    transpose_tile("t1", t, xn, XNB["t1"])
                w = wait_unit("0.wq")
                wait(("t1", g * TG + TG - 1))
                feature_major(("q",), w, T1, g)
            wait(("q", G - 1, C - 1))
            wait_banks(("c",))
            for t in range(T):
                for i in range(2 * C):
                    c = i % C
                    mm = nc.tensor.matmul(banks(("c",))[:, t:t + 1], B1[i // C][:, c, tok(t)].bitcast(F32), v_("bk0")[:, c:c + 1],
                                          start=(i == 0), stop=(i == 2 * C - 1))
            mm.then_inc(ready, 1)
            w = wait_unit("0.wk")
            for g in range(G):
                feature_major(("qk",), w, B1, g)

            def values_up(v):
                wait(("u", v))
                wait_banks(("ut", v))
                for c in range(C):
                    mm = nc.tensor.transpose(banks(("ut", v))[:, c * P:(c + 1) * P], XN[:, v % 2, c * P:(c + 1) * P], ident)
                mm.then_inc(ready, 1)

            for t in range(T + 1):
                if t < T:
                    wait(("qk", t // TG, C - 1))
                    wait_banks(("s", t))
                    for j in range(PB):
                        b = t * PB + j
                        pe.wait_ge(ctx_t_in[b % NCT], 16 * (b // NCT + 1))
                        for c in range(C):
                            mm = nc.tensor.matmul(banks(("s", t))[j * SEQ:(j + 1) * SEQ, 0:KEYS],
                                                  QK[:, c, b * SEQ:(b + 1) * SEQ], CT[b % NCT][:, c, 0:KEYS],
                                                  start=(c == 0), stop=(c == C - 1))
                        mm.then_inc(s_batch if j < PB - 1 else ready, 1)
                if t >= 1:
                    v = t - 1
                    pe.wait_ge(prob_ready, prob["s", v])
                    wait_banks(("pt", v))
                    bk = banks(("pt", v))
                    for k in range(KT):
                        nc.tensor.transpose(bk[:, k * P:(k + 1) * P], P1[:, v % 2, k * P:(k + 1) * P], ident)
                    pe.wait_ge(ownlast, v + 1)
                    nc.tensor.transpose(bk[0:PB, KT * P:(KT + 1) * P], PL[:, v % 2, :], ident).then_inc(ready, 1)
                    wait(("pt", v))
                    wait_banks(("u", v))
                    bk = banks(("u", v))
                    for j in range(PB):
                        b = v * PB + j
                        pe.wait_ge(ctx_in[b % NCK], 16 * (b // NCK + 1))
                        for k in range(KT):
                            mm = nc.tensor.matmul(bk[j * SEQ:(j + 1) * SEQ, :], PT1[:, v % 2, k * P + j * SEQ:k * P + (j + 1) * SEQ],
                                                  CK[b % NCK][:, k, :], start=(k == 0), stop=(k == KT - 1), skip_group_check=True)
                        if j < PB - 1:
                            mm.then_inc(u_batch, 1)
                    pe.wait_ge(cl_in[v % 2], 16 * (v // 2 + 1))
                    nc.tensor.matmul(bk, PT1[0:PB, v % 2, KT * P:(KT + 1) * P], CL[v % 2], start=False, stop=True,
                                     skip_group_check=True).then_inc(ready, 1)
                if t >= 2:
                    values_up(t - 2)
            values_up(T - 1)
            w = wait_unit("0.wv")
            for t in range(T):
                wait(("ut", t))
                token_major(("y", t), w, T1, t)
            if stop == 1:
                return

            def small_(name):
                a, n = SML[name]
                return sml[:, :, a:a + n]

            for t in range(T):
                pe.wait_ge(qk_scaled, t + 1)
                wait_banks(("t2", t))
                for c in range(C):
                    mm = nc.tensor.transpose(banks(("t2", t))[:, c * P:(c + 1) * P], HH[:, t, c * P:(c + 1) * P], ident)
                mm.then_inc(ready, 1)
            for t in range(T):
                wait(("t2", t))
                wait_banks(("uv", t))
                for c in range(C):
                    mm = nc.tensor.matmul(banks(("uv", t))[:, 0:2 * R], A0[:, c, tok(t)], small_("uv")[:, c, :],
                                          start=(c == 0), stop=(c == C - 1))
                mm.then_inc(ready, 1)
            for t in range(T):
                pe.wait_ge(qk_scaled, T + 1)
                wait_banks(("kq", t))
                for i in range(2):
                    mm = nc.tensor.transpose(banks(("kq", t))[0:R, i * P:(i + 1) * P], qk2[:, t, i * R:(i + 1) * R], ident)
                mm.then_inc(ready, 1)
            for t in range(T):
                wait(("kq", t))
                wait_banks(("A", t))
                nc.tensor.matmul(banks(("A", t))[:, 0:P], ksq[0:R, t, P:2 * P], ksq[0:R, t, 0:P],
                                 start=True, stop=True).then_inc(ready, 1)
            for t in range(T):
                wait(("A", t))
                wait_banks(("d", t))
                for c in range(C):
                    mm = nc.tensor.matmul(banks(("d", t))[:, c * P:(c + 1) * P], HH[:, t, c * P:(c + 1) * P], AT[:, t, :],
                                          start=True, stop=True)
                mm.then_inc(ready, 1)
            w = wait_unit("1.proj")
            for t in range(T):
                wait(("d", t))
                token_major(("pr", t), w, B1, t)
            transposes("t3", xn, XNB["t3"])
            wait(("t3", T - 1))
            for b in range(4):
                w = wait_unit(f"1.w1.{b}")
                for g in range(G):
                    feature_major(("h1", b), w, T1, g)
                w = wait_unit(f"1.w2.{b}")
                for t in range(T):
                    wait(("h1", b, t // TG, C - 1))
                    token_major(("o1", b, t), w, B1, t)
            if stop == 2:
                return

            def self_scores(name, t, pairs):
                wait_banks((name, t))
                bk = banks((name, t), 4)
                for hb in range(C):
                    for hl in range(HG):
                        hs = slice(hl * DK, (hl + 1) * DK)
                        for j in range(PB):
                            js = slice(j * SEQ, (j + 1) * SEQ)
                            ts = slice(t * P + j * SEQ, t * P + (j + 1) * SEQ)
                            for i, (a, k) in enumerate(pairs):
                                mm = nc.tensor.matmul(bk[js, hl, hb * SEQ:(hb + 1) * SEQ], a[hs, hb, ts], k[hs, hb, ts],
                                                      start=(i == 0), stop=(i == len(pairs) - 1))
                mm.then_inc(ready, 1)

            def self_values(name, t, V, PTs):
                wait_banks((name, t))
                bk = banks((name, t), 4)
                for hb in range(C):
                    for j in range(PB):
                        js = slice(j * SEQ, (j + 1) * SEQ)
                        for hl in range(HG):
                            h, ps = hb * HG + hl, hl * C + hb
                            mm = nc.tensor.matmul(bk[hl * DK:(hl + 1) * DK, j, hb * SEQ:(hb + 1) * SEQ], V[js, t, h * DK:(h + 1) * DK],
                                                  PTs[js, ps * SEQ:(ps + 1) * SEQ], start=True, stop=True)
                mm.then_inc(ready, 1)

            transposes("t4", xn, XNB["t4"])
            wait(("t4", T - 1))
            for n in ("q", "k"):
                w = wait_unit(f"2.{n}")
                for g in range(G):
                    feature_major((f"{n}3",), w, T1, g)
            w = wait_unit("2.v")
            for t in range(T):
                token_major(("v3", t), w, T1, t)
            wait(("v3", T - 1))
            for t in range(T + 1):
                if t < T:
                    self_scores("s3", t, [(A0, A1)])
                if t >= 1:
                    pe.wait_ge(prob_ready, prob["s3", t - 1])
                    self_values("o3", t - 1, A2t, SCP[:, 2 + (t - 1) % 2, :])
            w = wait_unit("2.o")
            for t in range(T):
                wait(("o3", t))
                token_major(("x3", t), w, T1, t)
            transposes("t6", xn, XNB["t6"])
            wait(("t6", T - 1))
            wait_banks(("g3",))
            for t in range(T):
                for i in range(2 * C):
                    c = i % C
                    mm = nc.tensor.matmul(banks(("g3",))[:, t * E:(t + 1) * E], T1[i // C][:, c, tok(t)].bitcast(F32),
                                          small_("wg")[:, c, :], start=(i == 0), stop=(i == 2 * C - 1))
            mm.then_inc(ready, 1)
            for b in range(4):
                w = wait_unit(f"2.w1.{b}")
                for g in range(G):
                    feature_major(("h2", b), w, T1, g)
                w = wait_unit(f"2.w2.{b}")
                for t in range(T):
                    wait(("h2", b, t // TG, C - 1))
                    for e in range(2):
                        token_major(("o2", b, t, e), w, B1, t, chunks=[2 * e, 2 * e + 1])
            if stop == 3:
                return

            transposes("t5", xn, XNB["t5"])
            wait(("t5", T - 1))
            w = wait_unit("3.q")
            for g in range(G):
                feature_major(("q4",), w, T1, g)
            wk = wait_unit("3.k")
            pe.wait_ge(ct_split, 1)
            cl = (clh, cll)
            wait_banks(("kl",))
            for m in range(C):
                for c in range(C):
                    mm = split_product(banks(("kl",))[:, m * BATCH:(m + 1) * BATCH], cut(wk, slice(None), c, slice(m * P, (m + 1) * P)),
                                       cut(cl, slice(None), c, slice(None)), c == 0, c == C - 1)
            mm.then_inc(ready, 1)
            wv = wait_unit("3.v")
            wait_banks(("vlt",))
            for m in range(C):
                for c in range(C):
                    mm = split_product(banks(("vlt",))[:, m * BATCH:(m + 1) * BATCH], cut(wv, slice(None), c, slice(m * P, (m + 1) * P)),
                                       cut(cl, slice(None), c, slice(None)), c == 0, c == C - 1)
            mm.then_inc(ready, 1)
            wait(("vlt",))
            wait_banks(("vl",))
            for m in range(C):
                mm = nc.tensor.transpose(banks(("vl",))[0:BATCH, m * P:(m + 1) * P], VLT[:, m, :], ident)
            mm.then_inc(ready, 1)
            for b in range(BATCH + 1):
                if b < BATCH:
                    pe.wait_ge(ct_split, b + 2)
                    ct = CTh[:, b % NC4, :, :], CTl[:, b % NC4, :, :]
                    wait_banks(("k4", b))
                    bk = banks(("k4", b), 4)
                    for m in range(C):
                        for c in range(C):
                            mm = split_product(bk[:, m, 0:KT * P], cut(wk, slice(None), c, slice(m * P, (m + 1) * P)),
                                               cut(ct, slice(None), c, slice(None)), c == 0, c == C - 1)
                    mm.then_inc(ready, 1)
                    wait_banks(("v4", b))
                    bk = banks(("v4", b), 2)
                    for k in range(KT):
                        for c in range(C):
                            mm = split_product(bk[:, k, :], cut(ct, slice(None), c, slice(k * P, (k + 1) * P)),
                                               cut(wv, slice(None), c, slice(None)), c == 0, c == C - 1)
                    mm.then_inc(ready, 1)
                    wait(("k4", b))
                    pe.wait_ge(qbd_ready, b + 1)
                    wait_banks(("s4", b))
                    bk = banks(("s4", b), 4)
                    for hb in range(C):
                        mm = nc.tensor.matmul(bk[:, hb, 0:KEYS], Qbd[b % 2][:, hb, :], KTb[b % 2][:, hb, :], start=True, stop=True)
                    mm.then_inc(ready, 1)
                if b >= 1:
                    v = b - 1
                    pe.wait_ge(prob_ready, prob["s4", v])
                    wait_banks(("p4", v))
                    bk = banks(("p4", v), 2)
                    for k in range(KT):
                        for hb in range(C):
                            mm = nc.tensor.transpose(bk[:, k, hb * P:(hb + 1) * P], S4[v % 2][:, hb, k * P:(k + 1) * P], ident)
                    mm.then_inc(ready, 1)
                    wait_banks(("l4", v))
                    bk = banks(("l4", v))
                    for hb in range(C):
                        mm = nc.tensor.transpose(bk[0:1, hb * P:(hb + 1) * P], S4[v % 2][:, hb, KT * P:KEYS], ident)
                    mm.then_inc(ready, 1)
                    wait(("l4", v))
                    wait(("v4", v))
                    pe.wait_ge(vrow_in[v % NVR], 16 * (v // NVR + 1))
                    wait_banks(("o4", v))
                    bk = banks(("o4", v))
                    for h in range(HEADS):
                        hb, hl = divmod(h, HG)
                        out_ = bk[hl * DK:(hl + 1) * DK, hb * SEQ:(hb + 1) * SEQ]
                        hs = slice(h * DK, (h + 1) * DK)
                        for k in range(KT):
                            nc.tensor.matmul(out_, Vb[v % 2][:, k, hs], PT4[v % 2][:, k, hs], start=(k == 0), stop=False)
                        mm = nc.tensor.matmul(out_, vrow[0:1, v % NVR, hs], pl4[0:1, v % 2, hs], start=False, stop=True)
                    mm.then_inc(ready, 1)
            w = wait_unit("3.o")
            wait(("o4", BATCH - 1))
            for t in range(T):
                token_major(("x4", t), w, T1, t)
            if stop == 4:
                return

            transposes("t7", xn, XNB["t7"])
            wait(("t7", T - 1))
            for n in ("q", "k"):
                w = wait_unit(f"4.{n}")
                for g in range(G):
                    feature_major((f"{n}5",), w, T1, g)
            wait(("k5", G - 1, C - 1))
            for g in range(G):
                for m in range(C):
                    wait_banks(("qj", g, m))
                    nc.tensor.matmul(banks(("qj", g, m)), jb[:, m, :], A2[:, m, grp(g)], start=True, stop=True).then_inc(ready, 1)
            w = wait_unit("4.v")
            for t in range(T):
                token_major(("v5", t), w, T1, t)
            wait(("v5", T - 1))
            wait(("qj", G - 1, C - 1))
            for t in range(T + 1):
                if t < T:
                    self_scores("s5", t, [(A0, A1), (QJ, A3)])
                if t >= 1:
                    pe.wait_ge(prob_ready, prob["s5", t - 1])
                    self_values("o5", t - 1, A2t, SCP[:, 2 + (t - 1) % 2, :])
            w = wait_unit("4.o")
            for t in range(T):
                wait(("o5", t))
                token_major(("x5", t), w, T1, t)
            if stop == 5:
                return

            transposes("t8", xn, XNB["t8"])
            wait(("t8", T - 1))
            wait_banks(("r6",))
            for t in range(T):
                for i in range(2 * C):
                    c = i % C
                    mm = nc.tensor.matmul(banks(("r6",))[:, t * (E + 1):(t + 1) * (E + 1)], T1[i // C][:, c, tok(t)].bitcast(F32),
                                          small_("router")[:, c, :], start=(i == 0), stop=(i == 2 * C - 1))
            mm.then_inc(ready, 1)
            for b in range(E):
                w = wait_unit(f"5.w1.{b}")
                for g in range(G):
                    feature_major(("h3", b), w, T1, g)
                w = wait_unit(f"5.w2.{b}")
                for t in range(T):
                    wait(("h3", b, t // TG, C - 1))
                    token_major(("o6", b, t), w, B1, t)
            wg = wait_unit("5.gate")
            wu = wait_unit("5.up")
            for g in range(G):
                for m in range(C):
                    for n, w in (("sg", wg), ("su", wu)):
                        wait_banks((n, g, m))
                        for c in range(C):
                            mm = split_product(banks((n, g, m)), cut(w, slice(None), c, slice(m * P, (m + 1) * P)),
                                               cut(T1, slice(None), c, grp(g)), c == 0, c == C - 1)
                        mm.then_inc(ready, 1)
            w = wait_unit("5.down")
            for t in range(T):
                wait(("su", t // TG, C - 1))
                token_major(("os", t), w, B1, t)

        @block.scalar
        def _(act):
            own = [0]

            def step(ins):
                own[0] += 1
                ins.then_inc(act_step, 1)

            def split_high(u):
                if u >= n_units:
                    return
                act.wait_ge(w_full[u % NW], 16 * (u // NW + 1))
                if u >= NW:
                    act.wait_ge(ready, J.last[UNITS[u - NW]])
                nc.scalar.copy(Wh[:, u % NW, :, :], W[:, u % NW, :, :]).then_inc(w_high, 1)

            def next_after(name):
                split_high(UNIT[name] + NW)

            def drain_features(name, dst, scale=1.0):
                for g in range(G):
                    for m in range(C):
                        act.wait_ge(ready, J.ready[name + (g, m)])
                        nc.scalar.activation(dst[:, m, grp(g)], banks(name + (g, m)), ACT.Copy, scale=scale).then_inc(act_drained, 1)

            def high_transposes(name, t):
                act.wait_ge(ready, J.ready[name, t])
                nc.scalar.copy(T1h[:, :, tok(t)], banks((name, t)).rearrange("p (c n) -> p c n", c=C)).then_inc(high, 1)

            def high_of_tmp(key, i, dst):
                act.wait_ge(tmp_ready, tmps[key])
                nc.scalar.copy(dst, SCP[:, i % NTMP, :].rearrange("p (c n) -> p c n", c=C) if len(dst.shape) == 3 else SCP[:, i % NTMP, :]).then_inc(high, 1)

            def high_after_func(name, func, bias):
                keys = [name + (g, m) for g in range(G) for m in range(C)]
                for i in range(len(keys) + 1):
                    if i < len(keys):
                        key = keys[i]
                        n = ring.index(key)
                        act.wait_ge(ready, J.ready[key])
                        if n >= NTMP:
                            act.wait_ge(dve_drained, J.drain[ring[n - NTMP]][1])
                        b = 0.0 if bias is None else bias[:, key[-1]:key[-1] + 1]
                        step(nc.scalar.activation(SCP[:, n % NTMP, :], banks(key), func, bias=b))
                        mine = own[0]
                    if i >= 1:
                        key = keys[i - 1]
                        n = ring.index(key)
                        act.wait_ge(act_step, before)
                        nc.scalar.copy(B1h[:, key[-1], grp(key[-2])], SCP[:, n % NTMP, :]).then_inc(high, 1)
                    before = mine

            def high_values(name, v):
                act.wait_ge(ready, J.ready[name, v])
                src = banks((name, v), 4)[:, :, 0:P].rearrange("p j (h q) -> p j h q", h=C)
                nc.scalar.copy(T1h[:, :, tok(v)].rearrange("p h (j q) -> p j h q", j=PB), src).then_inc(high, 1)

            act.wait_ge(const_in, 16 * 9)
            nc.scalar.activation(scl[:, 0:2 * R + 1], scl[:, 0:2 * R + 1], ACT.Exp, scale=-1.0).then_inc(exp_ready, 1)
            split_high(0)
            split_high(1)
            for g in range(G):
                for t in range(g * TG, g * TG + TG):
                    high_transposes("t1", t)
                for m in range(C):
                    act.wait_ge(ready, J.ready["q", g, m])
                    nc.scalar.activation(B1h[:, m, grp(g)], banks(("q", g, m)), ACT.Identity,
                                         bias=v_("bq0")[:, m:m + 1]).then_inc(high, 1)
            next_after("0.wq")
            drain_features(("qk",), QK)
            next_after("0.wk")
            for t in range(T + 1):
                if t < T:
                    act.wait_ge(bias_ready, soft["s", t])
                    nc.scalar.activation(P1[:, t % 2, :], banks(("s", t))[:, 0:KEYS], ACT.Exp, bias=tiny[:, 2 + t % 2, 0:1],
                                         scale=float(D) ** -0.5, accum_out=tiny[:, 4 + t % 2, 0:1]).then_inc(act_drained, 1)
                if t >= 1:
                    v = t - 1
                    act.wait_ge(ready, J.ready["pt", v])
                    step(nc.scalar.copy(PT1[:, v % 2, 0:KT * P], banks(("pt", v))[:, 0:KT * P]))
                    nc.scalar.copy(PT1[0:PB, v % 2, KT * P:], banks(("pt", v))[0:PB, KT * P:(KT + 1) * P]).then_inc(act_drained, 1)
                    act.wait_ge(ready, J.ready["u", v])
                    nc.scalar.copy(XN[:, v % 2, :], banks(("u", v))).then_inc(act_drained, 1)
                if t >= 2:
                    high_transposes("ut", t - 2)
            high_transposes("ut", T - 1)
            next_after("0.wv")
            if stop == 1:
                return
            for t in range(T):
                act.wait_ge(ready, J.ready["kq", t])
                nc.scalar.copy(ksq[0:R, t, :], banks(("kq", t))[0:R, 0:2 * P]).then_inc(act_drained, 1)
            for t in range(T):
                high_of_tmp(("d", t), t, B1h[:, :, tok(t)])
            next_after("1.proj")
            for t in range(T):
                high_of_tmp(("t3", t), t, T1h[:, :, tok(t)])
            for b in range(4):
                high_after_func(("h1", b), ACT.Gelu_apprx_tanh, v_(f"mb1{b}"))
                next_after(f"1.w1.{b}")
                next_after(f"1.w2.{b}")
            if stop == 2:
                return
            for t in range(T):
                high_of_tmp(("t4", t), t, T1h[:, :, tok(t)])
            drain_features(("q3",), A0)
            next_after("2.q")
            drain_features(("k3",), A1)
            next_after("2.k")
            for t in range(T):
                act.wait_ge(ready, J.ready["v3", t])
                nc.scalar.copy(A2t[:, t, :], banks(("v3", t))).then_inc(act_drained, 1)
            next_after("2.v")
            for t in range(T + 1):
                if t < T:
                    if t >= 2:
                        act.wait_ge(prob_ready, prob["s3", t - 2])
                    act.wait_ge(ready, J.ready["s3", t])
                    bk = banks(("s3", t), 4)
                    nc.scalar.activation(SCP[:, t % 2, :].rearrange("p (l n) -> p l n", l=HG), bk[:, :, 0:P], ACT.Copy,
                                         scale=float(DK) ** -0.5).then_inc(act_drained, 1)
                    act.wait_ge(bias_ready, soft["s3", t])
                    nc.scalar.activation(SCP[:, t % 2, :], SCP[:, t % 2, :], ACT.Exp).then_inc(exp_ready, 1)
                if t >= 1:
                    high_values("o3", t - 1)
            next_after("2.o")
            for t in range(T):
                high_of_tmp(("t6", t), t, T1h[:, :, tok(t)])
            act.wait_ge(bias_ready, soft["g3"])
            nc.scalar.activation(tiny[:, 6, :], tiny[:, 6, :], ACT.Exp).then_inc(exp_ready, 1)
            for b in range(4):
                for g in range(G):
                    for m in range(C):
                        act.wait_ge(ready, J.ready["h2", b, g, m])
                        nc.scalar.activation(B1h[:, m, grp(g)], banks(("h2", b, g, m)), ACT.Relu).then_inc(high, 1)
                next_after(f"2.w1.{b}")
                next_after(f"2.w2.{b}")
            if stop == 3:
                return
            act.wait_ge(last_in, 16)
            nc.scalar.copy(clh[:, :, :], ctxl).then_inc(ct_high, 1)
            for t in range(T):
                high_transposes("t5", t)
            drain_features(("q4",), A0, scale=float(DK) ** -0.5)
            next_after("3.q")
            act.wait_ge(ready, J.ready["kl",])
            nc.scalar.copy(KL, banks(("kl",))[:, 0:C * BATCH].rearrange("p (c b) -> p c b", c=C)).then_inc(act_drained, 1)
            act.wait_ge(ready, J.ready["vlt",])
            nc.scalar.copy(VLT, banks(("vlt",))[:, 0:C * BATCH].rearrange("p (c b) -> p c b", c=C)).then_inc(act_drained, 1)

            def high_context(b):
                act.wait_ge(ctx4_in[b % NC4], 16 * (b // NC4 + 1))
                if b >= NC4:
                    act.wait_ge(ready, J.ready["v4", b - NC4])
                nc.scalar.copy(CTh[:, b % NC4, :, :], CT4[b % NC4]).then_inc(ct_high, 1)

            high_context(0)
            act.wait_ge(ready, J.ready["vl",])
            nc.scalar.copy(VL[0:BATCH, :], banks(("vl",))[0:BATCH, :]).then_inc(act_drained, 1)
            for b in range(BATCH + 1):
                if b + 1 < BATCH:
                    high_context(b + 1)
                if b < BATCH:
                    act.wait_ge(ready, J.ready["k4", b])
                    step(nc.scalar.copy(KTb[b % 2][:, :, KT * P], KL[:, :, b]))
                    nc.scalar.copy(KTb[b % 2][:, :, 0:KT * P], banks(("k4", b), 4)[:, :, 0:KT * P]).then_inc(act_drained, 1)
                if b == BATCH - 1:
                    next_after("3.k")
                if b == BATCH:
                    next_after("3.v")
                if b >= 1:
                    v = b - 1
                    act.wait_ge(ready, J.ready["p4", v])
                    nc.scalar.copy(PT4[v % 2], banks(("p4", v), 2)).then_inc(act_drained, 1)
                    act.wait_ge(ready, J.ready["l4", v])
                    nc.scalar.copy(pl4[0:1, v % 2, :], banks(("l4", v))[0:1, :]).then_inc(act_drained, 1)
                if b < BATCH:
                    act.wait_ge(bias_ready, soft["s4", b])
                    for hb in range(C):
                        ins = nc.scalar.activation(S4[b % 2][:, hb, :], S4[b % 2][:, hb, :], ACT.Exp, bias=tiny[:, 7 + b % 2, hb:hb + 1],
                                                   accum_out=tiny[:, 9 + b % 2, hb:hb + 1])
                        if hb == C - 1:
                            ins.then_inc(exp_ready, 1)
                        else:
                            step(ins)
                if b >= 1:
                    v = b - 1
                    act.wait_ge(ready, J.ready["o4", v])
                    nc.scalar.copy(T1h[:, :, v * SEQ:(v + 1) * SEQ], banks(("o4", v))[:, 0:P].rearrange("p (h q) -> p h q", h=C)).then_inc(high, 1)
            if stop == 4:
                return
            next_after("3.o")
            for t in range(T):
                high_transposes("t7", t)
            for n, b, dst, th in (("q5", "bq5", A0, A2), ("k5", "bk5", A1, A3)):
                for g in range(G):
                    for m in range(C):
                        act.wait_ge(ready, J.ready[n, g, m])
                        step(nc.scalar.activation(dst[:, m, grp(g)], banks((n, g, m)), ACT.Identity, bias=v_(b)[:, m:m + 1]))
                        nc.scalar.activation(th[:, m, grp(g)], banks((n, g, m)), ACT.Tanh, bias=v_(b)[:, m:m + 1]).then_inc(act_drained, 1)
                next_after("4." + n[0])
            act.wait_ge(setup_ready, 1)
            for g in range(G):
                for m in range(C):
                    act.wait_ge(ready, J.ready["qj", g, m])
                    nc.scalar.activation(QJ[:, m, grp(g)], banks(("qj", g, m)), ACT.Copy, scale=tiny[:, 11, 0:1]).then_inc(act_drained, 1)
            next_after("4.v")
            for t in range(T + 1):
                if t < T:
                    act.wait_ge(bias_ready, soft["s5", t])
                    nc.scalar.activation(SCP[:, t % 2, :], SCP[:, t % 2, :], ACT.Exp).then_inc(exp_ready, 1)
                if t >= 1:
                    high_values("o5", t - 1)
            if stop == 5:
                return
            next_after("4.o")
            for t in range(T):
                high_transposes("t8", t)
            act.wait_ge(bias_ready, soft["r6"])
            nc.scalar.activation(tiny[:, 6, :], tiny[:, 6, :], ACT.Exp).then_inc(exp_ready, 1)
            nc.scalar.activation(tiny[:, 12, 0:T], tiny[:, 12, 0:T], ACT.Exp, scale=-1.0).then_inc(exp_ready, 1)
            for b in range(E):
                high_after_func(("h3", b), ACT.Silu, None)
                next_after(f"5.w1.{b}")
                next_after(f"5.w2.{b}")
            for g in range(G):
                for m in range(C):
                    act.wait_ge(ready, J.ready["sg", g, m])
                    nc.scalar.activation(A2[:, m, grp(g)], banks(("sg", g, m)), ACT.Silu).then_inc(act_drained, 1)
                    if g + m > 0:
                        gp, mp = (g, m - 1) if m else (g - 1, C - 1)
                        high_of_tmp(("su", gp, mp), gp * C + mp, B1h[:, mp, grp(gp)])
            high_of_tmp(("su", G - 1, C - 1), G * C - 1, B1h[:, C - 1, grp(G - 1)])
            next_after("5.gate")

        @block.gpsimd
        def _(pool):
            def power(name, out_, base, n):
                pool.wait_ge(base_ready, powers[name])
                nc.gpsimd.tensor_tensor(out_, base, half[:, 0:n], ALU.pow).then_inc(power_ready, 1)

            pool.wait_ge(base_ready, powers["dec"])
            nc.gpsimd.tensor_tensor(dec[:, 4, :], dec[:, 0, :], dec[:, 2, :], ALU.pow).then_inc(pool_step, 1)
            nc.gpsimd.tensor_tensor(dec[:, 5, :], dec[:, 0, :], dec[:, 3, :], ALU.pow).then_inc(power_ready, 1)
            power("n1", rs[:, 0, :], ve[:, 0, :], T)
            if stop == 1:
                return
            power("n2", rs[:, 0, :], ve[:, 0, :], T)
            power("n2r", rs[:, 1, :], ve[:, 1, :], T)
            pool.wait_ge(base_ready, powers["uv"])
            nc.gpsimd.tensor_tensor(tiny[:, 13, 0:2 * T], tiny[:, 14, 0:2 * T], half[:, 0:2 * T], ALU.pow).then_inc(power_ready, 1)
            power("n3", rs[:, 0, :], ve[:, 0, :], T)
            if stop == 2:
                return
            power("n4", rs[:, 0, :], ve[:, 0, :], T)
            power("n4r", rs[:, 1, :], ve[:, 1, :], T)
            power("n6", rs[:, 0, :], ve[:, 0, :], T)
            if stop == 3:
                return
            pool.wait_ge(ready, J.ready["o2", 3, T - 1, 1])
            for i in range(2):
                nc.gpsimd.memset(Qbd[i], 0.0).then_inc(zero_ready, 1)
            power("n5", rs[:, 0, :], ve[:, 0, :], T)
            pool.wait_ge(zero_ready, 2)
            pool.wait_ge(act_drained, J.drain["q4", G - 1, C - 1][1])
            for b in range(BATCH):
                if b >= 2:
                    pool.wait_ge(ready, J.ready["s4", b - 2])
                for hl in range(HG):
                    hs = slice(hl * DK, (hl + 1) * DK)
                    nc.gpsimd.tensor_copy(Qbd[b % 2][hs, :, hs], A0[hs, :, b * SEQ:(b + 1) * SEQ]).then_inc(
                        qbd_ready if hl == HG - 1 else pool_step, 1)
            if stop == 4:
                return
            power("n7", rs[:, 0, :], ve[:, 0, :], T)
            if stop == 5:
                return
            power("n8", rs[:, 0, :], ve[:, 0, :], T)

        @block.vector
        def _(dve):
            steps = [0]

            def link(ins):
                steps[0] += 1
                ins.then_inc(dve_step, 1)
                dve.wait_ge(dve_step, steps[0])

            def step(ins):
                steps[0] += 1
                ins.then_inc(dve_step, 1)

            def stats(src, t):
                link(nc.vector.bn_stats(bns[:, :], src[:, t, :]))
                link(nc.vector.bn_aggr(mv[:, t, :], bns[:, :]))

            def pipelined(first, second, tiles=range(T)):
                for t in tiles:
                    first(t)
                    if t > tiles[0]:
                        second(t - 1)
                second(tiles[-1])

            def normalise(name, job, src, eps, then, first=0, upto=T):
                if name is not None:
                    nc.vector.tensor_scalar(ve[:, 0, :], mv[:, :, 1], eps, None, ALU.add).then_inc(base_ready, 1)
                    dve.wait_ge(power_ready, powers[name])

                def one(t):
                    if t >= 2:
                        dve.wait_ge(ready, J.ready[job, t - 2])
                    nc.vector.tensor_scalar(XN[:, t % 2, :], src[:, t, :], mv[:, t, 0:1], rs[:, 0, t:t + 1],
                                            ALU.subtract, ALU.mult).then_inc(xn_ready, 1)

                pipelined(one, then, range(first, upto))

            def wait(sem_, n):
                dve.wait_ge(sem_, n)

            def fence():
                dve.wait_ge(dve_step, steps[0])

            def split_low(u):
                if u >= n_units:
                    return
                dve.wait_ge(w_high, u + 1)
                nc.vector.tensor_tensor(Wl[:, u % NW, :, :], W[:, u % NW, :, :], Wh[:, u % NW, :, :].bitcast(F32),
                                        ALU.subtract).then_inc(w_split, 1)

            def next_after(name):
                split_low(UNIT[name] + NW)

            def low(key, pair, at, src=None, bias=None):
                dve.wait_ge(high, J.hi[key])
                hi, lo = pair[0][at], pair[1][at]
                src = banks(key) if src is None else src
                if len(hi.shape) == 3:
                    src = src.rearrange("p (c n) -> p c n", c=C)
                if bias is None:
                    nc.vector.tensor_tensor(lo, src, hi.bitcast(F32), ALU.subtract).then_inc(dve_drained, 1)
                else:
                    nc.vector.scalar_tensor_tensor(lo, src, bias, hi.bitcast(F32), ALU.add, ALU.subtract).then_inc(dve_drained, 1)

            A_ = slice(None)

            def low_transposes(name, t):
                low((name, t), T1, (A_, A_, tok(t)))

            def low_func(name):
                for g in range(G):
                    for m in range(C):
                        key = name + (g, m)
                        low(key, B1, (A_, m, grp(g)), SCP[:, ring.index(key) % NTMP, :])

            def low_values(name, v):
                dve.wait_ge(high, J.hi[name, v])
                src = banks((name, v), 4)[:, :, 0:P].rearrange("p j (h q) -> p j h q", h=C)
                hi, lo = (x[:, :, tok(v)].rearrange("p h (j q) -> p j h q", j=PB) for x in T1)
                nc.vector.tensor_tensor(lo, src, hi.bitcast(F32), ALU.subtract).then_inc(dve_drained, 1)

            def row_bias(name):
                i = ROW.index(name)
                dve.wait_ge(row_in[i % NR], 16 * (i // NR + 1))
                return r_(name)

            link(nc.vector.memset(half[:, :], -0.5))
            dve.wait_ge(const_in, 16 * 9)
            dve.wait_ge(exp_ready, 1)
            link(nc.vector.tensor_scalar(scl[:, 0:2 * R + 1], scl[:, 0:2 * R + 1], 1.0, None, ALU.add))
            link(nc.vector.reciprocal(scl[:, 0:2 * R + 1], scl[:, 0:2 * R + 1]))
            step(nc.vector.tensor_scalar(dec[:, 0, :], s_("decay"), 0.15, 1.0, ALU.max, ALU.min))
            link(nc.vector.memset(dec[:, 1, :], 1.0))
            link(nc.vector.tensor_scalar(dec[:, 2, :], dec[:, 1, :], con_("pos"), None, ALU.mult))
            nc.vector.tensor_scalar(dec[:, 3, :], dec[:, 2, :], -1.0, None, ALU.mult).then_inc(base_ready, 1)
            dve.wait_ge(power_ready, powers["dec"])
            link(nc.vector.tensor_tensor(dec[:, 4, :], dec[:, 4, :], s_("alpha"), ALU.mult))
            link(nc.vector.tensor_scalar(s_("kern"), s_("kern"), s_("gate"), None, ALU.mult))
            link(nc.vector.tensor_scalar(convm, con_("shift")[:, 0:P], s_("kern")[:, 0:1], None, ALU.mult))
            for m in range(1, 4):
                link(nc.vector.scalar_tensor_tensor(convm, con_("shift")[:, m * P:(m + 1) * P], s_("kern")[:, m:m + 1],
                                                    convm, ALU.mult, ALU.add))
            link(nc.vector.tensor_copy(mk[:, :], mk8[:, :]))
            step(nc.vector.tensor_scalar(nm[:, :], mk[:, :], 1.0, 1e9, ALU.subtract, ALU.mult))
            nc.vector.tensor_scalar(tiny[:, 11, 0:1], s_("lam"), float(DK) ** 0.5, None, ALU.mult).then_inc(setup_ready, 1)

            dve.wait_ge(x_in, 16 * T)
            for t in range(T):
                stats(X, t)
            split_low(0)
            split_low(1)

            def after_tile(name):
                return lambda t: low_transposes(name, t)

            normalise("n1", "t1", X, 1e-5, after_tile("t1"), upto=TG)
            for m in range(C):
                low(("q", 0, m), B1, (A_, m, grp(0)), bias=v_("bq0")[:, m:m + 1])
            normalise(None, "t1", X, 1e-5, after_tile("t1"), first=TG)
            for m in range(C):
                low(("q", 1, m), B1, (A_, m, grp(1)), bias=v_("bq0")[:, m:m + 1])
            next_after("0.wq")
            dve.wait_ge(ready, J.ready["c",])
            isd = float(D) ** -0.5
            nc.vector.tensor_scalar(cs, banks(("c",))[:, 0:T], isd, None, ALU.mult).then_inc(dve_drained, 1)
            dve.wait_ge(dve_drained, J.drain["c",][1])

            next_after("0.wk")

            def u_drain(v):
                low(("ut", v), T1, (A_, A_, tok(v)))

            for t in range(T):
                dve.wait_ge(ready, J.ready["s", t])
                link(nc.vector.reduce_max(tiny[:, 1, 0:1], banks(("s", t))[:, 0:KEYS], AX_X))
                link(nc.vector.scalar_tensor_tensor(tiny[:, 1, 1:2], tiny[:, 1, 0:1], isd, cs[:, t:t + 1], ALU.mult, ALU.add))
                nc.vector.scalar_tensor_tensor(tiny[:, 2 + t % 2, 0:1], tiny[:, 1, 1:2], -1.0, cs[:, t:t + 1],
                                               ALU.mult, ALU.add).then_inc(bias_ready, 1)
                dve.wait_ge(act_drained, J.drain["s", t][1])
                link(nc.vector.reciprocal(tiny[:, 1, 2:3], tiny[:, 4 + t % 2, 0:1]))
                nc.vector.tensor_scalar(P1[:, t % 2, :], P1[:, t % 2, :], tiny[:, 1, 2:3], None, ALU.mult).then_inc(prob_ready, 1)
                dve.wait_ge(prob_ready, prob["s", t])
                nc.vector.tensor_scalar(PL[:, t % 2, :], con_("row_of"), P1[:, t % 2, KT * P:KEYS], None, ALU.mult).then_inc(ownlast, 1)
                if t >= 2:
                    u_drain(t - 2)
            u_drain(T - 2)
            u_drain(T - 1)

            def residual(key, dst, bias, fin=None, then=None):
                t = key[1] if fin is None else fin
                dve.wait_ge(ready, J.ready[key])
                if bias is None:
                    nc.vector.tensor_tensor(dst[:, t, :], banks(key), dst[:, t, :], ALU.add).then_inc(dve_drained, 1)
                else:
                    link(nc.vector.tensor_tensor(dst[:, t, :], banks(key), dst[:, t, :], ALU.add))
                    nc.vector.tensor_tensor(dst[:, t, :], dst[:, t, :], bias, ALU.add).then_inc(dve_drained, 1)

            for t in range(T):
                residual(("y", t), X, row_bias("bv0"))
                if stop > 1:
                    dve.wait_ge(dve_drained, J.drain["y", t][1])
                    stats(X, t)
            if stop == 1:
                return
            next_after("0.wv")

            def second_norm(n1, n2, eps2):
                nc.vector.tensor_scalar(ve[:, 0, :], mv[:, :, 1], 1e-5, None, ALU.add).then_inc(base_ready, 1)
                dve.wait_ge(power_ready, powers[n1])
                link(nc.vector.tensor_tensor(ve[:, 2, :], mv[:, :, 1], rs[:, 0, :], ALU.mult))
                link(nc.vector.tensor_tensor(ve[:, 2, :], ve[:, 2, :], rs[:, 0, :], ALU.mult))
                nc.vector.tensor_scalar(ve[:, 1, :], ve[:, 2, :], eps2, None, ALU.add).then_inc(base_ready, 1)
                dve.wait_ge(power_ready, powers[n2])

            second_norm("n2", "n2r", 1e-6)
            for t in range(T):
                link(nc.vector.tensor_scalar(H[:, t, :], X[:, t, :], mv[:, t, 0:1], rs[:, 0, t:t + 1], ALU.subtract, ALU.mult))
                nc.vector.tensor_scalar(HH[:, t, :], H[:, t, :], rs[:, 1, t:t + 1], None, ALU.mult).then_inc(qk_scaled, 1)

            def scaled(key, w, b=None):
                t = key[1]
                dve.wait_ge(ready, J.ready[key])
                src = banks(key).rearrange("p (c n) -> p c n", c=C)
                dst = SCP[:, t % NTMP, :].rearrange("p (c n) -> p c n", c=C)
                ins = nc.vector.tensor_tensor(dst, src, bc(w.unsqueeze(2), P, C, P), ALU.mult)
                if b is not None:
                    link(ins)
                    ins = nc.vector.tensor_tensor(dst, dst, bc(b.unsqueeze(2), P, C, P), ALU.add)
                ins.then_inc(tmp_ready, 1)

            def low_tmp(key, pair, at, i):
                low(key, pair, at, SCP[:, i % NTMP, :])

            def scaled_tiles(name, pair, w, b=None):
                return pipelined(lambda t: scaled((name, t), w, b), lambda t: low_tmp((name, t), pair, (A_, A_, tok(t)), t))

            for t in range(T):
                dve.wait_ge(ready, J.ready["t2", t])
                nc.vector.tensor_tensor(A0[:, :, tok(t)], banks(("t2", t)).rearrange("p (c n) -> p c n", c=C),
                                        bc(v_("norm1").unsqueeze(2), P, C, P), ALU.mult).then_inc(dve_drained, 1)
            for t in range(T):
                dve.wait_ge(ready, J.ready["uv", t])
                nc.vector.tensor_copy(qk2[:, t, :], banks(("uv", t))[:, 0:2 * R]).then_inc(dve_drained, 1)
            dve.wait_ge(dve_drained, J.drain["uv", T - 1][1])
            link(nc.vector.tensor_tensor(sq, qk2, qk2, ALU.mult))
            link(nc.vector.reduce_sum(tiny[:, 15, 0:2 * T].rearrange("p (t i) -> p t i", i=2), sq.rearrange("p t (i r) -> p t i r", i=2), AX_X))
            nc.vector.tensor_scalar(tiny[:, 14, 0:2 * T], tiny[:, 15, 0:2 * T], 1e-16, None, ALU.max).then_inc(base_ready, 1)
            dve.wait_ge(power_ready, powers["uv"])
            q4d = qk2.rearrange("p t (i r) -> p t i r", i=2)
            link(nc.vector.tensor_tensor(qk2.rearrange("p t (i r) -> p (t i) r", i=2), qk2.rearrange("p t (i r) -> p (t i) r", i=2),
                                         bc(tiny[:, 13, 0:2 * T].unsqueeze(2), P, 2 * T, R), ALU.mult))
            link(nc.vector.tensor_tensor(q4d[:, :, 0, :], q4d[:, :, 0, :], bc(dec[:, 4:5, :], P, T, R), ALU.mult))
            nc.vector.tensor_tensor(q4d[:, :, 1, :], q4d[:, :, 1, :], bc(dec[:, 5:6, :], P, T, R), ALU.mult).then_inc(qk_scaled, 1)
            for t in range(T):
                dve.wait_ge(ready, J.ready["A", t])
                link(nc.vector.tensor_tensor(AT[:, t, :], banks(("A", t))[:, 0:P], con_("lower"), ALU.mult))
                nc.vector.tensor_tensor(AT[:, t, :], AT[:, t, :], convm, ALU.add).then_inc(dve_drained, 1)
            scaled_tiles("d", B1, v_("norm1"))
            for t in range(T):
                residual(("pr", t), H, row_bias("proj_b"))
                dve.wait_ge(dve_drained, J.drain["pr", t][1])
                stats(H, t)
                step(nc.vector.tensor_tensor(X[:, t, :], X[:, t, :], H[:, t, :], ALU.add))
            next_after("1.proj")
            link(nc.vector.tensor_tensor(ve[:, 2, :], mv[:, :, 0], mv[:, :, 0], ALU.mult))
            link(nc.vector.tensor_tensor(ve[:, 2, :], ve[:, 2, :], mv[:, :, 1], ALU.add))
            nc.vector.tensor_scalar(ve[:, 0, :], ve[:, 2, :], 1e-6, None, ALU.add).then_inc(base_ready, 1)
            dve.wait_ge(power_ready, powers["n3"])

            def norm_h(t):
                if t >= 2:
                    dve.wait_ge(ready, J.ready["t3", t - 2])
                nc.vector.tensor_scalar(XN[:, t % 2, :], H[:, t, :], rs[:, 0, t:t + 1], None, ALU.mult).then_inc(xn_ready, 1)
                scaled_lag("t3", t, v_("norm2"))

            def scaled_lag(name, t, w, b=None):
                if t >= 1:
                    scaled((name, t - 1), w, b)
                if t >= 2:
                    low_tmp((name, t - 2), T1, (A_, A_, tok(t - 2)), t - 2)

            def scaled_rest(name, w, b=None):
                scaled((name, T - 1), w, b)
                low_tmp((name, T - 2), T1, (A_, A_, tok(T - 2)), T - 2)
                low_tmp((name, T - 1), T1, (A_, A_, tok(T - 1)), T - 1)

            for t in range(T):
                norm_h(t)
            scaled_rest("t3", v_("norm2"))
            for b in range(4):
                low_func(("h1", b))
                next_after(f"1.w1.{b}")
                bias = row_bias("mb2") if b == 3 else None
                for t in range(T):
                    if b:
                        dve.wait_ge(dve_drained, J.drain["o1", b - 1, t][1])
                    residual(("o1", b, t), X, bias, fin=t)
                    if b == 3 and stop > 2:
                        dve.wait_ge(dve_drained, J.drain["o1", b, t][1])
                        stats(X, t)
                next_after(f"1.w2.{b}")
            if stop == 2:
                return

            second_norm("n4", "n4r", 1e-5)
            for t in range(T):
                link(nc.vector.tensor_scalar(H[:, t, :], X[:, t, :], mv[:, t, 0:1], rs[:, 0, t:t + 1], ALU.subtract, ALU.mult))
                if t >= 2:
                    dve.wait_ge(ready, J.ready["t4", t - 2])
                nc.vector.tensor_scalar(XN[:, t % 2, :], H[:, t, :], rs[:, 1, t:t + 1], None, ALU.mult).then_inc(xn_ready, 1)
                scaled_lag("t4", t, v_("g1"), v_("b1"))
            scaled_rest("t4", v_("g1"), v_("b1"))
            next_after("2.q")
            next_after("2.k")
            next_after("2.v")

            def softmax(name, t, SC, PTs):
                s3 = SC.rearrange("p (h k) -> p h k", k=SEQ)
                link(nc.vector.reduce_max(tiny[:, 1, 0:HEADS], s3, AX_X))
                nc.vector.tensor_tensor(s3, s3, bc(tiny[:, 1, 0:HEADS].unsqueeze(2), P, HEADS, SEQ), ALU.subtract).then_inc(bias_ready, 1)
                dve.wait_ge(exp_ready, exps[name, t])
                link(nc.vector.reduce_sum(tiny[:, 1, 16:32], s3, AX_X))
                link(nc.vector.reciprocal(tiny[:, 1, 32:48], tiny[:, 1, 16:32]))
                link(nc.vector.tensor_tensor(s3, s3, bc(tiny[:, 1, 32:48].unsqueeze(2), P, HEADS, SEQ), ALU.mult))
                if t >= 2:
                    dve.wait_ge(ready, J.ready[{"s3": "o3", "s5": "o5"}[name], t - 2])
                nc.vector.transpose(PTs, SC).then_inc(prob_ready, 1)

            exps = {}
            for t in range(T):
                exps["s3", t] = len(exps) + 2
            exps["g3"] = len(exps) + 2
            for b in range(BATCH):
                exps["s4", b] = len(exps) + 2
            for t in range(T):
                exps["s5", t] = len(exps) + 2
            exps["r6"] = len(exps) + 2
            exps["sig"] = len(exps) + 2

            for t in range(T):
                dve.wait_ge(act_drained, J.drain["s3", t][1])
                softmax("s3", t, SCP[:, t % 2, :], SCP[:, 2 + t % 2, :])
                if t >= 1:
                    low_values("o3", t - 1)
            low_values("o3", T - 1)
            for t in range(T):
                residual(("x3", t), H, None)
                dve.wait_ge(dve_drained, J.drain["x3", t][1])
                stats(H, t)
                step(nc.vector.tensor_tensor(X[:, t, :], X[:, t, :], H[:, t, :], ALU.add))
            next_after("2.o")
            nc.vector.tensor_scalar(ve[:, 0, :], mv[:, :, 1], 1e-5, None, ALU.add).then_inc(base_ready, 1)
            dve.wait_ge(power_ready, powers["n6"])
            for t in range(T):
                if t >= 2:
                    dve.wait_ge(ready, J.ready["t6", t - 2])
                nc.vector.tensor_scalar(XN[:, t % 2, :], H[:, t, :], mv[:, t, 0:1], rs[:, 0, t:t + 1],
                                        ALU.subtract, ALU.mult).then_inc(xn_ready, 1)
                scaled_lag("t6", t, v_("g2"), v_("b2"))
            scaled_rest("t6", v_("g2"), v_("b2"))

            def route(name, cols, renorm):
                L = tiny[:, 0, :].rearrange("p (t e) -> p t e", e=E)
                X6 = tiny[:, 6, :].rearrange("p (t e) -> p t e", e=E)
                sel = tiny[:, 5, :].rearrange("p (t e) -> p t e", e=E)
                dve.wait_ge(ready, J.ready[name,])
                src = banks((name,))[:, 0:T * cols].rearrange("p (t e) -> p t e", e=cols)
                if cols > E:
                    step(nc.vector.tensor_copy(tiny[:, 12, 0:T], src[:, :, E]))
                nc.vector.tensor_copy(L, src[:, :, 0:E]).then_inc(dve_drained, 1)
                dve.wait_ge(dve_drained, J.drain[name,][1])
                fence()
                link(nc.vector.reduce_max(tiny[:, 1, 0:T], L, AX_X))
                nc.vector.tensor_tensor(X6, L, bc(tiny[:, 1, 0:T].unsqueeze(2), P, T, E), ALU.subtract).then_inc(bias_ready, 1)
                other = bc(L.unsqueeze(2), P, T, E, E)
                own = bc(L.unsqueeze(3), P, T, E, E)
                gt = rank_in[:, 0, :, :].rearrange("p t (e f) -> p t e f", f=E)
                eq = rank_in[:, 1, :, :].rearrange("p t (e f) -> p t e f", f=E)
                step(nc.vector.tensor_tensor(gt, other, own, ALU.is_gt))
                link(nc.vector.tensor_tensor(eq, other, own, ALU.is_equal))
                link(nc.vector.tensor_tensor(rank_in[:, 1, :, :], rank_in[:, 1, :, :], bc(con_("before").unsqueeze(1), P, T, E * E), ALU.mult))
                link(nc.vector.tensor_tensor(rank_in[:, 0, :, :], rank_in[:, 0, :, :], rank_in[:, 1, :, :], ALU.add))
                link(nc.vector.reduce_sum(sel, gt, AX_X))
                link(nc.vector.tensor_scalar(sel, sel, 1.5, None, ALU.is_lt))
                dve.wait_ge(exp_ready, exps[name])
                if not renorm:
                    link(nc.vector.reduce_sum(tiny[:, 1, 8:16], X6, AX_X))
                link(nc.vector.tensor_tensor(X6, X6, sel, ALU.mult))
                if renorm:
                    link(nc.vector.reduce_sum(tiny[:, 1, 8:16], X6, AX_X))
                link(nc.vector.reciprocal(tiny[:, 1, 16:24], tiny[:, 1, 8:16]))
                link(nc.vector.tensor_tensor(cw[:, :, 0:E], X6, bc(tiny[:, 1, 16:24].unsqueeze(2), P, T, E), ALU.mult))

            route("g3", E, True)

            def weighted(key, t, e):
                dve.wait_ge(ready, J.ready[key])
                nc.vector.scalar_tensor_tensor(X[:, t, :], banks(key), cw[:, t, e:e + 1], X[:, t, :],
                                               ALU.mult, ALU.add).then_inc(dve_drained, 1)

            for b in range(4):
                for g in range(G):
                    for m in range(C):
                        dve.wait_ge(high, J.hi["h2", b, g, m])
                        nc.vector.scalar_tensor_tensor(B1l[:, m, grp(g)], banks(("h2", b, g, m)), 0.0, B1h[:, m, grp(g)].bitcast(F32),
                                                       ALU.max, ALU.subtract).then_inc(dve_drained, 1)
                next_after(f"2.w1.{b}")
                for t in range(T):
                    for e in range(2):
                        if e == 1:
                            dve.wait_ge(dve_drained, J.drain["o2", b, t, 0][1])
                        weighted(("o2", b, t, e), t, 2 * b + e)
                    if b == 3 and stop > 3:
                        dve.wait_ge(dve_drained, J.drain["o2", b, t, 1][1])
                        stats(X, t)
                next_after(f"2.w2.{b}")
            if stop == 3:
                return

            dve.wait_ge(ct_high, 1)
            nc.vector.tensor_tensor(cll[:, :, :], ctxl, clh[:, :, :].bitcast(F32), ALU.subtract).then_inc(ct_split, 1)
            normalise("n5", "t5", X, 1e-5, after_tile("t5"))
            next_after("3.q")

            def low_context(b):
                dve.wait_ge(ct_high, b + 2)
                nc.vector.tensor_tensor(CTl[:, b % NC4, :, :], CT4[b % NC4], CTh[:, b % NC4, :, :].bitcast(F32),
                                        ALU.subtract).then_inc(ct_split, 1)

            def o4_drain(v):
                dve.wait_ge(high, J.hi["o4", v])
                qs = slice(v * SEQ, (v + 1) * SEQ)
                nc.vector.tensor_tensor(T1l[:, :, qs], banks(("o4", v))[:, 0:P].rearrange("p (h q) -> p h q", h=C),
                                        T1h[:, :, qs].bitcast(F32), ALU.subtract).then_inc(dve_drained, 1)

            low_context(0)
            for b in range(BATCH):
                if b + 1 < BATCH:
                    low_context(b + 1)
                S = S4[b % 2]
                dve.wait_ge(ready, J.ready["v4", b])
                nc.vector.tensor_copy(Vb[b % 2], banks(("v4", b), 2)).then_inc(dve_drained, 1)
                if b == BATCH - 1:
                    next_after("3.k")
                dve.wait_ge(ready, J.ready["s4", b])
                nc.vector.tensor_tensor(S, banks(("s4", b), 4)[:, :, 0:KEYS], bc(mk[:, :].unsqueeze(1), P, C, KEYS), ALU.mult).then_inc(dve_drained, 1)
                dve.wait_ge(dve_drained, J.drain["s4", b][1])
                link(nc.vector.tensor_tensor(S, S, bc(nm[:, :].unsqueeze(1), P, C, KEYS), ALU.add))
                link(nc.vector.reduce_max(tiny[:, 1, 0:C], S, AX_X))
                nc.vector.tensor_scalar(tiny[:, 7 + b % 2, 0:C], tiny[:, 1, 0:C], -1.0, None, ALU.mult).then_inc(bias_ready, 1)
                dve.wait_ge(exp_ready, exps["s4", b])
                link(nc.vector.reciprocal(tiny[:, 1, 8:8 + C], tiny[:, 9 + b % 2, 0:C]))
                nc.vector.tensor_tensor(S, S, bc(tiny[:, 1, 8:8 + C].unsqueeze(2), P, C, KEYS), ALU.mult).then_inc(prob_ready, 1)
                if b >= 1:
                    o4_drain(b - 1)
            next_after("3.v")
            o4_drain(BATCH - 1)
            for t in range(T):
                residual(("x4", t), X, row_bias("wo_b"))
                if stop > 4:
                    dve.wait_ge(dve_drained, J.drain["x4", t][1])
                    stats(X, t)
            if stop == 4:
                return

            next_after("3.o")
            normalise("n7", "t7", X, 1e-5, after_tile("t7"))
            next_after("4.q")
            next_after("4.k")
            bias = row_bias("bv5")
            for t in range(T):
                dve.wait_ge(ready, J.ready["v5", t])
                nc.vector.tensor_tensor(A2t[:, t, :], banks(("v5", t)), bias, ALU.add).then_inc(dve_drained, 1)
            next_after("4.v")
            for t in range(T):
                dve.wait_ge(ready, J.ready["s5", t])
                bk = banks(("s5", t), 4)
                nc.vector.scalar_tensor_tensor(SCP[:, t % 2, :].rearrange("p (l n) -> p l n", l=HG), bk[:, :, 0:P], float(DK) ** -0.5,
                                               bc(con_("causal").unsqueeze(1), P, HG, P), ALU.mult, ALU.add).then_inc(dve_drained, 1)
                dve.wait_ge(dve_drained, J.drain["s5", t][1])
                fence()
                softmax("s5", t, SCP[:, t % 2, :], SCP[:, 2 + t % 2, :])
                if t >= 1:
                    low_values("o5", t - 1)
            low_values("o5", T - 1)
            for t in range(T):
                residual(("x5", t), X, row_bias("bo5"))
                if stop > 5:
                    dve.wait_ge(dve_drained, J.drain["x5", t][1])
                    stats(X, t)
            if stop == 5:
                return

            next_after("4.o")
            normalise("n8", "t8", X, 1e-5, after_tile("t8"))
            route("r6", E + 1, False)
            dve.wait_ge(exp_ready, exps["sig"])
            link(nc.vector.tensor_scalar(tiny[:, 12, 0:T], tiny[:, 12, 0:T], 1.0, None, ALU.add))
            link(nc.vector.reciprocal(cw[:, :, E], tiny[:, 12, 0:T]))
            for b in range(E):
                low_func(("h3", b))
                next_after(f"5.w1.{b}")
                for t in range(T):
                    if b:
                        dve.wait_ge(dve_drained, J.drain["o6", b - 1, t][1])
                    weighted(("o6", b, t), t, b)
                next_after(f"5.w2.{b}")
            for g in range(G):
                for m in range(C):
                    i = g * C + m
                    dve.wait_ge(act_drained, J.drain["sg", g, m][1])
                    dve.wait_ge(ready, J.ready["su", g, m])
                    nc.vector.tensor_tensor(SCP[:, i % NTMP, :], banks(("su", g, m)), A2[:, m, grp(g)], ALU.mult).then_inc(tmp_ready, 1)
                    if i:
                        gp, mp = divmod(i - 1, C)
                        low_tmp(("su", gp, mp), B1, (A_, mp, grp(gp)), i - 1)
            low_tmp(("su", G - 1, C - 1), B1, (A_, C - 1, grp(G - 1)), G * C - 1)
            next_after("5.gate")
            for t in range(T):
                weighted(("os", t), t, E)


def kernel(**inp):
    import concourse.bacc as _bacc
    from concourse.bass_utils import run_bass_kernel_spmd as _run

    A = {k: np.asarray(v) for k, v in inp.items()}

    def unit(w):
        return w.reshape(C, P, D).transpose(1, 0, 2)

    mats = [A["L0_xattn_Wq"].T, A["L0_xattn_Wk"], A["L0_xattn_Wv"].T, A["L0_attn_proj_w"].T]
    for b in range(4):
        mats += [A["L0_attn_mlp_w1"][:, b * D:(b + 1) * D], A["L0_attn_mlp_w2"][b * D:(b + 1) * D]]
    mats += [A["L0_ffn_Wq"], A["L0_ffn_Wk"], A["L0_ffn_Wv"], A["L0_ffn_Wo"]]
    for b in range(4):
        mats += [np.concatenate([A["L0_ffn_W1"][2 * b], A["L0_ffn_W1"][2 * b + 1]], 1),
                 np.concatenate([A["L0_ffn_W2"][2 * b], A["L0_ffn_W2"][2 * b + 1]], 0)]
    mats += [A["L1_xattn_wq"].T, A["L1_xattn_wk"].T, A["L1_xattn_wv"].T, A["L1_xattn_wo_w"].T]
    mats += [A["L1_attn_Wq"].T, A["L1_attn_Wk"].T, A["L1_attn_Wv"].T, A["L1_attn_Wo"].T]
    for e in range(E):
        mats += [A["L1_ffn_w1"][e], A["L1_ffn_w2"][e]]
    mats += [A["L1_ffn_shared_gate_up"][:, :D], A["L1_ffn_shared_gate_up"][:, D:], A["L1_ffn_shared_down"]]
    units = np.ascontiguousarray(np.stack([unit(m) for m in mats]))

    mb1 = A["L0_attn_mlp_b1"].reshape(4, D)
    vs = [A["L0_xattn_bq"], A["L0_attn_norm1_w"], A["L0_attn_norm2_w"], *mb1, A["L0_ffn_g1"], A["L0_ffn_b1"], A["L0_ffn_g2"],
          A["L0_ffn_b2"], A["L1_attn_bq"], A["L1_attn_bk"], A["L0_xattn_bk"]]
    vecs = np.ascontiguousarray(np.stack(vs).reshape(len(VEC), C, P).transpose(2, 0, 1))
    rows = np.stack([A["L0_xattn_bv"], A["L0_attn_proj_b"], A["L0_attn_mlp_b2"], A["L1_xattn_wo_b"], A["L1_attn_bv"], A["L1_attn_bo"]])
    scalars = np.concatenate([A["L0_attn_decay_logit"], A["L0_attn_alpha_logit"], A["L0_attn_k_base_gate_logit"].reshape(1),
                              A["L0_attn_k_base_kernel"], A["L1_attn_lambda_attn"].reshape(1)])
    sm = np.concatenate([A["L0_attn_u"], A["L0_attn_v"], A["L0_ffn_Wg"], A["L1_ffn_router_w"], A["L1_ffn_shared_gate_w"]], 1)
    small = np.ascontiguousarray(sm.reshape(C, P, NSML).transpose(1, 0, 2))
    jbd = np.zeros((P, C, P), np.float32)
    for h in range(HEADS):
        a = (h % HG) * DK
        jbd[a:a + DK, h // HG, a:a + DK] = A["L1_attn_J_attn"][h]
    ctx = A["ctx_1024"]
    arrays = {
        "x_dram": np.ascontiguousarray(A["x"].reshape(T, P, D)),
        "ctx_dram": np.ascontiguousarray(ctx),
        "ctx_t_dram": np.pad(ctx.transpose(0, 2, 1).reshape(BATCH, C, P, KEYS).transpose(0, 2, 1, 3), ((0, 0), (0, 0), (0, 0), (0, 1))),
        "ctx_last_dram": np.ascontiguousarray(ctx[:, KEYS - 1, :].reshape(BATCH, C, P).transpose(2, 1, 0)),
        "mask_dram": np.ascontiguousarray(A["mask_1x1xSxS2_bk0"].reshape(SEQ, KEYS)),
        "units_dram": units, "vecs_dram": vecs, "rows_dram": rows, "scalars_dram": scalars, "small_dram": small,
        "jbd_dram": jbd, "con_dram": constants(),
    }
    nc = _bacc.Bacc("TRN2", target_bir_lowering=False, num_devices=1)
    args = [nc.dram_tensor(k, v.shape, mybir.dt.from_np(v.dtype), kind="ExternalInput").ap() for k, v in arrays.items()]
    args.append(nc.dram_tensor("out_dram", (T, P, D), F32, kind="ExternalOutput").ap())
    build(nc, *args)
    r = _run(nc, [arrays], core_ids=[0])
    return r.results[0]["out_dram"].reshape(BATCH, SEQ, D)
```

```python
from contextlib import ExitStack

import numpy as np

import concourse.bass as bass
from concourse import mybir

ALU = mybir.AluOpType
ACT = mybir.ActivationFunctionType
AX_X = mybir.AxisListType.X
F32 = mybir.dt.float32
F32R = mybir.dt.float32r
U8 = mybir.dt.uint8

P = 128
D = 512
C = D // P
BATCH, SEQ = 32, 32
TOK = BATCH * SEQ
T = TOK // P
PB = P // SEQ
G = TOK // 512
TG = T // G
KEYS = 257
KT = 2
HEADS, DK = 16, 32
HG = 4
R = 16
E = 8
NW = 2
NCT, NCK = 7, 5
NC4 = 2
NVR = 2
NR = 2
NCL = (C - 1) * BATCH + P
NTMP = 4

VEC = ["bq0", "norm1", "norm2", "mb10", "mb11", "mb12", "mb13", "g1", "b1", "g2", "b2", "bq5", "bk5"]
ROW = ["bv0", "proj_b", "mb2", "wo_b", "bv5", "bo5"]
SCL = {"decay": (0, R), "alpha": (R, R), "gate": (2 * R, 1), "kern": (2 * R + 1, 4), "lam": (2 * R + 5, 1)}
NSCL = 2 * R + 6
SML = {"uv": (0, 2 * R)}
NSML = 2 * R
SPL = {"wg": (0, E), "router": (E, E + 1), "bk0": (2 * E + 1, 1)}
NSPL = 2 * E + 2
NSPLW = C * NSPL - 1 + P
CON = {"ident": (0, P), "lower": (P, P), "shift": (2 * P, 4 * P), "causal": (6 * P, P), "before": (7 * P, E * E),
       "row_of": (7 * P + E * E, PB), "pos": (7 * P + E * E + PB, 1)}
NCON = 7 * P + E * E + PB + 1


def constants():
    con = np.zeros((P, NCON), np.float32)
    j, i = np.meshgrid(np.arange(P), np.arange(P), indexing="ij")
    same = (j // SEQ) == (i // SEQ)
    con[:, 0:P] = np.eye(P)
    con[:, P:2 * P] = same & (i >= j)
    for m in range(4):
        con[:, (2 + m) * P:(3 + m) * P] = same & (i - j == m)
    q, k = np.meshgrid(np.arange(P) % SEQ, np.arange(P) % SEQ, indexing="ij")
    con[:, 6 * P:7 * P] = np.where(k > q, -1e30, 0.0)
    e, f = np.meshgrid(np.arange(E), np.arange(E), indexing="ij")
    con[:, 7 * P:7 * P + E * E] = (f < e).astype(np.float32).reshape(1, -1)
    con[:, -1 - PB:-1] = (np.arange(P)[:, None] // SEQ) == np.arange(PB)
    con[:, -1] = np.arange(P) % SEQ
    return con


UNITS = (["0.wq", "0.wk", "0.wv", "1.proj"] + [f"1.w{i}.{b}" for b in range(4) for i in (1, 2)]
         + ["2.q", "2.k", "2.v", "2.o"] + [f"2.w{i}.{b}" for b in range(4) for i in (1, 2)]
         + ["3.q", "3.k", "3.v", "3.o", "4.q", "4.k", "4.v", "4.o"]
         + [f"5.w{i}.{b}" for b in range(E) for i in (1, 2)] + ["5.gate", "5.up", "5.down"])
UNIT = {name: i for i, name in enumerate(UNITS)}


LAG = 3
TAIL = 2


class Jobs:

    def __init__(self):
        self.ready, self.bank, self.drain, self.frees, self.last, self.hi = {}, {}, {}, {}, {}, {}
        self.at, self.count, self.owner = 0, {"act": 0, "dve": 0}, [None] * 8

    def add(self, key, drain, banks=1, unit=None, split=False, at=None):
        self.at = self.at + -self.at % banks if at is None else at
        b = self.at % 8
        before = [self.owner[x] for x in range(b, b + banks) if self.owner[x] is not None]
        need = {}
        for k in before:
            eng, n = self.drain[k]
            need[eng] = max(need.get(eng, 0), n)
        self.frees[key] = need
        for x in range(b, b + banks):
            self.owner[x] = key
        self.at = (b + banks) % 8
        self.bank[key] = b
        self.ready[key] = len(self.ready) + 1
        self.count[drain] += 1
        self.drain[key] = (drain, self.count[drain])
        if split:
            assert drain == "dve"
            self.hi[key] = len(self.hi) + 1
        if unit is not None:
            self.last[unit] = self.ready[key]


def plan():
    J = Jobs()

    def turn(product, name, first=None):
        for t in range(T):
            product(t)
            if t >= LAG:
                J.add((name, t - LAG), "dve", split=True)
        for t in range(T - LAG, T):
            if t == T - TAIL and first is not None:
                first(0)
            J.add((name, t), "dve", split=True)

    def features(name, eng, unit, g, split=False):
        for m in range(C):
            J.add(name + (g, m), eng, unit=unit, split=split)

    for g in range(G):
        for t in range(g * TG, g * TG + TG):
            J.add(("t1", t), "dve", split=True)
        for m in range(C):
            J.add(("q", g, m), "dve", unit="0.wq", split=True)
    def rows(name):
        for g in range(G):
            J.add((name, g), "act")

    rows("crow")
    features(("qk",), "act", "0.wk", 0)
    J.add(("c",), "dve")
    features(("qk",), "act", "0.wk", 1)
    for t in range(T + 1):
        if t < T:
            J.add(("s", t), "act")
        if t >= 1:
            J.add(("pt", t - 1), "act")
            J.add(("u", t - 1), "act")
        if t >= 2:
            J.add(("ut", t - 2), "dve", split=True)
    J.add(("ut", T - 1), "dve", split=True)
    def h_tile(t):
        J.add(("t2", t), "dve")
        if t >= 2:
            J.add(("uv", t - 2), "act")

    for t in range(T):
        J.add(("y", t), "dve", unit="0.wv")
        if t >= LAG:
            h_tile(t - LAG)
    for t in range(T - LAG, T):
        h_tile(t)
    for t in range(T - 2, T):
        J.add(("uv", t), "act")
    for name, eng in (("kq", "act"), ("A", "dve"), ("d", "dve")):
        for t in range(T):
            J.add((name, t), eng, split=name == "d")
    turn(lambda t: J.add(("pr", t), "dve", unit="1.proj"), "t3")
    for b in range(4):
        for g in range(G):
            for m in range(C):
                J.add(("h1", b, g, m), "dve", unit=f"1.w1.{b}", split=True)
        if b < 3:
            for t in range(T):
                J.add(("o1", b, t), "dve", unit=f"1.w2.{b}")
    turn(lambda t: J.add(("o1", 3, t), "dve", unit="1.w2.3"), "t4", lambda g: features(("q3",), "act", "2.q", g))
    features(("q3",), "act", "2.q", 1)
    for g in range(G):
        for m in range(C):
            J.add(("k3", g, m), "act", unit="2.k")
    for t in range(T):
        J.add(("v3", t), "act", unit="2.v")
    for t in range(T + 1):
        if t < T:
            J.add(("s3", t), "act", banks=4)
        if t >= 1:
            J.add(("o3", t - 1), "dve", banks=4, split=True)
    turn(lambda t: J.add(("x3", t), "dve", unit="2.o"), "t6", lambda g: features(("h2", 0), "dve", "2.w1.0", g, True))

    def moe(b, t):
        for e in range(2):
            J.add(("o2", b, t, e), "dve", unit=f"2.w2.{b}")

    for b in range(4):
        if b == 0:
            rows("grow")
        for g in range(0 if b else 1, G):
            features(("h2", b), "dve", f"2.w1.{b}", g, True)
        if b == 0:
            J.add(("g3",), "dve")
        if b < 3:
            for t in range(T):
                moe(b, t)
    turn(lambda t: moe(3, t), "t5", lambda g: features(("q4",), "act", "3.q", g))
    features(("q4",), "act", "3.q", 1)
    J.add(("kl",), "act")
    J.add(("vl",), "act")
    J.add(("klt",), "act")
    for b in range(BATCH + 1):
        if b < BATCH:
            J.add(("k4", b), "act", banks=2, unit="3.k", at=0)
            J.add(("v4", b), "dve", banks=2, unit="3.v", at=2)
        if b >= 1:
            J.add(("p4", b - 1), "act", banks=2, at=0)
            J.add(("l4", b - 1), "act", at=2)
        if b < BATCH:
            J.add(("s4", b), "dve", banks=4, at=4)
        if b >= 1:
            J.add(("o4", b - 1), "dve", split=True, at=3)
    turn(lambda t: J.add(("x4", t), "dve", unit="3.o"), "t7", lambda g: features(("q5",), "act", "4.q", g))
    features(("q5",), "act", "4.q", 1)
    for g in range(G):
        for m in range(C):
            J.add(("k5", g, m), "act", unit="4.k")
    for g in range(G):
        for m in range(C):
            J.add(("qj", g, m), "act")
    for t in range(T):
        J.add(("v5", t), "dve", unit="4.v")
    for t in range(T + 1):
        if t < T:
            J.add(("s5", t), "dve", banks=4)
        if t >= 1:
            J.add(("o5", t - 1), "dve", banks=4, split=True)
    turn(lambda t: J.add(("x5", t), "dve", unit="4.o"), "t8", lambda g: features(("h3", 0), "dve", "5.w1.0", g, True))
    for b in range(E):
        if b == 0:
            rows("rrow")
        for g in range(0 if b else 1, G):
            features(("h3", b), "dve", f"5.w1.{b}", g, True)
        if b == 0:
            J.add(("r6",), "dve")
        for t in range(T):
            J.add(("o6", b, t), "dve", unit=f"5.w2.{b}")
    for g in range(G):
        features(("sg",), "act", "5.gate", g)
    for g in range(G):
        features(("su",), "dve", "5.up", g, True)
    for t in range(T):
        J.add(("os", t), "dve", unit="5.down")
    return J


def build(nc, x, ctx, ctx_t, ctx_last, mask, units, vecs, rows, scalars, small, small2, jbd, con, out):
    J = plan()

    with ExitStack() as stack:
        def sb(name, shape, dt=F32):
            return stack.enter_context(nc.sbuf_tensor(name, shape, dt))

        def sem(name):
            return stack.enter_context(nc.semaphore(name))

        X = sb("X", [P, T, D])
        H = sb("H", [P, T, D])
        h_at = nc.sbuf_base - 4 * T * D
        pool_area = sb("pool_area", [P, 4 * 4096])
        area_at = nc.sbuf_base - 4 * 4 * 4096
        T1h = sb("T1h", [P, C, TOK], F32R)
        T1l = sb("T1l", [P, C, TOK], F32R)
        t1_at = nc.sbuf_base - 2 * 4 * C * TOK
        T1f = nc.alloc_sbuf_tensor_at("T1f", [P, 2 * C * TOK], F32, offset=t1_at)
        Wh = sb("Wh", [P, NW, C, D], F32R)
        Wl = sb("Wl", [P, NW, C, D], F32R)
        B1h = nc.alloc_sbuf_tensor_at("B1h", [P, C, TOK], F32R, offset=area_at)
        B1l = nc.alloc_sbuf_tensor_at("B1l", [P, C, TOK], F32R, offset=area_at + 4 * C * TOK)
        CTh = nc.alloc_sbuf_tensor_at("CTh", [P, NC4, C, KT * P], F32R, offset=h_at)
        CTl = nc.alloc_sbuf_tensor_at("CTl", [P, NC4, C, KT * P], F32R, offset=h_at + 4 * NC4 * C * KT * P)
        T1, B1 = (T1h, T1l), (B1h, B1l)
        W = sb("W", [P, NW, C, D])
        SCP = sb("SCP", [P, NTMP, D])
        clh = nc.alloc_sbuf_tensor_at("clh", [P, NCL], F32R, offset=nc.sbuf_base - 4 * 2 * D)
        cll = nc.alloc_sbuf_tensor_at("cll", [P, NCL], F32R, offset=nc.sbuf_base - 4 * D)
        XN = sb("XN", [P, 2, D])
        vec = sb("vec", [P, len(VEC), C])
        row = sb("row", [P, NR, D])
        scl = sb("scl", [P, NSCL])
        sml = sb("sml", [P, C, NSML])
        cst = sb("cst", [P, NCON])
        jb = sb("jb", [P, C, P])
        mk8 = sb("mk8", [P, KEYS], U8)
        mk = sb("mk", [P, KEYS])
        nm = sb("nm", [P, KEYS])
        half = sb("half", [P, R])
        bns = sb("bns", [P, 6])
        mv = sb("mv", [P, T, 2])
        ve = sb("ve", [P, T, 3])
        rs = sb("rs", [P, T, 2])
        tiny = sb("tiny", [P, 16, 64])
        cw = sb("cw", [P, T, E + 1])
        dec = sb("dec", [P, 8, R])
        smh = sb("smh", [P, NSPLW], F32R)
        sml_low = sb("sml_low", [P, NSPLW], F32R)
        PL = sb("PL", [P, 2, PB])
        PS = stack.enter_context(nc.psum_tensor("PS", [P, 8, 512], F32))

        def area(first, *shape):
            n = int(np.prod(shape))
            v = pool_area[:, first:first + n]
            names = " ".join("abcd"[:len(shape)])
            return v if len(shape) == 1 else v.rearrange(f"p ({names}) -> p {names}", **{k: s for k, s in zip("abcd", shape)})

        A0, A1, A2, A3 = (area(4096 * i, C, TOK) for i in range(4))
        A2t, A3t = (area(4096 * i, T, D) for i in (2, 3))
        XNf = XN[:, :, :].rearrange("p a b -> p (a b)")
        Hf = H[:, :, :].rearrange("p a b -> p (a b)")
        QJ = Hf.rearrange("p (c t) -> p c t", c=C)
        rank_in = area(3 * 4096, 2, T, E * E)
        ident = cst[:, 0:P]
        convm = cst[:, CON["shift"][0]:CON["shift"][0] + P]

        def con_(name):
            a, n = CON[name]
            return cst[:, a:a + n]

        def v_(name):
            return vec[:, VEC.index(name), :]

        def r_(name):
            return row[:, ROW.index(name) % NR, :]

        def s_(name):
            a, n = SCL[name]
            return scl[:, a:a + n]

        def bc(ap, *shape):
            return ap.to_broadcast(shape)

        ready = sem("ready")
        act_drained = sem("act_drained")
        dve_drained = sem("dve_drained")
        drained = {"act": act_drained, "dve": dve_drained}
        w_full = [sem(f"w_full{i}") for i in range(NW)]
        small_high = sem("small_high")
        small_split = sem("small_split")
        w_high = sem("w_high")
        w_split = sem("w_split")
        tmp_ready = sem("tmp_ready")
        high = sem("high")
        row_in = [sem(f"row_in{i}") for i in range(NR)]
        s_batch = sem("s_batch")
        u_batch = sem("u_batch")
        ct_high = sem("ct_high")
        ct_split = sem("ct_split")
        cst_in = sem("cst_in")
        const_in = sem("const_in")
        x_in = [sem(f"x_in{t}") for t in range(T)]
        ctx_t_in = [sem(f"ctx_t_in{i}") for i in range(NCT)]
        ctx_in = [sem(f"ctx_in{i}") for i in range(NCK)]
        ctx4_in = [sem(f"ctx4_in{i}") for i in range(NC4)]
        last_in = sem("last_in")
        cl_in = [sem(f"cl_in{i}") for i in range(2)]
        ownlast = sem("ownlast")
        vrow_in = [sem(f"vrow_in{i}") for i in range(NVR)]
        stored = sem("stored")
        dve_step = sem("dve_step")
        act_step = sem("act_step")
        pool_step = sem("pool_step")
        bias_added = sem("bias_added")
        base_ready = sem("base_ready")
        power_ready = sem("power_ready")
        xn_ready = sem("xn_ready")
        bias_ready = sem("bias_ready")
        exp_ready = sem("exp_ready")
        prob_ready = sem("prob_ready")
        qk_scaled = sem("qk_scaled")
        qbd_ready = sem("qbd_ready")
        zero_ready = sem("zero_ready")
        setup_ready = sem("setup_ready")

        XNB = {name: i * T for i, name in enumerate(["t1", "t3", "t4", "t6", "t5", "t7", "t8"])}
        powers = {}
        for name in ["n1", "dec", "n2", "uv", "n3", "n4", "n6", "n5", "n7", "n8"]:
            for t in range(1 if name in ("dec", "uv") else T):
                powers[name, t] = len(powers) + 1
        added = {}
        for name in ["bv0", "proj_b", "mb2", "wo_b", "bo5"]:
            for t in range(T):
                added[name, t] = len(added) + 1
        soft = {}
        for t in range(T):
            soft["s", t] = len(soft) + 1
        for t in range(T):
            soft["s3", t] = len(soft) + 1
        soft["g3"] = len(soft) + 1
        for b in range(BATCH):
            soft["s4", b] = len(soft) + 1
        for t in range(T):
            soft["s5", t] = len(soft) + 1
        soft["r6"] = len(soft) + 1
        prob = {}
        for key in soft:
            if key not in ("g3", "r6"):
                prob[key] = len(prob) + 1

        tmps = {}
        for key in J.hi:
            if key[0] == "su":
                tmps[key] = len(tmps) + 1
        ring = [key for key in J.hi if key[0] in ("h1", "h3")]

        def banks(key, n=1):
            b = J.bank[key]
            return PS[:, b, :] if n == 1 else PS[:, b:b + n, :]

        QK = A2
        KP = KEYS + 1
        ct_at = lambda base, at: base[:, at:at + C * KP].rearrange("p (c k) -> p c k", c=C)
        ck_at = lambda base, at: base[:, at:at + KT * D].rearrange("p (k d) -> p k d", k=KT)
        hi_area = 3 * 4096
        P1 = area(hi_area, 2, KEYS)
        PT1 = area(hi_area + 2 * KEYS, 2, 3 * P)
        free = hi_area + 2 * KEYS + 6 * P
        CT = [ct_at(Hf, i * C * KP) for i in range(3)] + [ct_at(pool_area, free)]
        CK = [ck_at(pool_area, free + C * KP)]
        CL = [Hf[0:PB, 3 * C * KP:3 * C * KP + D], pool_area[0:PB, free + C * KP + KT * D:free + C * KP + KT * D + D]]
        assert free + C * KP + (KT + 1) * D <= 4 * 4096
        CT += [ct_at(T1f, i * C * KP) for i in range(3)]
        CK += [ck_at(T1f, 3 * C * KP + i * KT * D) for i in range(4)]
        assert 3 * C * KP + 4 * KT * D <= 2 * 4096
        assert (NCT, NCK) == (len(CT), len(CK))
        CT_EARLY = 4
        HT = T1f[:, 0:C * TOK].rearrange("p (c t) -> p c t", c=C)
        cs = tiny[:, 0, 0:T]

        def keys_of(b):
            return banks(("k4", b), 2).rearrange("p a (m k) -> p (a m) k", k=KT * P)

        o = 4096
        take = []
        for shape in ([(C, KEYS)] * 2 + [(KT, D)] * 2 + [(C, KT * P)] * NC4 + [(C, KEYS)] * 2 + [(KT, D)] * 2 + [(C, P)] * 2):
            take.append(area(o, *shape))
            o += int(np.prod(shape))
        assert o <= 4 * 4096, o
        KTb, Vb, CT4, S4, PT4, Qbd = take[0:2], take[2:4], take[4:6], take[6:8], take[8:10], take[10:12]
        sc = SCP[:, :, :].rearrange("p a b -> p (a b)")
        ctxl = sc[:, 0:C * BATCH].rearrange("p (c b) -> p c b", c=C)
        KL = sc[:, P:P + C * BATCH].rearrange("p (c b) -> p c b", c=C)
        KLR = S4[0].rearrange("p c k -> p (c k)")[:, 0:D]
        VL = sc[:, 512:1024]
        pl4 = sc[:, 1024:2048].rearrange("p (n d) -> p n d", n=2)
        vrow = XN

        qk2 = area(4096, T, 2 * R)
        sq = area(4096 + 512, T, 2 * R)
        ksq = area(4096 + 1024, T, 2 * P)
        AT = area(2 * 4096, T, P)
        HH = A3t

        def tok(t):
            return slice(t * P, (t + 1) * P)

        def grp(g):
            return slice(g * 512, (g + 1) * 512)

        block = stack.enter_context(nc.Block())

        @block.sync
        def _(sp):
            def load_unit(u):
                if u >= NW:
                    sp.wait_ge(w_split, u - NW + 1)
                sp.dma_start(W[:, u % NW, :, :], units[u]).then_inc(w_full[u % NW], 16)

            def load_row(i, before=None):
                if before is not None:
                    sp.wait_ge(bias_added, added[before, T - 1])
                sp.dma_start(row[:, i % NR, :], rows[i:i + 1, :].to_broadcast([P, D])).then_inc(row_in[i % NR], 16)

            sp.dma_start(cst[:, :], con).then_inc(cst_in, 16)
            for t in range(T):
                sp.dma_start(X[:, t, :], x[t]).then_inc(x_in[t], 16)
            sp.dma_start(vec[:, :, :], vecs).then_inc(const_in, 16)
            load_unit(0)
            load_unit(1)
            sp.dma_start(scl[:, :], scalars.rearrange("(o r) -> o r", o=1).to_broadcast([P, NSCL])).then_inc(const_in, 16)
            sp.dma_start(sml[:, :, :], small).then_inc(const_in, 16)
            sp.dma_start(sc[:, 0:NSPLW], small2).then_inc(const_in, 16)
            sp.dma_start(jb[:, :, :], jbd).then_inc(const_in, 16)
            for j in range(PB):
                sp.dma_start(mk8[j * SEQ:(j + 1) * SEQ, :], mask).then_inc(const_in, 16)
            load_row(0)
            load_row(1)

            def load_ct(i):
                if i == CT_EARLY:
                    sp.wait_ge(ready, J.ready["q", G - 1, C - 1])
                if i >= NCT:
                    b = i - NCT
                    if b % PB == PB - 1:
                        sp.wait_ge(ready, J.ready["s", b // PB])
                    else:
                        sp.wait_ge(s_batch, (PB - 1) * (b // PB) + b % PB + 1)
                sp.dma_start(CT[i % NCT], ctx_t[i]).then_inc(ctx_t_in[i % NCT], 16)

            def load_ck(i):
                if i >= NCK:
                    b = i - NCK
                    if b % PB == PB - 1:
                        sp.wait_ge(ready, J.ready["u", b // PB])
                    else:
                        sp.wait_ge(u_batch, (PB - 1) * (b // PB) + b % PB + 1)
                sp.dma_start(CK[i % NCK][:, 0:KT, :], ctx[i, 0:KT * P, :].rearrange("(k p) d -> p k d", p=P)).then_inc(ctx_in[i % NCK], 16)

            def load_cl(t):
                if t >= 2:
                    sp.wait_ge(ready, J.ready["u", t - 2])
                sp.dma_start(CL[t % 2], ctx[t * PB:(t + 1) * PB, KT * P, :]).then_inc(cl_in[t % 2], 16)

            for i in range(CT_EARLY):
                load_ct(i)
            load_unit(2)
            load_ck(0)
            for i in range(CT_EARLY, BATCH + CT_EARLY + 3):
                if i < BATCH:
                    load_ct(i)
                if i == CT_EARLY + 1:
                    load_unit(3)
                b = i - CT_EARLY - 2
                if 0 <= b < BATCH and b % PB == 0:
                    load_cl(b // PB)
                if 1 <= b < BATCH:
                    load_ck(b)
            load_row(2, "bv0")
            for u in range(4, 28):
                load_unit(u)
                if u == 8:
                    load_row(3, "proj_b")
                if u == 14:
                    load_row(4, "mb2")
            sp.wait_ge(dve_drained, J.drain["t6", T - 1][1])
            sp.wait_ge(ready, J.ready["h2", 3, G - 1, C - 1])
            sp.dma_start(ctxl, ctx_last).then_inc(last_in, 16)
            sp.wait_ge(ready, J.ready["o2", 3, T - 1, 1])
            for b in range(BATCH):
                if b >= NC4:
                    sp.wait_ge(ct_split, b - NC4 + 2)
                sp.dma_start(CT4[b % NC4], ctx_t[b, :, :, 0:KT * P]).then_inc(ctx4_in[b % NC4], 16)
                if b == 1:
                    sp.wait_ge(act_drained, J.drain["vl",][1])
                    sp.wait_ge(ready, J.ready["t5", T - 1])
                if b >= 1:
                    v = b - 1
                    if v >= NVR:
                        sp.wait_ge(ready, J.ready["o4", v - NVR])
                    sp.dma_start(vrow[0:1, v % NVR, :], VL[v:v + 1, :]).then_inc(vrow_in[v % NVR], 16)
            v = BATCH - 1
            sp.wait_ge(ready, J.ready["o4", v - NVR])
            sp.dma_start(vrow[0:1, v % NVR, :], VL[v:v + 1, :]).then_inc(vrow_in[v % NVR], 16)
            for u in range(28, len(UNITS)):
                load_unit(u)
                if u == 29:
                    load_row(5, "wo_b")
            for t in range(T):
                sp.wait_ge(dve_drained, J.drain["os", t][1])
                sp.dma_start(out[t], X[:, t, :]).then_inc(stored, 16)
            sp.wait_ge(stored, 16 * T)

        @block.tensor
        def _(pe):
            def wait_banks(key):
                for eng, n in J.frees[key].items():
                    pe.wait_ge(drained[eng], n)

            def wait_unit(name):
                u = UNIT[name]
                pe.wait_ge(w_split, u + 1)
                return Wh[:, u % NW, :, :], Wl[:, u % NW, :, :]

            def split_product(out_, a, b, first, last):
                nc.tensor.matmul(out_, a[0], b[0], start=first, stop=False)
                nc.tensor.matmul(out_, a[0], b[1], start=False, stop=False)
                return nc.tensor.matmul(out_, a[1], b[0], start=False, stop=last)

            def cut(pair, *at):
                return pair[0][at], pair[1][at]

            xn = lambda t: XN[:, t % 2, :]

            def transpose_tile(name, t, src, ready_at):
                pe.wait_ge(xn_ready, ready_at + t + 1)
                wait_banks((name, t))
                o_ = banks((name, t))
                for c in range(C):
                    mm = nc.tensor.transpose(o_[:, c * P:(c + 1) * P], src(t)[:, c * P:(c + 1) * P], ident)
                mm.then_inc(ready, 1)

            def feature_major(name, w, src, g):
                for m in range(C):
                    wait_banks(name + (g, m))
                    for c in range(C):
                        mm = split_product(banks(name + (g, m)), cut(w, slice(None), c, slice(m * P, (m + 1) * P)),
                                           cut(src, slice(None), c, grp(g)), c == 0, c == C - 1)
                    mm.then_inc(ready, 1)

            def token_major(key, w, src, t, chunks=range(C)):
                wait_banks(key)
                for c in chunks:
                    mm = split_product(banks(key), cut(src, slice(None), c, tok(t)), cut(w, slice(None), c, slice(None)),
                                       c == chunks[0], c == chunks[-1])
                mm.then_inc(ready, 1)

            def turn(product, name, first=None):
                for t in range(T):
                    product(t)
                    if t >= LAG:
                        transpose_tile(name, t - LAG, xn, XNB[name])
                for t in range(T - LAG, T):
                    if t == T - TAIL and first is not None:
                        wait((name, TG - 1))
                        first()
                    transpose_tile(name, t, xn, XNB[name])
                wait((name, T - 1))

            def per_token_rows(key, src, name):
                a, n = SPL[name]
                for g in range(G):
                    wait_banks((key, g))
                    for c in range(C):
                        mm = split_product(banks((key, g)), cut((smh, sml_low), slice(None), slice(c * NSPL + a, c * NSPL + a + P)),
                                           cut(src, slice(None), c, grp(g)), c == 0, c == C - 1)
                    mm.then_inc(ready, 1)

            def per_token(key, rows_key, n):
                wait((rows_key, G - 1))
                wait_banks((key,))
                for t in range(T):
                    mm = nc.tensor.transpose(banks((key,))[:, t * n:(t + 1) * n], XNf[0:n, tok(t)], ident[0:n, 0:n])
                mm.then_inc(ready, 1)

            def after(key):
                eng, n = J.drain[key]
                return drained[eng], n

            def wait(key):
                pe.wait_ge(*after(key))

            pe.wait_ge(cst_in, 16)
            for g in range(G):
                for t in range(g * TG, g * TG + TG):
                    transpose_tile("t1", t, xn, XNB["t1"])
                w = wait_unit("0.wq")
                wait(("t1", g * TG + TG - 1))
                feature_major(("q",), w, T1, g)
            wait(("q", G - 1, C - 1))
            pe.wait_ge(small_split, 1)
            per_token_rows("crow", B1, "bk0")
            w = wait_unit("0.wk")
            feature_major(("qk",), w, B1, 0)
            per_token("c", "crow", 1)
            feature_major(("qk",), w, B1, 1)

            def values_up(v):
                wait(("u", v))
                wait_banks(("ut", v))
                for c in range(C):
                    mm = nc.tensor.transpose(banks(("ut", v))[:, c * P:(c + 1) * P], XN[:, v % 2, c * P:(c + 1) * P], ident)
                mm.then_inc(ready, 1)

            for t in range(T + 1):
                if t < T:
                    wait(("qk", t // TG, C - 1))
                    wait_banks(("s", t))
                    for j in range(PB):
                        b = t * PB + j
                        pe.wait_ge(ctx_t_in[b % NCT], 16 * (b // NCT + 1))
                        for c in range(C):
                            mm = nc.tensor.matmul(banks(("s", t))[j * SEQ:(j + 1) * SEQ, 0:KEYS],
                                                  QK[:, c, b * SEQ:(b + 1) * SEQ], CT[b % NCT][:, c, 0:KEYS],
                                                  start=(c == 0), stop=(c == C - 1))
                        mm.then_inc(s_batch if j < PB - 1 else ready, 1)
                if t >= 1:
                    v = t - 1
                    pe.wait_ge(prob_ready, prob["s", v])
                    wait_banks(("pt", v))
                    bk = banks(("pt", v))
                    for k in range(KT):
                        nc.tensor.transpose(bk[:, k * P:(k + 1) * P], P1[:, v % 2, k * P:(k + 1) * P], ident)
                    pe.wait_ge(ownlast, v + 1)
                    nc.tensor.transpose(bk[0:PB, KT * P:(KT + 1) * P], PL[:, v % 2, :], ident).then_inc(ready, 1)
                    wait(("pt", v))
                    wait_banks(("u", v))
                    bk = banks(("u", v))
                    for j in range(PB):
                        b = v * PB + j
                        pe.wait_ge(ctx_in[b % NCK], 16 * (b // NCK + 1))
                        for k in range(KT):
                            mm = nc.tensor.matmul(bk[j * SEQ:(j + 1) * SEQ, :], PT1[:, v % 2, k * P + j * SEQ:k * P + (j + 1) * SEQ],
                                                  CK[b % NCK][:, k, :], start=(k == 0), stop=(k == KT - 1), skip_group_check=True)
                        if j < PB - 1:
                            mm.then_inc(u_batch, 1)
                    pe.wait_ge(cl_in[v % 2], 16 * (v // 2 + 1))
                    nc.tensor.matmul(bk, PT1[0:PB, v % 2, KT * P:(KT + 1) * P], CL[v % 2], start=False, stop=True,
                                     skip_group_check=True).then_inc(ready, 1)
                if t >= 2:
                    values_up(t - 2)
            values_up(T - 1)
            w = wait_unit("0.wv")

            def small_(name):
                a, n = SML[name]
                return sml[:, :, a:a + n]

            def transpose_h(t):
                pe.wait_ge(qk_scaled, t + 1)
                wait_banks(("t2", t))
                for c in range(C):
                    mm = nc.tensor.transpose(banks(("t2", t))[:, c * P:(c + 1) * P], HH[:, t, c * P:(c + 1) * P], ident)
                mm.then_inc(ready, 1)

            def rank_products(t):
                wait(("t2", t))
                wait_banks(("uv", t))
                for c in range(C):
                    mm = nc.tensor.matmul(banks(("uv", t))[:, 0:2 * R], HT[:, c, tok(t)], small_("uv")[:, c, :],
                                          start=(c == 0), stop=(c == C - 1))
                mm.then_inc(ready, 1)

            def h_tile(t):
                transpose_h(t)
                if t >= 2:
                    rank_products(t - 2)

            for t in range(T):
                wait(("ut", t))
                token_major(("y", t), w, B1, t)
                if t >= LAG:
                    h_tile(t - LAG)
            for t in range(T - LAG, T):
                h_tile(t)
            for t in range(T - 2, T):
                rank_products(t)
            for t in range(T):
                pe.wait_ge(qk_scaled, T + 1)
                wait_banks(("kq", t))
                for i in range(2):
                    mm = nc.tensor.transpose(banks(("kq", t))[0:R, i * P:(i + 1) * P], qk2[:, t, i * R:(i + 1) * R], ident)
                mm.then_inc(ready, 1)
            for t in range(T):
                wait(("kq", t))
                wait_banks(("A", t))
                nc.tensor.matmul(banks(("A", t))[:, 0:P], ksq[0:R, t, P:2 * P], ksq[0:R, t, 0:P],
                                 start=True, stop=True).then_inc(ready, 1)
            for t in range(T):
                wait(("A", t))
                wait_banks(("d", t))
                for c in range(C):
                    mm = nc.tensor.matmul(banks(("d", t))[:, c * P:(c + 1) * P], HH[:, t, c * P:(c + 1) * P], AT[:, t, :],
                                          start=True, stop=True)
                mm.then_inc(ready, 1)
            w = wait_unit("1.proj")
            wp = w

            def project(t):
                wait(("d", t))
                token_major(("pr", t), wp, B1, t)

            turn(project, "t3")
            for b in range(4):
                w = wait_unit(f"1.w1.{b}")
                for g in range(G):
                    feature_major(("h1", b), w, T1, g)
                w2 = wait_unit(f"1.w2.{b}")

                def mlp_out(t):
                    wait(("h1", b, t // TG, C - 1))
                    token_major(("o1", b, t), w2, B1, t)

                if b < 3:
                    for t in range(T):
                        mlp_out(t)

            def self_scores(name, t, pairs):
                wait_banks((name, t))
                bk = banks((name, t), 4)
                for hb in range(C):
                    for hl in range(HG):
                        hs = slice(hl * DK, (hl + 1) * DK)
                        for j in range(PB):
                            js = slice(j * SEQ, (j + 1) * SEQ)
                            ts = slice(t * P + j * SEQ, t * P + (j + 1) * SEQ)
                            for i, (a, k) in enumerate(pairs):
                                mm = nc.tensor.matmul(bk[js, hl, hb * SEQ:(hb + 1) * SEQ], a[hs, hb, ts], k[hs, hb, ts],
                                                      start=(i == 0), stop=(i == len(pairs) - 1))
                mm.then_inc(ready, 1)

            def self_values(name, t, V, PTs):
                wait_banks((name, t))
                bk = banks((name, t), 4)
                for hb in range(C):
                    for j in range(PB):
                        js = slice(j * SEQ, (j + 1) * SEQ)
                        for hl in range(HG):
                            h, ps = hb * HG + hl, hl * C + hb
                            mm = nc.tensor.matmul(bk[hl * DK:(hl + 1) * DK, j, hb * SEQ:(hb + 1) * SEQ], V[js, t, h * DK:(h + 1) * DK],
                                                  PTs[js, ps * SEQ:(ps + 1) * SEQ], start=True, stop=True)
                mm.then_inc(ready, 1)

            turn(mlp_out, "t4", lambda: feature_major(("q3",), wait_unit("2.q"), T1, 0))
            feature_major(("q3",), wait_unit("2.q"), T1, 1)
            w = wait_unit("2.k")
            for g in range(G):
                feature_major(("k3",), w, T1, g)
            w = wait_unit("2.v")
            for t in range(T):
                token_major(("v3", t), w, T1, t)
            wait(("v3", T - 1))
            for t in range(T + 1):
                if t < T:
                    self_scores("s3", t, [(A0, A1)])
                if t >= 1:
                    pe.wait_ge(prob_ready, prob["s3", t - 1])
                    self_values("o3", t - 1, A2t, SCP[:, 2 + (t - 1) % 2, :])
            wo3 = wait_unit("2.o")

            def out3(t):
                wait(("o3", t))
                token_major(("x3", t), wo3, T1, t)

            turn(out3, "t6", lambda: feature_major(("h2", 0), wait_unit("2.w1.0"), T1, 0))
            for b in range(4):
                if b == 0:
                    per_token_rows("grow", T1, "wg")
                w = wait_unit(f"2.w1.{b}")
                for g in range(0 if b else 1, G):
                    feature_major(("h2", b), w, T1, g)
                if b == 0:
                    per_token("g3", "grow", E)
                w2 = wait_unit(f"2.w2.{b}")

                def experts_out(t):
                    wait(("h2", b, t // TG, C - 1))
                    for e in range(2):
                        token_major(("o2", b, t, e), w2, B1, t, chunks=[2 * e, 2 * e + 1])

                if b < 3:
                    for t in range(T):
                        experts_out(t)

            turn(experts_out, "t5", lambda: feature_major(("q4",), wait_unit("3.q"), T1, 0))
            feature_major(("q4",), wait_unit("3.q"), T1, 1)
            wk = wait_unit("3.k")
            pe.wait_ge(ct_split, 1)
            cl = (clh, cll)
            wv = wait_unit("3.v")
            for key, w in ((("kl",), wk), (("vl",), wv)):
                wait_banks(key)
                for c in range(C):
                    mm = split_product(banks(key), cut(cl, slice(None), slice(c * BATCH, c * BATCH + P)),
                                       cut(w, slice(None), c, slice(None)), c == 0, c == C - 1)
                mm.then_inc(ready, 1)
            wait(("kl",))
            wait_banks(("klt",))
            for m in range(C):
                mm = nc.tensor.transpose(banks(("klt",))[:, m * BATCH:(m + 1) * BATCH], KLR[0:BATCH, m * P:(m + 1) * P], ident[0:BATCH, 0:BATCH])
            mm.then_inc(ready, 1)
            for b in range(BATCH + 1):
                if b < BATCH:
                    pe.wait_ge(ct_split, b + 2)
                    ct = CTh[:, b % NC4, :, :], CTl[:, b % NC4, :, :]
                    wait_banks(("k4", b))
                    bk = keys_of(b)
                    for m in range(C):
                        for c in range(C):
                            mm = split_product(bk[:, m, :], cut(wk, slice(None), c, slice(m * P, (m + 1) * P)),
                                               cut(ct, slice(None), c, slice(None)), c == 0, c == C - 1)
                    mm.then_inc(ready, 1)
                    wait_banks(("v4", b))
                    bk = banks(("v4", b), 2)
                    for k in range(KT):
                        for c in range(C):
                            mm = split_product(bk[:, k, :], cut(ct, slice(None), c, slice(k * P, (k + 1) * P)),
                                               cut(wv, slice(None), c, slice(None)), c == 0, c == C - 1)
                    mm.then_inc(ready, 1)
                if b >= 1:
                    v = b - 1
                    pe.wait_ge(prob_ready, prob["s4", v])
                    wait_banks(("p4", v))
                    bk = banks(("p4", v), 2)
                    for k in range(KT):
                        for hb in range(C):
                            mm = nc.tensor.transpose(bk[:, k, hb * P:(hb + 1) * P], S4[v % 2][:, hb, k * P:(k + 1) * P], ident)
                    mm.then_inc(ready, 1)
                    wait_banks(("l4", v))
                    bk = banks(("l4", v))
                    for hb in range(C):
                        mm = nc.tensor.transpose(bk[0:1, hb * P:(hb + 1) * P], S4[v % 2][:, hb, KT * P:KEYS], ident)
                    mm.then_inc(ready, 1)
                if b < BATCH:
                    wait(("k4", b))
                    pe.wait_ge(qbd_ready, b + 1)
                    wait_banks(("s4", b))
                    bk = banks(("s4", b), 4)
                    for hb in range(C):
                        mm = nc.tensor.matmul(bk[:, hb, 0:KEYS], Qbd[b % 2][:, hb, :], KTb[b % 2][:, hb, :], start=True, stop=True)
                    mm.then_inc(ready, 1)
                if b >= 1:
                    wait(("l4", v))
                    wait(("v4", v))
                    pe.wait_ge(vrow_in[v % NVR], 16 * (v // NVR + 1))
                    wait_banks(("o4", v))
                    bk = banks(("o4", v))
                    for h in range(HEADS):
                        hb, hl = divmod(h, HG)
                        out_ = bk[hl * DK:(hl + 1) * DK, hb * SEQ:(hb + 1) * SEQ]
                        hs = slice(h * DK, (h + 1) * DK)
                        for k in range(KT):
                            nc.tensor.matmul(out_, Vb[v % 2][:, k, hs], PT4[v % 2][:, k, hs], start=(k == 0), stop=False)
                        mm = nc.tensor.matmul(out_, vrow[0:1, v % NVR, hs], pl4[0:1, v % 2, hs], start=False, stop=True)
                    mm.then_inc(ready, 1)

            wo4 = wait_unit("3.o")
            wait(("o4", BATCH - 1))
            turn(lambda t: token_major(("x4", t), wo4, T1, t), "t7", lambda: feature_major(("q5",), wait_unit("4.q"), T1, 0))
            feature_major(("q5",), wait_unit("4.q"), T1, 1)
            w = wait_unit("4.k")
            for g in range(G):
                feature_major(("k5",), w, T1, g)
            wait(("k5", G - 1, C - 1))
            for g in range(G):
                for m in range(C):
                    wait_banks(("qj", g, m))
                    nc.tensor.matmul(banks(("qj", g, m)), jb[:, m, :], A2[:, m, grp(g)], start=True, stop=True).then_inc(ready, 1)
            w = wait_unit("4.v")
            for t in range(T):
                token_major(("v5", t), w, T1, t)
            wait(("v5", T - 1))
            wait(("qj", G - 1, C - 1))
            for t in range(T + 1):
                if t < T:
                    self_scores("s5", t, [(A0, A1), (QJ, A3)])
                if t >= 1:
                    pe.wait_ge(prob_ready, prob["s5", t - 1])
                    self_values("o5", t - 1, A2t, SCP[:, 2 + (t - 1) % 2, :])
            wo5 = wait_unit("4.o")

            def out5(t):
                wait(("o5", t))
                token_major(("x5", t), wo5, T1, t)

            turn(out5, "t8", lambda: feature_major(("h3", 0), wait_unit("5.w1.0"), T1, 0))
            for b in range(E):
                if b == 0:
                    per_token_rows("rrow", T1, "router")
                w = wait_unit(f"5.w1.{b}")
                for g in range(0 if b else 1, G):
                    feature_major(("h3", b), w, T1, g)
                if b == 0:
                    per_token("r6", "rrow", E + 1)
                w = wait_unit(f"5.w2.{b}")
                for t in range(T):
                    wait(("h3", b, t // TG, C - 1))
                    token_major(("o6", b, t), w, B1, t)
            for n, unit in (("sg", "5.gate"), ("su", "5.up")):
                w = wait_unit(unit)
                for g in range(G):
                    feature_major((n,), w, T1, g)
            w = wait_unit("5.down")
            for t in range(T):
                wait(("su", t // TG, C - 1))
                token_major(("os", t), w, B1, t)

        @block.scalar
        def _(act):
            own = [0]

            def step(ins):
                own[0] += 1
                ins.then_inc(act_step, 1)

            def split_high(u):
                if u >= len(UNITS):
                    return
                act.wait_ge(w_full[u % NW], 16 * (u // NW + 1))
                if u >= NW:
                    act.wait_ge(ready, J.last[UNITS[u - NW]])
                nc.scalar.copy(Wh[:, u % NW, :, :], W[:, u % NW, :, :]).then_inc(w_high, 1)

            def next_after(name):
                split_high(UNIT[name] + NW)

            def drain_features(name, dst, scale=1.0, groups=range(G)):
                for g in groups:
                    for m in range(C):
                        act.wait_ge(ready, J.ready[name + (g, m)])
                        nc.scalar.activation(dst[:, m, grp(g)], banks(name + (g, m)), ACT.Copy, scale=scale).then_inc(act_drained, 1)

            def drain_rows(name, n):
                for g in range(G):
                    act.wait_ge(ready, J.ready[name, g])
                    nc.scalar.copy(XNf[0:n, grp(g)], banks((name, g))[0:n, :]).then_inc(act_drained, 1)

            def high_transposes(name, t, high_part=T1h):
                act.wait_ge(ready, J.ready[name, t])
                nc.scalar.copy(high_part[:, :, tok(t)], banks((name, t)).rearrange("p (c n) -> p c n", c=C)).then_inc(high, 1)

            def high_scaled(name, t, dst, w, b, before):
                act.wait_ge(ready, J.ready[name, t])
                free = before if t < NTMP else (name, t - NTMP)
                if free is not None:
                    act.wait_ge(dve_drained, J.drain[free][1])
                for c in range(C):
                    step(nc.scalar.activation(SCP[:, t % NTMP, c * P:(c + 1) * P], banks((name, t))[:, c * P:(c + 1) * P], ACT.Identity,
                                              scale=w[:, c:c + 1], bias=0.0 if b is None else b[:, c:c + 1]))
                act.wait_ge(act_step, own[0])
                nc.scalar.copy(dst[:, :, tok(t)], SCP[:, t % NTMP, :].rearrange("p (c n) -> p c n", c=C)).then_inc(high, 1)

            def high_of_tmp(key, i, dst):
                act.wait_ge(tmp_ready, tmps[key])
                nc.scalar.copy(dst, SCP[:, i % NTMP, :].rearrange("p (c n) -> p c n", c=C) if len(dst.shape) == 3 else SCP[:, i % NTMP, :]).then_inc(high, 1)

            def high_after_func(name, func, bias, groups=range(G)):
                keys = [name + (g, m) for g in groups for m in range(C)]
                for i in range(len(keys) + 1):
                    if i < len(keys):
                        key = keys[i]
                        n = ring.index(key)
                        act.wait_ge(ready, J.ready[key])
                        if n >= NTMP:
                            act.wait_ge(dve_drained, J.drain[ring[n - NTMP]][1])
                        b = 0.0 if bias is None else bias[:, key[-1]:key[-1] + 1]
                        step(nc.scalar.activation(SCP[:, n % NTMP, :], banks(key), func, bias=b))
                        mine = own[0]
                    if i >= 1:
                        key = keys[i - 1]
                        n = ring.index(key)
                        act.wait_ge(act_step, before)
                        nc.scalar.copy(B1h[:, key[-1], grp(key[-2])], SCP[:, n % NTMP, :]).then_inc(high, 1)
                    before = mine

            def high_values(name, v):
                act.wait_ge(ready, J.ready[name, v])
                src = banks((name, v), 4)[:, :, 0:P].rearrange("p j (h q) -> p j h q", h=C)
                nc.scalar.copy(T1h[:, :, tok(v)].rearrange("p h (j q) -> p j h q", j=PB), src).then_inc(high, 1)

            split_high(0)
            for g in range(G):
                for t in range(g * TG, g * TG + TG):
                    high_transposes("t1", t)
                for m in range(C):
                    if g + m == 0:
                        act.wait_ge(const_in, 16 * 9)
                    act.wait_ge(ready, J.ready["q", g, m])
                    nc.scalar.activation(B1h[:, m, grp(g)], banks(("q", g, m)), ACT.Identity,
                                         bias=v_("bq0")[:, m:m + 1]).then_inc(high, 1)
                if g == 0:
                    nc.scalar.copy(smh[:, :], sc[:, 0:NSPLW]).then_inc(small_high, 1)
                    split_high(1)
            next_after("0.wq")
            drain_rows("crow", 1)
            nc.scalar.activation(scl[:, 0:2 * R + 1], scl[:, 0:2 * R + 1], ACT.Exp, scale=-1.0).then_inc(exp_ready, 1)
            drain_features(("qk",), QK)
            next_after("0.wk")
            for t in range(T + 1):
                if t < T:
                    act.wait_ge(bias_ready, soft["s", t])
                    nc.scalar.activation(P1[:, t % 2, :], banks(("s", t))[:, 0:KEYS], ACT.Exp, bias=tiny[:, 2 + t % 2, 0:1],
                                         scale=float(D) ** -0.5, accum_out=tiny[:, 4 + t % 2, 0:1]).then_inc(act_drained, 1)
                if t >= 1:
                    v = t - 1
                    act.wait_ge(ready, J.ready["pt", v])
                    step(nc.scalar.copy(PT1[:, v % 2, 0:KT * P], banks(("pt", v))[:, 0:KT * P]))
                    nc.scalar.copy(PT1[0:PB, v % 2, KT * P:], banks(("pt", v))[0:PB, KT * P:(KT + 1) * P]).then_inc(act_drained, 1)
                    act.wait_ge(ready, J.ready["u", v])
                    nc.scalar.copy(XN[:, v % 2, :], banks(("u", v))).then_inc(act_drained, 1)
                if t >= 2:
                    high_transposes("ut", t - 2, B1h)
            high_transposes("ut", T - 1, B1h)
            for t in range(T):
                act.wait_ge(ready, J.ready["uv", t])
                nc.scalar.copy(qk2[:, t, :], banks(("uv", t))[:, 0:2 * R]).then_inc(act_drained, 1)
            next_after("0.wv")
            for t in range(T):
                act.wait_ge(ready, J.ready["kq", t])
                nc.scalar.copy(ksq[0:R, t, :], banks(("kq", t))[0:R, 0:2 * P]).then_inc(act_drained, 1)
            for t in range(T):
                high_scaled("d", t, B1h, v_("norm1"), None, None)
            for t in range(T):
                high_scaled("t3", t, T1h, v_("norm2"), None, ("d", T - 1))
            next_after("1.proj")
            for b in range(4):
                high_after_func(("h1", b), ACT.Gelu_apprx_tanh, v_(f"mb1{b}"))
                next_after(f"1.w1.{b}")
                if b < 3:
                    next_after(f"1.w2.{b}")
            for t in range(T - TAIL):
                high_scaled("t4", t, T1h, v_("g1"), v_("b1"), ("h1", 3, G - 1, C - 1))
            drain_features(("q3",), A0, groups=[0])
            for t in range(T - TAIL, T):
                high_scaled("t4", t, T1h, v_("g1"), v_("b1"), ("h1", 3, G - 1, C - 1))
            next_after("1.w2.3")
            drain_features(("q3",), A0, groups=[1])
            next_after("2.q")
            drain_features(("k3",), A1)
            next_after("2.k")
            for t in range(T):
                act.wait_ge(ready, J.ready["v3", t])
                nc.scalar.copy(A2t[:, t, :], banks(("v3", t))).then_inc(act_drained, 1)
            next_after("2.v")
            for t in range(T + 1):
                if t < T:
                    if t >= 2:
                        act.wait_ge(prob_ready, prob["s3", t - 2])
                    act.wait_ge(ready, J.ready["s3", t])
                    bk = banks(("s3", t), 4)
                    nc.scalar.activation(SCP[:, t % 2, :].rearrange("p (l n) -> p l n", l=HG), bk[:, :, 0:P], ACT.Copy,
                                         scale=float(DK) ** -0.5).then_inc(act_drained, 1)
                    act.wait_ge(bias_ready, soft["s3", t])
                    nc.scalar.activation(SCP[:, t % 2, :], SCP[:, t % 2, :], ACT.Exp).then_inc(exp_ready, 1)
                if t >= 1:
                    high_values("o3", t - 1)

            def high_relu(b, g):
                for m in range(C):
                    act.wait_ge(ready, J.ready["h2", b, g, m])
                    nc.scalar.activation(B1h[:, m, grp(g)], banks(("h2", b, g, m)), ACT.Relu).then_inc(high, 1)

            for t in range(T - TAIL):
                high_scaled("t6", t, T1h, v_("g2"), v_("b2"), ("o3", T - 1))
            high_relu(0, 0)
            for t in range(T - TAIL, T):
                high_scaled("t6", t, T1h, v_("g2"), v_("b2"), ("o3", T - 1))
            next_after("2.o")
            drain_rows("grow", E)
            for b in range(4):
                for g in range(0 if b else 1, G):
                    high_relu(b, g)
                next_after(f"2.w1.{b}")
                if b == 0:
                    act.wait_ge(bias_ready, soft["g3"])
                    nc.scalar.activation(tiny[:, 6, :], tiny[:, 6, :], ACT.Exp).then_inc(exp_ready, 1)
                if b < 3:
                    next_after(f"2.w2.{b}")
            for t in range(T - TAIL):
                high_transposes("t5", t)
            drain_features(("q4",), A0, scale=float(DK) ** -0.5, groups=[0])
            for t in range(T - TAIL, T):
                high_transposes("t5", t)
            next_after("2.w2.3")
            drain_features(("q4",), A0, scale=float(DK) ** -0.5, groups=[1])
            act.wait_ge(last_in, 16)
            nc.scalar.copy(clh[:, :], sc[:, 0:NCL]).then_inc(ct_high, 1)
            next_after("3.q")
            act.wait_ge(ready, J.ready["kl",])
            nc.scalar.copy(KLR[0:BATCH, :], banks(("kl",))[0:BATCH, :]).then_inc(act_drained, 1)

            def high_context(b):
                act.wait_ge(ctx4_in[b % NC4], 16 * (b // NC4 + 1))
                if b >= NC4:
                    act.wait_ge(ready, J.ready["v4", b - NC4])
                nc.scalar.copy(CTh[:, b % NC4, :, :], CT4[b % NC4]).then_inc(ct_high, 1)

            high_context(0)
            act.wait_ge(ready, J.ready["vl",])
            nc.scalar.copy(VL[0:BATCH, :], banks(("vl",))[0:BATCH, :]).then_inc(act_drained, 1)
            act.wait_ge(ready, J.ready["klt",])
            nc.scalar.copy(KL, banks(("klt",))[:, 0:C * BATCH].rearrange("p (c b) -> p c b", c=C)).then_inc(act_drained, 1)
            act.wait_ge(act_drained, J.drain["klt",][1])
            for b in range(BATCH + 1):
                if b + 1 < BATCH:
                    high_context(b + 1)
                if b < BATCH:
                    act.wait_ge(ready, J.ready["k4", b])
                    step(nc.scalar.copy(KTb[b % 2][:, :, KT * P], KL[:, :, b]))
                    nc.scalar.copy(KTb[b % 2][:, :, 0:KT * P], keys_of(b)).then_inc(act_drained, 1)
                if b == BATCH - 1:
                    next_after("3.k")
                if b == BATCH:
                    next_after("3.v")
                if b >= 1:
                    v = b - 1
                    act.wait_ge(ready, J.ready["p4", v])
                    nc.scalar.copy(PT4[v % 2], banks(("p4", v), 2)).then_inc(act_drained, 1)
                    act.wait_ge(ready, J.ready["l4", v])
                    nc.scalar.copy(pl4[0:1, v % 2, :], banks(("l4", v))[0:1, :]).then_inc(act_drained, 1)
                    act.wait_ge(ready, J.ready["o4", v])
                    nc.scalar.copy(T1h[:, :, v * SEQ:(v + 1) * SEQ], banks(("o4", v))[:, 0:P].rearrange("p (h q) -> p h q", h=C)).then_inc(high, 1)
                if b < BATCH:
                    act.wait_ge(bias_ready, soft["s4", b])
                    for hb in range(C):
                        ins = nc.scalar.activation(S4[b % 2][:, hb, :], S4[b % 2][:, hb, :], ACT.Exp, bias=tiny[:, 7 + b % 2, hb:hb + 1],
                                                   accum_out=tiny[:, 9 + b % 2, hb:hb + 1])
                        if hb == C - 1:
                            ins.then_inc(exp_ready, 1)
                        else:
                            step(ins)
            def drain_tanh(n, b, dst, th, g):
                for m in range(C):
                    act.wait_ge(ready, J.ready[n, g, m])
                    step(nc.scalar.activation(dst[:, m, grp(g)], banks((n, g, m)), ACT.Identity, bias=v_(b)[:, m:m + 1]))
                    nc.scalar.activation(th[:, m, grp(g)], banks((n, g, m)), ACT.Tanh, bias=v_(b)[:, m:m + 1]).then_inc(act_drained, 1)

            for t in range(T - TAIL):
                high_transposes("t7", t)
            drain_tanh("q5", "bq5", A0, A2, 0)
            for t in range(T - TAIL, T):
                high_transposes("t7", t)
            next_after("3.o")
            drain_tanh("q5", "bq5", A0, A2, 1)
            next_after("4.q")
            for g in range(G):
                drain_tanh("k5", "bk5", A1, A3, g)
            next_after("4.k")
            act.wait_ge(setup_ready, 1)
            for g in range(G):
                for m in range(C):
                    act.wait_ge(ready, J.ready["qj", g, m])
                    nc.scalar.activation(QJ[:, m, grp(g)], banks(("qj", g, m)), ACT.Copy, scale=tiny[:, 11, 0:1]).then_inc(act_drained, 1)
            next_after("4.v")
            for t in range(T + 1):
                if t < T:
                    act.wait_ge(bias_ready, soft["s5", t])
                    nc.scalar.activation(SCP[:, t % 2, :], SCP[:, t % 2, :], ACT.Exp).then_inc(exp_ready, 1)
                if t >= 1:
                    high_values("o5", t - 1)
            for t in range(T - TAIL):
                high_transposes("t8", t)
            high_after_func(("h3", 0), ACT.Silu, None, groups=[0])
            for t in range(T - TAIL, T):
                high_transposes("t8", t)
            next_after("4.o")
            drain_rows("rrow", E + 1)
            for b in range(E):
                high_after_func(("h3", b), ACT.Silu, None, groups=range(0 if b else 1, G))
                next_after(f"5.w1.{b}")
                if b == 0:
                    act.wait_ge(bias_ready, soft["r6"])
                    nc.scalar.activation(tiny[:, 6, :], tiny[:, 6, :], ACT.Exp).then_inc(exp_ready, 1)
                    nc.scalar.activation(tiny[:, 12, 0:T], tiny[:, 12, 0:T], ACT.Exp, scale=-1.0).then_inc(exp_ready, 1)
                next_after(f"5.w2.{b}")
            for g in range(G):
                for m in range(C):
                    act.wait_ge(ready, J.ready["sg", g, m])
                    nc.scalar.activation(A2[:, m, grp(g)], banks(("sg", g, m)), ACT.Silu).then_inc(act_drained, 1)
            next_after("5.gate")
            for g in range(G):
                for m in range(C):
                    high_of_tmp(("su", g, m), g * C + m, B1h[:, m, grp(g)])

        @block.gpsimd
        def _(pool):
            def power(name, n=1):
                for t in range(T):
                    pool.wait_ge(base_ready, powers[name, t])
                    nc.gpsimd.tensor_tensor(rs[:, t, 0:n], ve[:, t, 0:n], half[:, 0:n], ALU.pow).then_inc(power_ready, 1)

            def add_row(name, dst, reader, first):
                i = ROW.index(name)
                pool.wait_ge(row_in[i % NR], 16 * (i // NR + 1))
                for t in range(T):
                    pool.wait_ge(reader, first + t + 1)
                    nc.gpsimd.tensor_tensor(dst[:, t, :], dst[:, t, :], r_(name), ALU.add).then_inc(bias_added, 1)

            power("n1")
            pool.wait_ge(base_ready, powers["dec", 0])
            nc.gpsimd.tensor_tensor(dec[:, 4, :], dec[:, 0, :], dec[:, 2, :], ALU.pow).then_inc(pool_step, 1)
            nc.gpsimd.tensor_tensor(dec[:, 5, :], dec[:, 0, :], dec[:, 3, :], ALU.pow).then_inc(power_ready, 1)
            add_row("bv0", X, xn_ready, XNB["t1"])
            power("n2", 2)
            add_row("proj_b", H, qk_scaled, 0)
            pool.wait_ge(base_ready, powers["uv", 0])
            nc.gpsimd.tensor_tensor(tiny[:, 13, 0:2 * T], tiny[:, 14, 0:2 * T], half[:, 0:2 * T], ALU.pow).then_inc(power_ready, 1)
            add_row("mb2", X, qk_scaled, 0)
            power("n3")
            power("n4", 2)
            power("n6")
            power("n5")
            pool.wait_ge(ready, J.ready["o2", 3, T - 1, 1])
            for i in range(2):
                nc.gpsimd.memset(Qbd[i], 0.0).then_inc(zero_ready, 1)
            pool.wait_ge(zero_ready, 2)
            pool.wait_ge(act_drained, J.drain["q4", G - 1, C - 1][1])
            for b in range(BATCH):
                if b >= 2:
                    pool.wait_ge(ready, J.ready["s4", b - 2])
                for hl in range(HG):
                    hs = slice(hl * DK, (hl + 1) * DK)
                    nc.gpsimd.tensor_copy(Qbd[b % 2][hs, :, hs], A0[hs, :, b * SEQ:(b + 1) * SEQ]).then_inc(
                        qbd_ready if hl == HG - 1 else pool_step, 1)
            pool.wait_ge(qbd_ready, BATCH)
            pool.wait_ge(pool_step, 1 + (HG - 1) * BATCH)
            add_row("wo_b", X, xn_ready, XNB["t5"])
            power("n7")
            add_row("bo5", X, xn_ready, XNB["t7"])
            power("n8")

        @block.vector
        def _(dve):
            steps = [0]

            def link(ins):
                steps[0] += 1
                ins.then_inc(dve_step, 1)
                dve.wait_ge(dve_step, steps[0])

            def step(ins):
                steps[0] += 1
                ins.then_inc(dve_step, 1)

            def stats(src, t):
                link(nc.vector.bn_stats(bns[:, :], src[:, t, :]))
                link(nc.vector.bn_aggr(mv[:, t, :], bns[:, :]))

            def base(name, t):
                if name == "n3":
                    link(nc.vector.tensor_scalar(ve[:, t, 2:3], mv[:, t, 0:1], mv[:, t, 0:1], mv[:, t, 1:2], ALU.mult, ALU.add))
                    nc.vector.tensor_scalar(ve[:, t, 0:1], ve[:, t, 2:3], 1e-6, None, ALU.add).then_inc(base_ready, 1)
                elif name in ("n2", "n4"):
                    link(nc.vector.tensor_scalar(ve[:, t, 0:1], mv[:, t, 1:2], 1e-5, None, ALU.add))
                    link(nc.vector.reciprocal(ve[:, t, 2:3], ve[:, t, 0:1]))
                    nc.vector.tensor_scalar(ve[:, t, 1:2], ve[:, t, 2:3], mv[:, t, 1:2], 1e-6 if name == "n2" else 1e-5,
                                            ALU.mult, ALU.add).then_inc(base_ready, 1)
                else:
                    nc.vector.tensor_scalar(ve[:, t, 0:1], mv[:, t, 1:2], 1e-5, None, ALU.add).then_inc(base_ready, 1)

            def norm(name, job, src, t):
                dve.wait_ge(power_ready, powers[name, t])
                if t >= 2 and job != "t2":
                    dve.wait_ge(ready, J.ready[job, t - 2])
                xt = XN[:, t % 2, :]
                if name == "n3":
                    nc.vector.tensor_scalar(xt, H[:, t, :], rs[:, t, 0:1], None, ALU.mult).then_inc(xn_ready, 1)
                elif name == "n2":
                    link(nc.vector.tensor_scalar(H[:, t, :], X[:, t, :], mv[:, t, 0:1], rs[:, t, 0:1], ALU.subtract, ALU.mult))
                    nc.vector.tensor_scalar(HH[:, t, :], H[:, t, :], rs[:, t, 1:2], None, ALU.mult).then_inc(qk_scaled, 1)
                elif name == "n4":
                    link(nc.vector.tensor_scalar(H[:, t, :], X[:, t, :], mv[:, t, 0:1], rs[:, t, 0:1], ALU.subtract, ALU.mult))
                    nc.vector.tensor_scalar(xt, H[:, t, :], rs[:, t, 1:2], None, ALU.mult).then_inc(xn_ready, 1)
                else:
                    nc.vector.tensor_scalar(xt, src[:, t, :], mv[:, t, 0:1], rs[:, t, 0:1],
                                            ALU.subtract, ALU.mult).then_inc(xn_ready, 1)

            def turn(drain_product, name, job, src, drain_tile, first=None):
                for t in range(T):
                    done = drain_product(t)
                    if t >= LAG:
                        drain_tile(t - LAG)
                    dve.wait_ge(dve_drained, J.drain[done][1])
                    stats(src, t)
                    base(name, t)
                    if t >= 1:
                        norm(name, job, src, t - 1)
                norm(name, job, src, T - 1)
                for t in range(T - LAG, T):
                    if t == T - TAIL and first is not None:
                        first()
                    drain_tile(t)

            def fence():
                dve.wait_ge(dve_step, steps[0])

            def split_low(u):
                if u >= len(UNITS):
                    return
                dve.wait_ge(w_high, u + 1)
                nc.vector.tensor_tensor(Wl[:, u % NW, :, :], W[:, u % NW, :, :], Wh[:, u % NW, :, :].bitcast(F32),
                                        ALU.subtract).then_inc(w_split, 1)

            def next_after(name):
                split_low(UNIT[name] + NW)

            def low(key, pair, at, src=None, bias=None):
                dve.wait_ge(high, J.hi[key])
                hi, lo = pair[0][at], pair[1][at]
                src = banks(key) if src is None else src
                if len(hi.shape) == 3:
                    src = src.rearrange("p (c n) -> p c n", c=C)
                if bias is None:
                    nc.vector.tensor_tensor(lo, src, hi.bitcast(F32), ALU.subtract).then_inc(dve_drained, 1)
                else:
                    nc.vector.scalar_tensor_tensor(lo, src, bias, hi.bitcast(F32), ALU.add, ALU.subtract).then_inc(dve_drained, 1)

            A_ = slice(None)

            def low_transposes(name, t):
                low((name, t), T1, (A_, A_, tok(t)))

            def low_func(name, groups=range(G)):
                for g in groups:
                    for m in range(C):
                        key = name + (g, m)
                        low(key, B1, (A_, m, grp(g)), SCP[:, ring.index(key) % NTMP, :])

            def low_values(name, v):
                dve.wait_ge(high, J.hi[name, v])
                src = banks((name, v), 4)[:, :, 0:P].rearrange("p j (h q) -> p j h q", h=C)
                hi, lo = (x[:, :, tok(v)].rearrange("p h (j q) -> p j h q", j=PB) for x in T1)
                nc.vector.tensor_tensor(lo, src, hi.bitcast(F32), ALU.subtract).then_inc(dve_drained, 1)

            def row_bias(name):
                i = ROW.index(name)
                dve.wait_ge(row_in[i % NR], 16 * (i // NR + 1))
                return r_(name)

            link(nc.vector.memset(half[:, :], -0.5))
            def start(t):
                dve.wait_ge(x_in[t], 16)
                stats(X, t)
                base("n1", t)

            for t in range(TG):
                start(t)
                if t >= 1:
                    norm("n1", "t1", X, t - 1)
                if t >= 2:
                    low_transposes("t1", t - 2)
            norm("n1", "t1", X, TG - 1)
            for t in range(TG - 2, TG):
                low_transposes("t1", t)
            split_low(0)
            for t in range(TG, T):
                start(t)
            for t in range(TG, TG + 2):
                norm("n1", "t1", X, t)
            dve.wait_ge(const_in, 16 * 9)
            for m in range(C):
                low(("q", 0, m), B1, (A_, m, grp(0)), bias=v_("bq0")[:, m:m + 1])
            for t in range(TG, T):
                low_transposes("t1", t)
                if t + 2 < T:
                    norm("n1", "t1", X, t + 2)
            dve.wait_ge(small_high, 1)
            nc.vector.tensor_tensor(sml_low[:, :], sc[:, 0:NSPLW], smh[:, :].bitcast(F32), ALU.subtract).then_inc(small_split, 1)
            split_low(1)
            for m in range(C):
                low(("q", 1, m), B1, (A_, m, grp(1)), bias=v_("bq0")[:, m:m + 1])
            next_after("0.wq")
            dve.wait_ge(ready, J.ready["c",])
            isd = float(D) ** -0.5
            nc.vector.tensor_scalar(cs, banks(("c",))[:, 0:T], isd, None, ALU.mult).then_inc(dve_drained, 1)
            dve.wait_ge(dve_drained, J.drain["c",][1])

            dve.wait_ge(const_in, 16 * 9)
            dve.wait_ge(exp_ready, 1)
            link(nc.vector.tensor_scalar(scl[:, 0:2 * R + 1], scl[:, 0:2 * R + 1], 1.0, None, ALU.add))
            link(nc.vector.reciprocal(scl[:, 0:2 * R + 1], scl[:, 0:2 * R + 1]))
            step(nc.vector.tensor_scalar(dec[:, 0, :], s_("decay"), 0.15, 1.0, ALU.max, ALU.min))
            link(nc.vector.memset(dec[:, 1, :], 1.0))
            link(nc.vector.tensor_scalar(dec[:, 2, :], dec[:, 1, :], con_("pos"), None, ALU.mult))
            nc.vector.tensor_scalar(dec[:, 3, :], dec[:, 2, :], -1.0, None, ALU.mult).then_inc(base_ready, 1)
            dve.wait_ge(power_ready, powers["dec", 0])
            link(nc.vector.tensor_tensor(dec[:, 4, :], dec[:, 4, :], s_("alpha"), ALU.mult))
            link(nc.vector.tensor_scalar(s_("kern"), s_("kern"), s_("gate"), None, ALU.mult))
            link(nc.vector.tensor_scalar(convm, con_("shift")[:, 0:P], s_("kern")[:, 0:1], None, ALU.mult))
            for m in range(1, 4):
                link(nc.vector.scalar_tensor_tensor(convm, con_("shift")[:, m * P:(m + 1) * P], s_("kern")[:, m:m + 1],
                                                    convm, ALU.mult, ALU.add))
            link(nc.vector.tensor_copy(mk[:, :], mk8[:, :]))
            step(nc.vector.tensor_scalar(nm[:, :], mk[:, :], 1.0, 1e9, ALU.subtract, ALU.mult))
            nc.vector.tensor_scalar(tiny[:, 11, 0:1], s_("lam"), float(DK) ** 0.5, None, ALU.mult).then_inc(setup_ready, 1)
            next_after("0.wk")

            def u_drain(v):
                low(("ut", v), B1, (A_, A_, tok(v)))

            for t in range(T):
                dve.wait_ge(ready, J.ready["s", t])
                link(nc.vector.reduce_max(tiny[:, 1, 0:1], banks(("s", t))[:, 0:KEYS], AX_X))
                link(nc.vector.scalar_tensor_tensor(tiny[:, 1, 1:2], tiny[:, 1, 0:1], isd, cs[:, t:t + 1], ALU.mult, ALU.add))
                nc.vector.scalar_tensor_tensor(tiny[:, 2 + t % 2, 0:1], tiny[:, 1, 1:2], -1.0, cs[:, t:t + 1],
                                               ALU.mult, ALU.add).then_inc(bias_ready, 1)
                dve.wait_ge(act_drained, J.drain["s", t][1])
                link(nc.vector.reciprocal(tiny[:, 1, 2:3], tiny[:, 4 + t % 2, 0:1]))
                nc.vector.tensor_scalar(P1[:, t % 2, :], P1[:, t % 2, :], tiny[:, 1, 2:3], None, ALU.mult).then_inc(prob_ready, 1)
                dve.wait_ge(prob_ready, prob["s", t])
                nc.vector.tensor_scalar(PL[:, t % 2, :], con_("row_of"), P1[:, t % 2, KT * P:KEYS], None, ALU.mult).then_inc(ownlast, 1)
                if t >= 2:
                    u_drain(t - 2)
            u_drain(T - 2)
            u_drain(T - 1)

            def residual(key, dst, bias, fin=None):
                t = key[1] if fin is None else fin
                if bias is not None:
                    dve.wait_ge(bias_added, added[bias, t])
                dve.wait_ge(ready, J.ready[key])
                nc.vector.tensor_tensor(dst[:, t, :], banks(key), dst[:, t, :], ALU.add).then_inc(dve_drained, 1)

            def value_drain(t):
                residual(("y", t), X, "bv0")
                return "y", t

            def h_drain(t):
                dve.wait_ge(ready, J.ready["t2", t])
                nc.vector.tensor_tensor(HT[:, :, tok(t)], banks(("t2", t)).rearrange("p (c n) -> p c n", c=C),
                                        bc(v_("norm1").unsqueeze(2), P, C, P), ALU.mult).then_inc(dve_drained, 1)

            turn(value_drain, "n2", "t2", X, h_drain)

            def low_tmp(key, pair, at, i):
                low(key, pair, at, SCP[:, i % NTMP, :])

            def low_scaled(name, pair):
                return lambda t: low_tmp((name, t), pair, (A_, A_, tok(t)), t)

            dve.wait_ge(act_drained, J.drain["uv", T - 1][1])
            link(nc.vector.tensor_tensor(sq, qk2, qk2, ALU.mult))
            link(nc.vector.reduce_sum(tiny[:, 15, 0:2 * T].rearrange("p (t i) -> p t i", i=2), sq.rearrange("p t (i r) -> p t i r", i=2), AX_X))
            nc.vector.tensor_scalar(tiny[:, 14, 0:2 * T], tiny[:, 15, 0:2 * T], 1e-16, None, ALU.max).then_inc(base_ready, 1)
            dve.wait_ge(power_ready, powers["uv", 0])
            q4d = qk2.rearrange("p t (i r) -> p t i r", i=2)
            link(nc.vector.tensor_tensor(qk2.rearrange("p t (i r) -> p (t i) r", i=2), qk2.rearrange("p t (i r) -> p (t i) r", i=2),
                                         bc(tiny[:, 13, 0:2 * T].unsqueeze(2), P, 2 * T, R), ALU.mult))
            link(nc.vector.tensor_tensor(q4d[:, :, 0, :], q4d[:, :, 0, :], bc(dec[:, 4:5, :], P, T, R), ALU.mult))
            nc.vector.tensor_tensor(q4d[:, :, 1, :], q4d[:, :, 1, :], bc(dec[:, 5:6, :], P, T, R), ALU.mult).then_inc(qk_scaled, 1)
            for t in range(T):
                dve.wait_ge(ready, J.ready["A", t])
                link(nc.vector.tensor_tensor(AT[:, t, :], banks(("A", t))[:, 0:P], con_("lower"), ALU.mult))
                nc.vector.tensor_tensor(AT[:, t, :], AT[:, t, :], convm, ALU.add).then_inc(dve_drained, 1)
            next_after("0.wv")
            for t in range(T):
                low_scaled("d", B1)(t)

            def project_drain(t):
                residual(("pr", t), H, "proj_b")
                return "pr", t

            turn(project_drain, "n3", "t3", H, low_scaled("t3", T1))
            next_after("1.proj")
            for b in range(4):
                low_func(("h1", b))
                next_after(f"1.w1.{b}")
                if b == 3:
                    break
                for t in range(T):
                    if b:
                        dve.wait_ge(dve_drained, J.drain["o1", b - 1, t][1])
                    else:
                        dve.wait_ge(bias_added, added["mb2", t])
                        link(nc.vector.tensor_tensor(X[:, t, :], X[:, t, :], H[:, t, :], ALU.add))
                    residual(("o1", b, t), X, None, fin=t)
                next_after(f"1.w2.{b}")

            def mlp_drain(t):
                residual(("o1", 3, t), X, None, fin=t)
                return "o1", 3, t

            turn(mlp_drain, "n4", "t4", X, low_scaled("t4", T1))
            next_after("1.w2.3")
            next_after("2.q")
            next_after("2.k")
            next_after("2.v")

            def softmax(name, t, SC, PTs):
                s3 = SC.rearrange("p (h k) -> p h k", k=SEQ)
                link(nc.vector.reduce_max(tiny[:, 1, 0:HEADS], s3, AX_X))
                nc.vector.tensor_tensor(s3, s3, bc(tiny[:, 1, 0:HEADS].unsqueeze(2), P, HEADS, SEQ), ALU.subtract).then_inc(bias_ready, 1)
                dve.wait_ge(exp_ready, exps[name, t])
                link(nc.vector.reduce_sum(tiny[:, 1, 16:32], s3, AX_X))
                link(nc.vector.reciprocal(tiny[:, 1, 32:48], tiny[:, 1, 16:32]))
                link(nc.vector.tensor_tensor(s3, s3, bc(tiny[:, 1, 32:48].unsqueeze(2), P, HEADS, SEQ), ALU.mult))
                if t >= 2:
                    dve.wait_ge(ready, J.ready[{"s3": "o3", "s5": "o5"}[name], t - 2])
                nc.vector.transpose(PTs, SC).then_inc(prob_ready, 1)

            exps = {}
            for t in range(T):
                exps["s3", t] = len(exps) + 2
            exps["g3"] = len(exps) + 2
            for b in range(BATCH):
                exps["s4", b] = len(exps) + 2
            for t in range(T):
                exps["s5", t] = len(exps) + 2
            exps["r6"] = len(exps) + 2
            exps["sig"] = len(exps) + 2

            for t in range(T):
                dve.wait_ge(act_drained, J.drain["s3", t][1])
                softmax("s3", t, SCP[:, t % 2, :], SCP[:, 2 + t % 2, :])
                if t >= 1:
                    low_values("o3", t - 1)
            low_values("o3", T - 1)
            def out3_drain(t):
                residual(("x3", t), H, None)
                return "x3", t

            def low_relu(b, g):
                for m in range(C):
                    dve.wait_ge(high, J.hi["h2", b, g, m])
                    nc.vector.scalar_tensor_tensor(B1l[:, m, grp(g)], banks(("h2", b, g, m)), 0.0, B1h[:, m, grp(g)].bitcast(F32),
                                                   ALU.max, ALU.subtract).then_inc(dve_drained, 1)

            turn(out3_drain, "n6", "t6", H, low_scaled("t6", T1), lambda: low_relu(0, 0))
            next_after("2.o")

            def route(name, cols, renorm):
                L = tiny[:, 0, :].rearrange("p (t e) -> p t e", e=E)
                X6 = tiny[:, 6, :].rearrange("p (t e) -> p t e", e=E)
                sel = tiny[:, 5, :].rearrange("p (t e) -> p t e", e=E)
                dve.wait_ge(ready, J.ready[name,])
                src = banks((name,))[:, 0:T * cols].rearrange("p (t e) -> p t e", e=cols)
                if cols > E:
                    step(nc.vector.tensor_copy(tiny[:, 12, 0:T], src[:, :, E]))
                nc.vector.tensor_copy(L, src[:, :, 0:E]).then_inc(dve_drained, 1)
                dve.wait_ge(dve_drained, J.drain[name,][1])
                fence()
                link(nc.vector.reduce_max(tiny[:, 1, 0:T], L, AX_X))
                nc.vector.tensor_tensor(X6, L, bc(tiny[:, 1, 0:T].unsqueeze(2), P, T, E), ALU.subtract).then_inc(bias_ready, 1)
                other = bc(L.unsqueeze(2), P, T, E, E)
                own = bc(L.unsqueeze(3), P, T, E, E)
                gt = rank_in[:, 0, :, :].rearrange("p t (e f) -> p t e f", f=E)
                eq = rank_in[:, 1, :, :].rearrange("p t (e f) -> p t e f", f=E)
                step(nc.vector.tensor_tensor(gt, other, own, ALU.is_gt))
                link(nc.vector.tensor_tensor(eq, other, own, ALU.is_equal))
                link(nc.vector.tensor_tensor(rank_in[:, 1, :, :], rank_in[:, 1, :, :], bc(con_("before").unsqueeze(1), P, T, E * E), ALU.mult))
                link(nc.vector.tensor_tensor(rank_in[:, 0, :, :], rank_in[:, 0, :, :], rank_in[:, 1, :, :], ALU.add))
                link(nc.vector.reduce_sum(sel, gt, AX_X))
                link(nc.vector.tensor_scalar(sel, sel, 1.5, None, ALU.is_lt))
                dve.wait_ge(exp_ready, exps[name])
                if not renorm:
                    link(nc.vector.reduce_sum(tiny[:, 1, 8:16], X6, AX_X))
                link(nc.vector.tensor_tensor(X6, X6, sel, ALU.mult))
                if renorm:
                    link(nc.vector.reduce_sum(tiny[:, 1, 8:16], X6, AX_X))
                link(nc.vector.reciprocal(tiny[:, 1, 16:24], tiny[:, 1, 8:16]))
                link(nc.vector.tensor_tensor(cw[:, :, 0:E], X6, bc(tiny[:, 1, 16:24].unsqueeze(2), P, T, E), ALU.mult))

            def weighted(key, t, e):
                dve.wait_ge(ready, J.ready[key])
                nc.vector.scalar_tensor_tensor(X[:, t, :], banks(key), cw[:, t, e:e + 1], X[:, t, :],
                                               ALU.mult, ALU.add).then_inc(dve_drained, 1)

            def experts_drain(b, t):
                for e in range(2):
                    if e == 1:
                        dve.wait_ge(dve_drained, J.drain["o2", b, t, 0][1])
                    weighted(("o2", b, t, e), t, 2 * b + e)
                return "o2", b, t, 1

            for b in range(4):
                for g in range(0 if b else 1, G):
                    low_relu(b, g)
                next_after(f"2.w1.{b}")
                if b == 0:
                    route("g3", E, True)
                if b == 3:
                    break
                for t in range(T):
                    if b == 0:
                        link(nc.vector.tensor_tensor(X[:, t, :], X[:, t, :], H[:, t, :], ALU.add))
                    else:
                        dve.wait_ge(dve_drained, J.drain["o2", b - 1, t, 1][1])
                    experts_drain(b, t)
                next_after(f"2.w2.{b}")
            turn(lambda t: experts_drain(3, t), "n5", "t5", X, lambda t: low_transposes("t5", t))
            next_after("2.w2.3")

            dve.wait_ge(ct_high, 1)
            nc.vector.tensor_tensor(cll[:, :], sc[:, 0:NCL], clh[:, :].bitcast(F32), ALU.subtract).then_inc(ct_split, 1)
            next_after("3.q")

            def low_context(b):
                dve.wait_ge(ct_high, b + 2)
                nc.vector.tensor_tensor(CTl[:, b % NC4, :, :], CT4[b % NC4], CTh[:, b % NC4, :, :].bitcast(F32),
                                        ALU.subtract).then_inc(ct_split, 1)

            def o4_drain(v):
                dve.wait_ge(high, J.hi["o4", v])
                qs = slice(v * SEQ, (v + 1) * SEQ)
                nc.vector.tensor_tensor(T1l[:, :, qs], banks(("o4", v))[:, 0:P].rearrange("p (h q) -> p h q", h=C),
                                        T1h[:, :, qs].bitcast(F32), ALU.subtract).then_inc(dve_drained, 1)

            low_context(0)
            for b in range(BATCH):
                if b + 1 < BATCH:
                    low_context(b + 1)
                S = S4[b % 2]
                dve.wait_ge(ready, J.ready["v4", b])
                nc.vector.tensor_copy(Vb[b % 2], banks(("v4", b), 2)).then_inc(dve_drained, 1)
                if b == BATCH - 1:
                    next_after("3.k")
                dve.wait_ge(ready, J.ready["s4", b])
                nc.vector.tensor_tensor(S, banks(("s4", b), 4)[:, :, 0:KEYS], bc(mk[:, :].unsqueeze(1), P, C, KEYS), ALU.mult).then_inc(dve_drained, 1)
                dve.wait_ge(dve_drained, J.drain["s4", b][1])
                link(nc.vector.tensor_tensor(S, S, bc(nm[:, :].unsqueeze(1), P, C, KEYS), ALU.add))
                link(nc.vector.reduce_max(tiny[:, 1, 0:C], S, AX_X))
                nc.vector.tensor_scalar(tiny[:, 7 + b % 2, 0:C], tiny[:, 1, 0:C], -1.0, None, ALU.mult).then_inc(bias_ready, 1)
                if b >= 1:
                    o4_drain(b - 1)
                dve.wait_ge(exp_ready, exps["s4", b])
                link(nc.vector.reciprocal(tiny[:, 1, 8:8 + C], tiny[:, 9 + b % 2, 0:C]))
                nc.vector.tensor_tensor(S, S, bc(tiny[:, 1, 8:8 + C].unsqueeze(2), P, C, KEYS), ALU.mult).then_inc(prob_ready, 1)
            next_after("3.v")
            o4_drain(BATCH - 1)

            def out4_drain(t):
                residual(("x4", t), X, "wo_b")
                return "x4", t

            turn(out4_drain, "n7", "t7", X, lambda t: low_transposes("t7", t))
            next_after("3.o")
            next_after("4.q")
            next_after("4.k")
            bias = row_bias("bv5")
            for t in range(T):
                dve.wait_ge(ready, J.ready["v5", t])
                nc.vector.tensor_tensor(A2t[:, t, :], banks(("v5", t)), bias, ALU.add).then_inc(dve_drained, 1)
            next_after("4.v")
            for t in range(T):
                dve.wait_ge(ready, J.ready["s5", t])
                bk = banks(("s5", t), 4)
                nc.vector.scalar_tensor_tensor(SCP[:, t % 2, :].rearrange("p (l n) -> p l n", l=HG), bk[:, :, 0:P], float(DK) ** -0.5,
                                               bc(con_("causal").unsqueeze(1), P, HG, P), ALU.mult, ALU.add).then_inc(dve_drained, 1)
                dve.wait_ge(dve_drained, J.drain["s5", t][1])
                fence()
                softmax("s5", t, SCP[:, t % 2, :], SCP[:, 2 + t % 2, :])
                if t >= 1:
                    low_values("o5", t - 1)
            low_values("o5", T - 1)

            def out5_drain(t):
                residual(("x5", t), X, "bo5")
                return "x5", t

            turn(out5_drain, "n8", "t8", X, lambda t: low_transposes("t8", t), lambda: low_func(("h3", 0), [0]))
            next_after("4.o")
            for b in range(E):
                low_func(("h3", b), range(0 if b else 1, G))
                next_after(f"5.w1.{b}")
                if b == 0:
                    route("r6", E + 1, False)
                    dve.wait_ge(exp_ready, exps["sig"])
                    link(nc.vector.tensor_scalar(tiny[:, 12, 0:T], tiny[:, 12, 0:T], 1.0, None, ALU.add))
                    link(nc.vector.reciprocal(cw[:, :, E], tiny[:, 12, 0:T]))
                for t in range(T):
                    if b:
                        dve.wait_ge(dve_drained, J.drain["o6", b - 1, t][1])
                    weighted(("o6", b, t), t, b)
                next_after(f"5.w2.{b}")
            next_after("5.gate")
            for g in range(G):
                for m in range(C):
                    i = g * C + m
                    dve.wait_ge(act_drained, J.drain["sg", g, m][1])
                    dve.wait_ge(ready, J.ready["su", g, m])
                    nc.vector.tensor_tensor(SCP[:, i % NTMP, :], banks(("su", g, m)), A2[:, m, grp(g)], ALU.mult).then_inc(tmp_ready, 1)
                    if i:
                        gp, mp = divmod(i - 1, C)
                        low_tmp(("su", gp, mp), B1, (A_, mp, grp(gp)), i - 1)
            low_tmp(("su", G - 1, C - 1), B1, (A_, C - 1, grp(G - 1)), G * C - 1)
            for t in range(T):
                weighted(("os", t), t, E)


def kernel(**inp):
    import concourse.bacc as _bacc
    from concourse.bass_utils import run_bass_kernel_spmd as _run

    A = {k: np.asarray(v) for k, v in inp.items()}

    def unit(w):
        return w.reshape(C, P, D).transpose(1, 0, 2)

    mats = [A["L0_xattn_Wq"].T, A["L0_xattn_Wk"], A["L0_xattn_Wv"].T, A["L0_attn_proj_w"].T]
    for b in range(4):
        mats += [A["L0_attn_mlp_w1"][:, b * D:(b + 1) * D], A["L0_attn_mlp_w2"][b * D:(b + 1) * D]]
    mats += [A["L0_ffn_Wq"], A["L0_ffn_Wk"], A["L0_ffn_Wv"], A["L0_ffn_Wo"]]
    for b in range(4):
        mats += [np.concatenate([A["L0_ffn_W1"][2 * b], A["L0_ffn_W1"][2 * b + 1]], 1),
                 np.concatenate([A["L0_ffn_W2"][2 * b], A["L0_ffn_W2"][2 * b + 1]], 0)]
    mats += [A["L1_xattn_wq"].T, A["L1_xattn_wk"].T, A["L1_xattn_wv"].T, A["L1_xattn_wo_w"].T]
    mats += [A["L1_attn_Wq"].T, A["L1_attn_Wk"].T, A["L1_attn_Wv"].T, A["L1_attn_Wo"].T]
    for e in range(E):
        mats += [A["L1_ffn_w1"][e], A["L1_ffn_w2"][e]]
    mats += [A["L1_ffn_shared_gate_up"][:, :D], A["L1_ffn_shared_gate_up"][:, D:], A["L1_ffn_shared_down"]]
    units = np.ascontiguousarray(np.stack([unit(m) for m in mats]))

    mb1 = A["L0_attn_mlp_b1"].reshape(4, D)
    vs = [A["L0_xattn_bq"], A["L0_attn_norm1_w"], A["L0_attn_norm2_w"], *mb1, A["L0_ffn_g1"], A["L0_ffn_b1"], A["L0_ffn_g2"],
          A["L0_ffn_b2"], A["L1_attn_bq"], A["L1_attn_bk"]]
    vecs = np.ascontiguousarray(np.stack(vs).reshape(len(VEC), C, P).transpose(2, 0, 1))
    rows = np.stack([A["L0_xattn_bv"], A["L0_attn_proj_b"], A["L0_attn_mlp_b2"], A["L1_xattn_wo_b"], A["L1_attn_bv"], A["L1_attn_bo"]])
    scalars = np.concatenate([A["L0_attn_decay_logit"], A["L0_attn_alpha_logit"], A["L0_attn_k_base_gate_logit"].reshape(1),
                              A["L0_attn_k_base_kernel"], A["L1_attn_lambda_attn"].reshape(1)])
    sm = np.concatenate([A["L0_attn_u"], A["L0_attn_v"]], 1)
    spl = np.concatenate([A["L0_ffn_Wg"], A["L1_ffn_router_w"], A["L1_ffn_shared_gate_w"], A["L0_xattn_bk"].reshape(D, 1)], 1)
    spl = spl.reshape(C, P, NSPL).transpose(1, 0, 2).reshape(P, C * NSPL)
    small = np.ascontiguousarray(sm.reshape(C, P, NSML).transpose(1, 0, 2))
    jbd = np.zeros((P, C, P), np.float32)
    for h in range(HEADS):
        a = (h % HG) * DK
        jbd[a:a + DK, h // HG, a:a + DK] = A["L1_attn_J_attn"][h]
    ctx = A["ctx_1024"]
    arrays = {
        "x_dram": np.ascontiguousarray(A["x"].reshape(T, P, D)),
        "ctx_dram": np.ascontiguousarray(ctx),
        "ctx_t_dram": np.pad(ctx.transpose(0, 2, 1).reshape(BATCH, C, P, KEYS).transpose(0, 2, 1, 3), ((0, 0), (0, 0), (0, 0), (0, 1))),
        "ctx_last_dram": np.ascontiguousarray(ctx[:, KEYS - 1, :].reshape(BATCH, C, P).transpose(2, 1, 0)),
        "mask_dram": np.ascontiguousarray(A["mask_1x1xSxS2_bk0"].reshape(SEQ, KEYS)),
        "units_dram": units, "vecs_dram": vecs, "rows_dram": rows, "scalars_dram": scalars, "small_dram": small,
        "small_split_dram": np.pad(spl, ((0, 0), (0, NSPLW - C * NSPL))),
        "jbd_dram": jbd, "con_dram": constants(),
    }
    nc = _bacc.Bacc("TRN2", target_bir_lowering=False, num_devices=1)
    args = [nc.dram_tensor(k, v.shape, mybir.dt.from_np(v.dtype), kind="ExternalInput").ap() for k, v in arrays.items()]
    args.append(nc.dram_tensor("out_dram", (T, P, D), F32, kind="ExternalOutput").ap())
    build(nc, *args)
    r = _run(nc, [arrays], core_ids=[0])
    return r.results[0]["out_dram"].reshape(BATCH, SEQ, D)
```
